# Optimizing a Trainium2 kernel written in Bass

```python
import numpy as np
import jax
import jax.numpy as jnp

def _softmax(x, axis=-1):
    return jax.nn.softmax(x, axis=axis)

def _gelu(x):
    return jax.nn.gelu(x, approximate=True)

def _silu(x):
    return jax.nn.silu(x)

def _sigmoid(x):
    return jax.nn.sigmoid(x)

def _layernorm(x, axis=-1, eps=1e-05):
    m = jnp.mean(x, axis=axis, keepdims=True)
    v = jnp.var(x, axis=axis, keepdims=True)
    return (x - m) / jnp.sqrt(v + eps)

def _scatter_add(tgt, idx, src, axis=0):
    return tgt.at[idx].add(src)

def _segment_sum(src, seg, n):
    return jax.ops.segment_sum(src, seg, n)
kernel_name = 'mk_decoder_preln_d1_seqx_r4_62c8fa'

def setup_inputs(seed: int=0):
    np.random.seed(seed)
    _w = jnp.asarray

    def _rec_inputs():
        import jax
        import jax.numpy as jnp
        _rk = jax.random.key(seed)
        x = -0.0003929 + 0.9999 * jax.random.normal(jax.random.fold_in(_rk, 1), (16, 128, 1024), jnp.float32)
        _lenS = 128 - jax.random.randint(jax.random.fold_in(_rk, 7), (16,), 0, max(1, 128 // 4) + 1, jnp.int32)
        _lenS2 = 128 - jax.random.randint(jax.random.fold_in(_rk, 8), (16,), 0, max(1, 128 // 4) + 1, jnp.int32)
        _ctx_4096P = jax.random.normal(jax.random.fold_in(_rk, 11), (16, 16, 1024), jnp.float32)
        _ctx_4096c = jax.random.dirichlet(jax.random.fold_in(_rk, 511), 0.3 * jnp.ones((16,), jnp.float32), (16, 128))
        _ctx_4096t = jnp.einsum('bsk,bkd->bsd', _ctx_4096c, _ctx_4096P)
        _ctx_4096t = _ctx_4096t * jax.lax.rsqrt(jnp.mean(jnp.square(_ctx_4096t)) + 1e-12) * 0.953939
        ctx_4096 = 2.81802e-05 + 1.00001 * (_ctx_4096t + 0.3 * jax.random.normal(jax.random.fold_in(_rk, 611), (16, 128, 1024), jnp.float32))
        return (x, ctx_4096)
    x, ctx_4096 = _rec_inputs()

    def _L0_attn_setup():
        import jax, jax.numpy as jnp
        import numpy as np
        D_MODEL = 1024
        N_HEADS = 32
        HEAD_DIM = D_MODEL // N_HEADS
        CLIP_QKV = 8.0
        ALIBI_BIAS_MAX = 8.0
        LN_EPS = 1e-05

        def _alibi_slopes(n_heads: int, bias_max: float) -> jnp.ndarray:
            next_pow2 = 2 ** int(np.ceil(np.log2(n_heads)))
            m = np.arange(1, next_pow2 + 1, dtype=np.float32) * (bias_max / next_pow2)
            slopes = 1.0 / np.power(2.0, m)
            if next_pow2 != n_heads:
                slopes = np.concatenate([slopes[1::2], slopes[::2]])[:n_heads]
            return jnp.asarray(slopes)

        def _layer_norm(x, w, b):
            mu = jnp.mean(x, axis=-1, keepdims=True)
            var = jnp.mean(jnp.square(x - mu), axis=-1, keepdims=True)
            return (x - mu) * jax.lax.rsqrt(var + LN_EPS) * w + b
        key = jax.random.key(seed)
        ks = jax.random.split(key, 3)
        B, S = (1, 512)
        hidden_states = jax.random.normal(ks[0], (B, S, D_MODEL), dtype=jnp.float32)
        Wqkv = jax.random.normal(ks[1], (3 * D_MODEL, D_MODEL), dtype=jnp.float32) * 0.02
        Wout = jax.random.normal(ks[2], (D_MODEL, D_MODEL), dtype=jnp.float32) * 0.02
        return {'hidden_states': hidden_states, 'Wqkv': Wqkv, 'q_ln_w': jnp.ones((D_MODEL,), jnp.float32), 'q_ln_b': jnp.zeros((D_MODEL,), jnp.float32), 'k_ln_w': jnp.ones((D_MODEL,), jnp.float32), 'k_ln_b': jnp.zeros((D_MODEL,), jnp.float32), 'Wout': Wout}
    _L0_attn_all = _L0_attn_setup()
    _L0_attn_in = {k: v for k, v in _L0_attn_all.items() if k in ('Wqkv', 'q_ln_w', 'q_ln_b', 'k_ln_w', 'k_ln_b', 'Wout')}
    del _L0_attn_all

    def _L0_xattn_setup():
        import jax, jax.numpy as jnp
        import numpy as np
        DIM = 128
        HEADS = 8
        DIM_HEAD = 64
        HIDDEN = HEADS * DIM_HEAD
        SCALE = DIM_HEAD ** (-0.5)
        key = jax.random.key(seed)
        ks = jax.random.split(key, 9)
        b, n = (8, 1024)
        std = 1.0 / np.sqrt(DIM)
        return {'q': jax.random.normal(ks[0], (b, DIM, n), jnp.float32), 'k': jax.random.normal(ks[1], (b, DIM, n), jnp.float32), 'v': jax.random.normal(ks[2], (b, DIM, n), jnp.float32), 'Wq': jax.random.normal(ks[3], (HIDDEN, DIM), jnp.float32) * std, 'Wk': jax.random.normal(ks[4], (HIDDEN, DIM), jnp.float32) * std, 'Wv': jax.random.normal(ks[5], (HIDDEN, DIM), jnp.float32) * std, 'Wo': jax.random.normal(ks[6], (DIM, HIDDEN), jnp.float32) * (1.0 / np.sqrt(HIDDEN)), 'bo': jax.random.normal(ks[7], (DIM,), jnp.float32) * 0.01, 'g': jnp.ones((1, DIM, 1), jnp.float32)}
    _L0_xattn_all = _L0_xattn_setup()
    _L0_xattn_in = {k: v for k, v in _L0_xattn_all.items() if k in ('Wq', 'Wk', 'Wv', 'Wo', 'bo', 'g')}
    del _L0_xattn_all

    def _L0_ffn_setup():
        import jax, jax.numpy as jnp
        import numpy as np
        GROUP = 64

        def dequant_q40(w, s, out_features, in_features):
            msb = w >> 4
            lsb = (w & 15 ^ 8) - 8
            g = jnp.concatenate([msb, lsb], axis=1).reshape(-1, GROUP)
            deq = g.astype(s.dtype) * s[:, None]
            return deq.reshape(out_features, in_features)
        key = jax.random.key(seed)
        ks = jax.random.split(key, 7)
        dim, hidden = (1024, 2752)
        B, S = (2, 512)

        def packed(k, din, dout):
            return jax.random.randint(k, (din * dout // GROUP // 2, GROUP), -128, 128, dtype=jnp.int32)

        def scales(k, din, dout):
            return (jax.random.uniform(k, (din * dout // GROUP,), dtype=jnp.float32) + 0.5) * 0.01
        x = jax.random.normal(ks[0], (B, S, dim), dtype=jnp.float32)
        w1 = packed(ks[1], dim, hidden)
        s1 = scales(ks[2], dim, hidden)
        w2 = packed(ks[3], hidden, dim)
        s2 = scales(ks[4], hidden, dim)
        w3 = packed(ks[5], dim, hidden)
        s3 = scales(ks[6], dim, hidden)
        return {'x': x, 'w1': w1, 's1': s1, 'w2': w2, 's2': s2, 'w3': w3, 's3': s3}
    _L0_ffn_all = _L0_ffn_setup()
    _L0_ffn_in = {k: v for k, v in _L0_ffn_all.items() if k in ('w1', 's1', 'w2', 's2', 'w3', 's3')}
    del _L0_ffn_all
    return {'x': x, 'ctx_4096': ctx_4096, 'L0_attn_Wqkv': _L0_attn_in['Wqkv'], 'L0_attn_q_ln_w': _L0_attn_in['q_ln_w'], 'L0_attn_q_ln_b': _L0_attn_in['q_ln_b'], 'L0_attn_k_ln_w': _L0_attn_in['k_ln_w'], 'L0_attn_k_ln_b': _L0_attn_in['k_ln_b'], 'L0_attn_Wout': _L0_attn_in['Wout'], 'L0_xattn_Wq': _L0_xattn_in['Wq'], 'L0_xattn_Wk': _L0_xattn_in['Wk'], 'L0_xattn_Wv': _L0_xattn_in['Wv'], 'L0_xattn_Wo': _L0_xattn_in['Wo'], 'L0_xattn_bo': _L0_xattn_in['bo'], 'L0_xattn_g': _L0_xattn_in['g'], 'L0_ffn_w1': _L0_ffn_in['w1'], 'L0_ffn_s1': _L0_ffn_in['s1'], 'L0_ffn_w2': _L0_ffn_in['w2'], 'L0_ffn_s2': _L0_ffn_in['s2'], 'L0_ffn_w3': _L0_ffn_in['w3'], 'L0_ffn_s3': _L0_ffn_in['s3']}

def reference(x, ctx_4096, L0_attn_Wqkv, L0_attn_q_ln_w, L0_attn_q_ln_b, L0_attn_k_ln_w, L0_attn_k_ln_b, L0_attn_Wout, L0_xattn_Wq, L0_xattn_Wk, L0_xattn_Wv, L0_xattn_Wo, L0_xattn_bo, L0_xattn_g, L0_ffn_w1, L0_ffn_s1, L0_ffn_w2, L0_ffn_s2, L0_ffn_w3, L0_ffn_s3):
    import jax
    import jax.numpy as jnp

    def _L0_attn_ref(hidden_states, Wqkv, q_ln_w, q_ln_b, k_ln_w, k_ln_b, Wout):
        import jax, jax.numpy as jnp
        import numpy as np
        D_MODEL = 1024
        N_HEADS = 32
        HEAD_DIM = D_MODEL // N_HEADS
        CLIP_QKV = 8.0
        ALIBI_BIAS_MAX = 8.0
        LN_EPS = 1e-05

        def _alibi_slopes(n_heads: int, bias_max: float) -> jnp.ndarray:
            next_pow2 = 2 ** int(np.ceil(np.log2(n_heads)))
            m = np.arange(1, next_pow2 + 1, dtype=np.float32) * (bias_max / next_pow2)
            slopes = 1.0 / np.power(2.0, m)
            if next_pow2 != n_heads:
                slopes = np.concatenate([slopes[1::2], slopes[::2]])[:n_heads]
            return jnp.asarray(slopes)

        def _layer_norm(x, w, b):
            mu = jnp.mean(x, axis=-1, keepdims=True)
            var = jnp.mean(jnp.square(x - mu), axis=-1, keepdims=True)
            return (x - mu) * jax.lax.rsqrt(var + LN_EPS) * w + b
        B, S, _ = hidden_states.shape
        qkv = jnp.einsum('bsd,ed->bse', hidden_states, Wqkv)
        qkv = jnp.clip(qkv, -CLIP_QKV, CLIP_QKV)
        q, k, v = jnp.split(qkv, [D_MODEL, 2 * D_MODEL], axis=-1)
        q = _layer_norm(q, q_ln_w, q_ln_b)
        k = _layer_norm(k, k_ln_w, k_ln_b)
        q = q.reshape(B, S, N_HEADS, HEAD_DIM)
        k = k.reshape(B, S, N_HEADS, HEAD_DIM)
        v = v.reshape(B, S, N_HEADS, HEAD_DIM)
        scale = HEAD_DIM ** (-0.5)
        scores = jnp.einsum('bqhd,bkhd->bhqk', q, k) * scale
        slopes = _alibi_slopes(N_HEADS, ALIBI_BIAS_MAX)
        pos = jnp.arange(S)
        rel = (pos[None, :] - pos[:, None]).astype(jnp.float32)
        scores = scores + slopes[None, :, None, None] * rel[None, None]
        causal = pos[None, :] <= pos[:, None]
        scores = jnp.where(causal[None, None], scores, jnp.float32(-1e+30))
        probs = jax.nn.softmax(scores, axis=-1)
        out = jnp.einsum('bhqk,bkhd->bqhd', probs, v).reshape(B, S, D_MODEL)
        return jnp.einsum('bsd,ed->bse', out, Wout)

    def _L0_xattn_ref(q, k, v, Wq, Wk, Wv, Wo, bo, g):
        import jax, jax.numpy as jnp
        import numpy as np
        DIM = 128
        HEADS = 8
        DIM_HEAD = 64
        HIDDEN = HEADS * DIM_HEAD
        SCALE = DIM_HEAD ** (-0.5)
        b = q.shape[0]
        qh = jnp.einsum('bcn,oc->bon', q, Wq).reshape(b, HEADS, DIM_HEAD, -1)
        kh = jnp.einsum('bcn,oc->bon', k, Wk).reshape(b, HEADS, DIM_HEAD, -1)
        vh = jnp.einsum('bcn,oc->bon', v, Wv).reshape(b, HEADS, DIM_HEAD, -1)
        qh = jax.nn.softmax(qh, axis=-2) * SCALE
        kh = jax.nn.softmax(kh, axis=-1)
        context = jnp.einsum('bhdn,bhen->bhde', kh, vh)
        out = jnp.einsum('bhde,bhdn->bhen', context, qh)
        out = out.reshape(b, HIDDEN, -1)
        out = jnp.einsum('bcn,oc->bon', out, Wo) + bo[None, :, None]
        norm = jnp.maximum(jnp.sqrt(jnp.sum(out * out, axis=1, keepdims=True)), 1e-12)
        return out / norm * g * np.sqrt(DIM)

    def _L0_ffn_ref(x, w1, s1, w2, s2, w3, s3):
        import jax, jax.numpy as jnp
        import numpy as np
        GROUP = 64

        def dequant_q40(w, s, out_features, in_features):
            msb = w >> 4
            lsb = (w & 15 ^ 8) - 8
            g = jnp.concatenate([msb, lsb], axis=1).reshape(-1, GROUP)
            deq = g.astype(s.dtype) * s[:, None]
            return deq.reshape(out_features, in_features)
        dim = x.shape[-1]
        hidden = w1.shape[0] * w1.shape[1] * 2 // dim
        W1 = dequant_q40(w1, s1, hidden, dim)
        W3 = dequant_q40(w3, s3, hidden, dim)
        W2 = dequant_q40(w2, s2, dim, hidden)
        a = jnp.einsum('bsd,hd->bsh', x, W1)
        b = jnp.einsum('bsd,hd->bsh', x, W3)
        h = jax.nn.silu(a) * b
        return jnp.einsum('bsh,dh->bsd', h, W2)
    x = x + _L0_attn_ref(_layernorm(x, axis=-1), L0_attn_Wqkv, L0_attn_q_ln_w, L0_attn_q_ln_b, L0_attn_k_ln_w, L0_attn_k_ln_b, L0_attn_Wout)
    x = x + _L0_xattn_ref(_layernorm(x, axis=-1), ctx_4096, ctx_4096, L0_xattn_Wq, L0_xattn_Wk, L0_xattn_Wv, L0_xattn_Wo, L0_xattn_bo, L0_xattn_g)
    x = x + _L0_ffn_ref(_layernorm(x, axis=-1), L0_ffn_w1, L0_ffn_s1, L0_ffn_w2, L0_ffn_s2, L0_ffn_w3, L0_ffn_s3)
    return x

_drawn_inputs = setup_inputs


def setup_inputs(seed=0):
    import zlib

    import numpy as np

    out = dict(_drawn_inputs(seed))
    spreads = {'L0_attn_q_ln_w': (1.0, 0.2),
     'L0_attn_q_ln_b': (0.0, 0.442),
     'L0_attn_k_ln_w': (1.0, 0.2),
     'L0_attn_k_ln_b': (0.0, 0.8),
     'L0_xattn_g': (1.0, 0.2)}
    factors = {}
    for name, (base, spread) in spreads.items():
        noise = np.random.default_rng([zlib.crc32(name.encode()), seed]).standard_normal(out[name].shape)
        drawn = base * np.exp(spread * noise) if base else spread * noise
        out[name] = jnp.asarray(drawn.astype(out[name].dtype))
    for name, factor in factors.items():
        out[name] = (out[name] * factor).astype(out[name].dtype)
    return out
```

```python
import concourse.bass as bass
from concourse import mybir
from contextlib import ExitStack

F32 = mybir.dt.float32
F32R = mybir.dt.float32r
I32 = mybir.dt.int32
ALU = mybir.AluOpType
ACT = mybir.ActivationFunctionType
AX = mybir.AxisListType

P = 128
NB = 16
D = 1024
KT = D // P
N = 512
HEADS, HD = 32, 32
HG = P // HD
G = HEADS // HG
CLIP = 8.0
EPS = 1e-5
ALIBI_MAX = 8.0
MASKED = -1e30
XO = 512
XD = 64
XT = XO // P
FF = 2752
GROUP = 64
NT = -(-FF // P)
CHUNKS = 4 * D // N
QKV_CHUNKS = 3 * D // N
PIECES = KT // 2
HALF = NB // 2
SL = HALF * P // N
DIM = P


def flat(ap):
    return ap.rearrange("p a b -> p (a b)")


class LayerNormT:

    def __init__(self, nc, sem, holds, source, rows, columns, ident, half_neg, banks, hi, lo, stats, moments):
        self.hold_dve, self.hold_pool = holds
        self.nc, self.source, self.rows, self.columns = nc, source, rows, columns
        self.ident, self.half_neg, self.banks, self.hi, self.lo = ident, half_neg, banks, hi, lo
        self.stats, self.moments = stats, moments
        self.loaded = [sem(f"ln_loaded{p}") for p in range(2)]
        self.stats_done = sem("ln_stats_done")
        self.aggregated = sem("ln_aggregated")
        self.moments_done = sem("ln_moments_done")
        self.rstd_done = sem("ln_rstd_done")
        self.normalised = sem("ln_normalised")
        self.transposed = sem("ln_transposed")
        self.hi_done = sem("ln_hi_done")
        self.lo_done = sem("ln_lo_done")

    def load(self, sp, done, pairs):
        with sp.Fori(0, pairs) as i:
            for p in range(2):
                sp.wait_ge(self.transposed, (done + i) * 2 + p + 1)
                sp.dma_start(self.rows[:, p, :], self.source[(done + i) * 2 + p, :, :]).then_inc(self.loaded[p], 16)

    def _stats(self, dve, n, p):
        nc = self.nc
        dve.wait_ge(self.loaded[p], (n + 1) * 16)
        nc.vector.bn_stats(self.stats[:, p, 0:6], self.rows[:, p, 0:N])
        nc.vector.bn_stats(self.stats[:, p, 6:12], self.rows[:, p, N:D]).then_inc(self.stats_done, 1)
        dve.wait_ge(self.stats_done, n * 2 + p + 1)
        self.hold_dve()
        nc.vector.bn_aggr(self.moments[:, p, 0:2], self.stats[:, p, :]).then_inc(self.aggregated, 1)
        dve.wait_ge(self.aggregated, n * 2 + p + 1)
        nc.vector.tensor_scalar(self.moments[:, p, 2:3], self.moments[:, p, 0:1], -1.0, None, ALU.mult)
        nc.vector.tensor_scalar(self.moments[:, p, 3:4], self.moments[:, p, 1:2], EPS, None, ALU.add).then_inc(
            self.moments_done, 1)

    def _lo(self, dve, n, p, at):
        dve.wait_ge(self.hi_done, n * 2 + p + 1)
        self.nc.vector.tensor_tensor(self.lo[:, at, :, :], self.banks[p],
                                     self.hi[:, at, :, :].bitcast(F32), ALU.subtract).then_inc(self.lo_done, 1)

    def vector(self, dve, done, pairs):
        self._stats(dve, done, 0)
        with dve.Fori(0, pairs - 1) as i:
            self._stats(dve, done + i, 1)
            self._lo(dve, done + i, 0, i * 2)
            self._stats(dve, done + i + 1, 0)
            self._lo(dve, done + i, 1, i * 2 + 1)
        last = done + pairs - 1
        self._stats(dve, last, 1)
        self._lo(dve, last, 0, pairs * 2 - 2)
        self._lo(dve, last, 1, pairs * 2 - 1)

    def gpsimd(self, pool, done, pairs):
        nc = self.nc
        with pool.Fori(0, pairs) as i:
            for p in range(2):
                t = (done + i) * 2 + p + 1
                pool.wait_ge(self.moments_done, t)
                nc.gpsimd.tensor_tensor(self.moments[:, p, 4:5], self.moments[:, p, 3:4], self.half_neg[:, :],
                                        ALU.pow).then_inc(self.rstd_done, 1)
                pool.wait_ge(self.rstd_done, t)
                self.hold_pool()
                nc.gpsimd.tensor_scalar(self.rows[:, p, :], self.rows[:, p, :], self.moments[:, p, 2:3],
                                        self.moments[:, p, 4:5], ALU.add, ALU.mult).then_inc(self.normalised, 1)

    def tensor(self, pe, done, pairs, banks_free=lambda: None):
        with pe.Fori(0, pairs) as i:
            for p in range(2):
                banks_free()
                t = (done + i) * 2 + p + 1
                pe.wait_ge(self.normalised, t)
                pe.wait_ge(self.lo_done, t)
                for k in range(KT):
                    last = self.nc.tensor.transpose(self.banks[p][:, k, :], self.columns(self.rows[:, p, :], k),
                                                    self.ident[:, :])
                last.then_inc(self.transposed, 1)

    def scalar(self, act, done, pairs):
        with act.Fori(0, pairs) as i:
            for p in range(2):
                act.wait_ge(self.transposed, (done + i) * 2 + p + 3)
                self.nc.scalar.activation(self.hi[:, i * 2 + p, :, :], self.banks[p], ACT.Copy).then_inc(self.hi_done, 1)


def program(nc, x, ctx_kv, w_attn, q_w, q_b, k_w, k_b, wqk, wv, wo, bo, g, w13, s13, w2, s2, shifts, out, qkv, x2):
    top = ExitStack()
    with top:
        def sb(name, shape, dt=F32, where=top):
            return where.enter_context(nc.sbuf_tensor(name, shape, dt))

        def pb(name, shape, where=top):
            return where.enter_context(nc.psum_tensor(name, shape, F32))

        def sem(name):
            return top.enter_context(nc.semaphore(name))

        ident = sb("ident", [P, P])
        half_neg = sb("half_neg", [P, 1])
        ln_stats = sb("ln_stats", [P, 2, 12])
        ln_moments = sb("ln_moments", [P, 2, 5])
        held = sb("held", [P, 2])

        def hold_dve():
            nc.vector.memset(held[:, 0:1], 0.0)

        def hold_pool():
            nc.gpsimd.tensor_tensor(held[:, 1:2], half_neg[:, :], half_neg[:, :], ALU.mult)

        holds = hold_dve, hold_pool
        constants(nc, sem, ident, half_neg)
        with ExitStack() as both:
            w_hi = [sb(f"w_hi{i}", [P, KT, N], F32R, both) for i in range(2)]
            w_lo = [sb(f"w_lo{i}", [P, KT, N], F32R, both) for i in range(2)]
            with ExitStack() as ph:
                qkv_phase(nc, sb, pb, sem, holds, ph, x, w_attn, qkv, ident, half_neg, ln_stats, ln_moments,
                          w_hi, w_lo)
            with ExitStack() as ph:
                attention_phase(nc, sb, pb, sem, holds, ph, x, ctx_kv, qkv, x2, q_w, q_b, k_w, k_b, wqk, wv, wo,
                                bo, g, ident, half_neg, w_hi, w_lo)
        with ExitStack() as ph:
            feed_forward_phase(nc, sb, pb, sem, holds, ph, w13, s13, w2, s2, shifts, x2, out, ident, half_neg,
                               ln_stats, ln_moments)


def constants(nc, sem, ident, half_neg):
    zeroed = sem("ident_zeroed")
    with nc.Block() as block:
        @block.gpsimd
        def _(pool):
            nc.gpsimd.memset(ident[:, :], 0.0).then_inc(zeroed, 1)
            pool.wait_ge(zeroed, 1)
            nc.gpsimd.affine_select(out=ident[:, :], in_=ident[:, :], compare_op=ALU.not_equal, fill=1.0, base=0,
                                    pattern=[[-1, P]], channel_multiplier=1)
            nc.gpsimd.memset(half_neg[:, :], -0.5)


def qkv_phase(nc, sb, pb, sem, holds, ph, x, w_attn, qkv, ident, half_neg, ln_stats, ln_moments, w_hi, w_lo):
    xT_hi = sb("xT_hi", [P, NB, KT, P], F32R, ph)
    xT_lo = sb("xT_lo", [P, NB, KT, P], F32R, ph)
    with ExitStack() as inner:
        rows = sb("qkv_rows", [P, 2, D], F32, inner)
        turn = [pb(f"qkv_turn{p}", [P, KT, P], inner) for p in range(2)]
        ln = LayerNormT(nc, lambda n: sem("x_" + n), holds, x, rows, lambda r, k: r[:, k * P:(k + 1) * P], ident, half_neg,
                        [t[:, :, :] for t in turn], xT_hi, xT_lo, ln_stats, ln_moments)
        with nc.Block() as block:
            @block.sync
            def _(sp):
                sp.sem_inc(ln.transposed, 2)
                ln.load(sp, 0, HALF)

            @block.vector
            def _(dve):
                dve.sem_inc(ln.lo_done, 2)
                ln.vector(dve, 0, HALF)

            @block.gpsimd
            def _(pool):
                ln.gpsimd(pool, 0, HALF)

            @block.tensor
            def _(pe):
                ln.tensor(pe, 0, HALF)

            @block.scalar
            def _(act):
                ln.scalar(act, 0, HALF)

    stage = [sb(f"w_stage{i}", [P, 2, N], F32, ph) for i in range(2)]
    res = [sb(f"qkv_out{i}", [P, N], F32, ph) for i in range(2)]
    BANKS = 4
    acc = pb("qkv_acc", [P, BANKS, N], ph)
    w_in = [sem(f"w_in{i}") for i in range(2)]
    w_hi_done = sem("w_hi_done")
    w_lo_done = sem("w_lo_done")
    mm_done = sem("qkv_mm_done")
    clipped = sem("qkv_clipped")
    stored = [sem(f"qkv_stored{i}") for i in range(2)]
    LOAD_AT = {0: 0, 3: 1, 6: 2, 9: 3}
    LO_AT = {2: 0, 5: 1, 8: 2, 11: 3}

    with nc.Block() as block:
        @block.sync
        def _(sp):
            def load(c, r, wait):
                if wait:
                    sp.wait_ge(w_lo_done, c * PIECES + r - 1)
                sp.dma_start(stage[r % 2][:, :, :], w_attn[c, :, 2 * r:2 * r + 2, :]).then_inc(w_in[r % 2], 16)

            for r in range(PIECES):
                load(0, r, r >= 2)
            with sp.Fori(0, QKV_CHUNKS // 2) as i:
                for h in range(2):
                    c = i * 2 + h
                    for t in range(NB):
                        if t in LOAD_AT:
                            load(c + 1, LOAD_AT[t], True)
                        sp.wait_ge(clipped, c * NB + t + 1 + BANKS)
                        sp.dma_start(qkv[t, :, bass.ds(c * N, N)], res[t % 2][:, :]).then_inc(stored[t % 2], 16)
            for r in range(PIECES):
                load(CHUNKS - 1, r, True)
            for p in range(2):
                sp.wait_ge(stored[p], 16 * (QKV_CHUNKS * NB // 2 + 1))

        @block.scalar
        def _(act):
            def high(c, r, dst):
                act.wait_ge(w_in[r % 2], (c * 2 + r // 2 + 1) * 16)
                nc.scalar.activation(dst[:, 2 * r:2 * r + 2, :], stage[r % 2][:, :, :], ACT.Copy).then_inc(w_hi_done, 1)

            act.sem_inc(stored[0], 16)
            act.sem_inc(stored[1], 16)
            for r in range(PIECES):
                high(0, r, w_hi[0])
            with act.Fori(0, QKV_CHUNKS // 2) as i:
                for h in range(2):
                    c = i * 2 + h
                    act.wait_ge(mm_done, c * NB + 1)
                    for r in range(PIECES):
                        high(c + 1, r, w_hi[1 - h])
            act.wait_ge(mm_done, QKV_CHUNKS * NB)
            for r in range(PIECES):
                high(CHUNKS - 1, r, w_hi[1])

        @block.vector
        def _(dve):
            def low(c, r, hi, lo):
                dve.wait_ge(w_hi_done, c * PIECES + r + 1)
                nc.vector.tensor_tensor(lo[:, 2 * r:2 * r + 2, :], stage[r % 2][:, :, :],
                                        hi[:, 2 * r:2 * r + 2, :].bitcast(F32), ALU.subtract).then_inc(w_lo_done, 1)

            for r in range(PIECES):
                low(0, r, w_hi[0], w_lo[0])
            with dve.Fori(0, QKV_CHUNKS // 2) as i:
                for h in range(2):
                    c = i * 2 + h
                    for t in range(NB):
                        dve.wait_ge(mm_done, c * NB + t + 1)
                        dve.wait_ge(stored[t % 2], (c * (NB // 2) + t // 2 + 1) * 16)
                        nc.vector.tensor_scalar(res[t % 2][:, :], acc[:, t % BANKS, :], CLIP, -CLIP, ALU.min,
                                                ALU.max).then_inc(clipped, 1)
                        if t in LO_AT:
                            low(c + 1, LO_AT[t], w_hi[1 - h], w_lo[1 - h])
            for r in range(PIECES):
                low(CHUNKS - 1, r, w_hi[1], w_lo[1])

        @block.tensor
        def _(pe):
            pe.sem_inc(clipped, BANKS)
            with pe.Fori(0, QKV_CHUNKS // 2) as i:
                for h in range(2):
                    c = i * 2 + h
                    pe.wait_ge(w_lo_done, (c + 1) * PIECES)
                    for t in range(NB):
                        pe.wait_ge(clipped, c * NB + t + 1)
                        product(nc, acc[:, t % BANKS, :],
                                [(a[:, t, k, :], b[:, k, :]) for k in range(KT)
                                 for a, b in ((xT_hi, w_hi[h]), (xT_hi, w_lo[h]), (xT_lo, w_hi[h]))]).then_inc(mm_done, 1)


def product(nc, out, pairs):
    for n, (left, right) in enumerate(pairs):
        last = nc.tensor.matmul(out, left, right, start=n == 0, stop=n == len(pairs) - 1)
    return last


def attention_phase(nc, sb, pb, sem, holds, ph, x, ctx_kv, qkv, x2, q_w, q_b, k_w, k_b, wqk, wv, wo, bo, g,
                    ident, half_neg, w_hi, w_lo):
    hold_dve, hold_pool = holds
    bias = sb("alibi", [P, HEADS, P], F32, ph)
    rel = sb("rel", [P, P], F32, ph)
    ones = sb("ones", [P, P], F32, ph)
    wq_sb = sb("wqk_sb", [P, 2, XO], F32, ph)
    wv_sb = sb("wv_sb", [P, XO], F32, ph)
    wo_sb = sb("wo_sb", [P, XT, P], F32, ph)
    affine = sb("affine", [P, 4, KT], F32, ph)
    bo_sb = sb("bo_sb", [P, 1], F32, ph)
    g_sb = sb("g_sb", [P, 1], F32, ph)
    qk_in = sb("qk_in", [P, 2, D], F32, ph)
    v_in = sb("v_in", [P, D], F32, ph)
    ctx_in = sb("ctx_in", [P, D], F32, ph)
    qk_stats = sb("qk_stats", [P, 2, 12], F32, ph)
    qk_mom = sb("qk_mom", [P, 2, 5], F32, ph)
    qkT = sb("qkT", [P, 2, KT, P], F32, ph)
    kD = sb("kD", [P, G, HG, P], F32, ph)
    SR = 3
    sc = sb("scores", [P, SR, HG, P], F32, ph)
    neg_max = sb("neg_max", [P, G, HG], F32, ph)
    row_sum = sb("row_sum", [P, G, HG], F32, ph)
    row_rec = sb("row_rec", [P, G, HG], F32, ph)
    probT = sb("probT", [P, 2, HG, P], F32, ph)
    oT_hi = sb("oT_hi", [P, KT, P], F32R, ph)
    oT_lo = sb("oT_lo", [P, KT, P], F32R, ph)
    x1 = sb("x1", [P, D], F32, ph)
    xn = sb("xn", [P, D], F32, ph)
    x1_stats = sb("x1_stats", [P, 12], F32, ph)
    x1_mom = sb("x1_mom", [P, 5], F32, ph)
    ctxT = sb("ctxT", [P, KT, P], F32, ph)
    kE = sb("kE", [P, D], F32, ph)
    kneg = sb("kneg", [P, XT], F32, ph)
    ksum = sb("ksum", [P, XT], F32, ph)
    krec = sb("krec", [P, 2, XT], F32, ph)
    kT = sb("kT", [P, KT, XO], F32, ph)
    mT = flat(probT[:, 0, :, :])
    cT = sb("cT", [P, XT, P], F32, ph)
    z = sb("z", [P, XT, P], F32, ph)
    qr = sb("qr", [P, SR, XO], F32, ph)
    q_max = sb("q_max", [P, KT, 8], F32, ph)
    q_sum = sb("q_sum", [P, KT, 8], F32, ph)
    q_rec = sb("q_rec", [P, KT, 8], F32, ph)
    qT = sb("qT", [P, XT, D], F32, ph)
    y = v_in
    y_sq = kE
    diag = xn[:, :].rearrange("p (a b) -> p a b", a=KT)
    n_sq = sb("n_sq", [P, 2, KT], F32, ph)
    neg8 = sb("neg8", [P, KT], F32, ph)

    bank_s = pb("bank_s", [P, N], ph)
    bank_q = pb("bank_q", [P, N], ph)
    bank_p = pb("bank_p", [P, HG, P], ph)
    bank_d = pb("bank_d", [P, XT, P], ph)
    pair_o = pb("pair_o", [P, 2 * N], ph)
    pair_k = pb("pair_k", [P, 2 * N], ph)
    turn4 = [bank_s[:, :].rearrange("p (a b) -> p a b", a=4), bank_q[:, :].rearrange("p (a b) -> p a b", a=4),
             bank_p[:, :, :], bank_d[:, :, :]]

    names = ("qk_loaded v_loaded x_loaded ctx_loaded stored setup_in setup_v setup_g "
             "qk_stats qk_aggr qk_mom qk_rstd qk_norm a_done a_out kd_out c_done c_out "
             "s_done s_biased s_max s_exp s_rec s_norm p_done p_out o_done o_hi o_lo "
             "q_done q_maxed q_subbed q_exped q_summed q_recced q_normed d_done d_out "
             "k_done k_maxed k_exped kt_done kt_out k_recced m_done m_out b_done b_out z_done z_out "
             "x_done x1_done x1_stats x1_aggr x1_mom x1_rstd x1_norm "
             "y_done y_out y_squared n_done n_clamped n_pow n_diag r_done y_scaled fin").split()
    s = {n: sem("a_" + n) for n in names}

    with nc.Block() as block:
        @block.sync
        def _(sp):
            sp.dma_start(wq_sb[:, :, :], wqk).then_inc(s["setup_in"], 16)
            sp.dma_start(wv_sb[:, :], wv).then_inc(s["setup_in"], 16)
            sp.dma_start(wo_sb[:, :, :], wo.rearrange("(a p) n -> p a n", p=P)).then_inc(s["setup_in"], 16)
            for i, v in enumerate((q_w, q_b, k_w, k_b)):
                sp.dma_start(affine[:, i, :], v).then_inc(s["setup_in"], 16)
            sp.dma_start(bo_sb[:, :], bo.rearrange("(p a) -> p a", a=1)).then_inc(s["setup_in"], 16)
            sp.dma_start(g_sb[:, :], g.rearrange("a p b -> p (a b)")).then_inc(s["setup_in"], 16)
            sp.wait_ge(s["setup_in"], 9 * 16)

        @block.gpsimd
        def _(pool):
            nc.gpsimd.iota(rel[:, :], [[1, P]], 0, channel_multiplier=-1, allow_small_or_imprecise_dtypes=True).then_inc(
                s["setup_g"], 1)
            nc.gpsimd.memset(ones[:, :], 1.0)
            nc.gpsimd.memset(neg8[:, :], -0.5)
            nc.gpsimd.memset(cT[:, :, :], 0.0)
            nc.gpsimd.memset(kD[:, :, :, :], 0.0)
            pool.wait_ge(s["setup_v"], 1)
            nc.gpsimd.affine_select(out=bias[:, :, :], in_=bias[:, :, :], compare_op=ALU.is_ge, fill=MASKED, base=0,
                                    pattern=[[0, HEADS], [-1, P]], channel_multiplier=1)

        @block.vector
        def _(dve):
            dve.wait_ge(s["setup_g"], 1)
            for h in range(HEADS):
                slope = 0.5 ** ((h + 1) * ALIBI_MAX / HEADS)
                ins = nc.vector.tensor_scalar(bias[:, h, :], rel[:, :], slope, None, ALU.mult)
            ins.then_inc(s["setup_v"], 1)
            dve.wait_ge(s["setup_in"], 9 * 16)
            nc.vector.tensor_scalar(g_sb[:, :], g_sb[:, :], float(DIM) ** 0.5, None, ALU.mult)

    STEPS = 12

    def k_tile(step):
        return (step - 1) // 2 if step in (1, 3, 5, 7) else None

    def kt_tile(step):
        return (step - 2) // 2 if step in (2, 4, 6, 8) else None

    def turn_sync(sp, b, own, cross):
        if own is not None:
            if own:
                sp.wait_ge(s["a_done"], b + 1)
                sp.dma_start(qk_in[:, :, :], qkv[b + 1, :, 0:2 * D].rearrange("p (a d) -> p a d", a=2)).then_inc(
                    s["qk_loaded"], 16)
                sp.wait_ge(s["k_done"], (b + 1) * XT)
                sp.dma_start(ctx_in[:, :], ctx_kv[b + 1, :, :]).then_inc(s["ctx_loaded"], 16)
                sp.wait_ge(s["o_done"], b + 1)
                if cross:
                    sp.wait_ge(s["fin"], b + 1)
                sp.dma_start(v_in[:, :], qkv[b + 1, :, 2 * D:3 * D]).then_inc(s["v_loaded"], 16)
        if cross:
            c = b - 1
            sp.wait_ge(s["fin"], c + 2)
            sp.dma_start(x2[c, :, :], x1[:, :]).then_inc(s["stored"], 16)
            sp.wait_ge(s["stored"], (c + 1) * 16)
            if own is not None:
                sp.dma_start(x1[:, :], x[b, :, :]).then_inc(s["x_loaded"], 16)

    def turn_tensor(pe, b, own, cross):
        c = b - 1
        if cross:
            pe.wait_ge(s["o_lo"], c + 1)
            for e in range(2):
                product(nc, pair_o[:, e * N:(e + 1) * N],
                        [(l[:, k, :], r[:, k, :]) for k in range(KT)
                         for l, r in ((oT_hi, w_hi[e]), (oT_hi, w_lo[e]), (oT_lo, w_hi[e]))]).then_inc(s["x_done"], 1)
        if own:
            pe.wait_ge(s["qk_norm"], b + 1)
            if cross:
                pe.wait_ge(s["s_biased"], b * G)
                pe.wait_ge(s["fin"], b)
                pe.wait_ge(s["p_out"], b * G)
            for n in range(4):
                for j in range(4):
                    last = nc.tensor.transpose(turn4[n][:, j, :], qk_in[:, n // 2, (n % 2 * 4 + j) * P:(n % 2 * 4 + j + 1) * P],
                                               ident[:, :])
            last.then_inc(s["a_done"], 1)
            pe.wait_ge(s["ctx_loaded"], (b + 1) * 16)
            if cross:
                pe.wait_ge(s["z_out"], b)
            for k in range(KT):
                last = nc.tensor.transpose(pair_k[:, k * P:(k + 1) * P], ctx_in[:, k * P:(k + 1) * P], ident[:, :])
            last.then_inc(s["c_done"], 1)
            pe.wait_ge(s["kd_out"], b + 1)
        for t in range(STEPS):
            if own and t < G:
                if t:
                    pe.wait_ge(s["s_biased"], b * G + t)
                nc.tensor.matmul(bank_s[:, :], qkT[:, 0, t, :], flat(kD[:, t, :, :]), start=True,
                                 stop=True).then_inc(s["s_done"], 1)
            n = t - 2
            if cross and 0 <= n < KT:
                if n == 0:
                    pe.wait_ge(s["x1_norm"], c + 1)
                else:
                    pe.wait_ge(s["q_subbed"], c * KT + n)
                nc.tensor.matmul(bank_q[:, :], xn[:, n * P:(n + 1) * P], wq_sb[:, 0, :], start=True,
                                 stop=True).then_inc(s["q_done"], 1)
            if own and (i := k_tile(t)) is not None:
                if i == 0:
                    pe.wait_ge(s["c_out"], b + 1)
                else:
                    pe.wait_ge(s["kt_out"], b * XT + i)
                for e in range(2):
                    last = nc.tensor.matmul(pair_k[:, e * N:(e + 1) * N], wq_sb[:, 1, i * P:(i + 1) * P],
                                            ctx_in[:, e * N:(e + 1) * N], start=True, stop=True)
                last.then_inc(s["k_done"], 1)
            if own and (i := kt_tile(t)) is not None:
                pe.wait_ge(s["k_exped"], b * XT + i + 1)
                for k in range(KT):
                    last = nc.tensor.transpose(pair_k[:, k * P:(k + 1) * P], kE[:, k * P:(k + 1) * P], ident[:, :])
                last.then_inc(s["kt_done"], 1)
            n = t - 2
            if own and 0 <= n < G:
                pe.wait_ge(s["s_norm"], b * G + n + 1)
                if n:
                    pe.wait_ge(s["p_out"], b * G + n)
                for j in range(HG):
                    last = nc.tensor.transpose(bank_p[:, j, :], sc[:, n % SR, j, :], ident[:, :])
                last.then_inc(s["p_done"], 1)
            n = t - 4
            if cross and 0 <= n < KT:
                pe.wait_ge(s["q_normed"], c * KT + n + 1)
                if n:
                    pe.wait_ge(s["d_out"], c * KT + n)
                for j in range(XT):
                    last = nc.tensor.transpose(bank_d[:, j, :], qr[:, n % SR, j * P:(j + 1) * P], ident[:, :])
                last.then_inc(s["d_done"], 1)
            n = t - 3
            if own and 0 <= n < G:
                if n == 0:
                    pe.wait_ge(s["v_loaded"], (b + 1) * 16)
                    if cross:
                        pe.wait_ge(s["x1_done"], 2 * (c + 1))
                pe.wait_ge(s["p_out"], b * G + n + 1)
                for j in range(HG):
                    h = n * HG + j
                    last = nc.tensor.matmul(pair_o[j * HD:(j + 1) * HD, n * P:(n + 1) * P], v_in[:, h * HD:(h + 1) * HD],
                                            probT[:, n % 2, j, :], start=True, stop=True)
                if n == G - 1:
                    last.then_inc(s["o_done"], 1)
        if cross:
            pe.wait_ge(s["d_out"], (c + 1) * KT)
            if own:
                pe.wait_ge(s["s_biased"], (b + 1) * G)
            for e, bank in enumerate((bank_s, bank_q)):
                for j in range(XT):
                    last = nc.tensor.matmul(bank[:, :], z[:, j, :], qT[:, j, e * N:(e + 1) * N], start=j == 0,
                                            stop=j == XT - 1)
            last.then_inc(s["y_done"], 1)
        if own:
            pe.wait_ge(s["kt_out"], (b + 1) * XT)
            for k in range(KT):
                last = nc.tensor.matmul(pair_k[:, 0:N], ctxT[:, k, :], kT[:, k, :], start=k == 0, stop=k == KT - 1)
            last.then_inc(s["m_done"], 1)
        if cross:
            pe.wait_ge(s["y_squared"], c + 1)
            for k in range(KT):
                last = nc.tensor.matmul(pair_k[:, N + k:N + k + 1], y_sq[:, k * P:(k + 1) * P], ones[:, 0:1],
                                        start=True, stop=True)
            last.then_inc(s["n_done"], 1)
        if own:
            pe.wait_ge(s["m_out"], b + 1)
            for j in range(XT):
                last = nc.tensor.matmul(pair_k[:, j * P:(j + 1) * P], wv_sb[:, j * P:(j + 1) * P],
                                        mT[:, j * P:(j + 1) * P], start=True, stop=True)
            last.then_inc(s["b_done"], 1)
            pe.wait_ge(s["b_out"], b + 1)
            if cross:
                pe.wait_ge(s["n_clamped"], c + 1)
            for j in range(XT):
                last = nc.tensor.matmul(pair_k[:, N + j * P:N + (j + 1) * P], cT[:, j, :], wo_sb[:, j, :],
                                        start=True, stop=True)
            last.then_inc(s["z_done"], 1)
        if cross:
            pe.wait_ge(s["n_diag"], c + 1)
            for e, bank in enumerate((bank_s, bank_q)):
                last = nc.tensor.matmul(bank[:, :], ones[:, :], flat(diag[:, 4 * e:4 * e + 4, :]), start=True, stop=True)
            last.then_inc(s["r_done"], 1)

    def turn_scalar(act, b, own, cross):
        c = b - 1
        if own:
            act.wait_ge(s["a_done"], b + 1)
            for n in range(4):
                for j in range(4):
                    i, k = n // 2, n % 2 * 4 + j
                    last = nc.scalar.activation(qkT[:, i, k, :], turn4[n][:, j, :], ACT.Identity,
                                                scale=affine[:, 2 * i, k:k + 1], bias=affine[:, 2 * i + 1, k:k + 1])
            last.then_inc(s["a_out"], 1)
            act.wait_ge(s["c_done"], b + 1)
            nc.scalar.activation(flat(ctxT[:, :, :]), pair_k[:, :], ACT.Copy).then_inc(s["c_out"], 1)
        for t in range(STEPS):
            if own and t < G:
                act.wait_ge(s["s_max"], b * G + t + 1)
                for j in range(HG):
                    last = nc.scalar.activation(sc[:, t % SR, j, :], sc[:, t % SR, j, :], ACT.Exp,
                                                bias=neg_max[:, t, j:j + 1], accum_out=row_sum[:, t, j:j + 1])
                last.then_inc(s["s_exp"], 1)
            n = t - 2
            if own and 0 <= n < G:
                act.wait_ge(s["p_done"], b * G + n + 1)
                nc.scalar.activation(probT[:, n % 2, :, :], bank_p[:, :, :], ACT.Copy).then_inc(s["p_out"], 1)
            if cross and 0 <= n < KT:
                act.wait_ge(s["q_subbed"], c * KT + n + 1)
                nc.scalar.activation(qr[:, n % SR, :], qr[:, n % SR, :], ACT.Exp).then_inc(s["q_exped"], 1)
            if own and (i := k_tile(t)) is not None:
                act.wait_ge(s["k_maxed"], b * XT + i + 1)
                nc.scalar.activation(kE[:, :], pair_k[:, :], ACT.Exp, bias=kneg[:, i:i + 1],
                                     accum_out=ksum[:, i:i + 1]).then_inc(s["k_exped"], 1)
            if own and (i := kt_tile(t)) is not None:
                act.wait_ge(s["kt_done"], b * XT + i + 1)
                nc.scalar.activation(kT[:, :, i * P:(i + 1) * P], pair_k[:, :].rearrange("p (a b) -> p a b", a=KT),
                                     ACT.Copy).then_inc(s["kt_out"], 1)
            n = t - 4
            if cross and 0 <= n < KT:
                act.wait_ge(s["d_done"], c * KT + n + 1)
                nc.scalar.activation(qT[:, :, n * P:(n + 1) * P], bank_d[:, :, :], ACT.Copy).then_inc(s["d_out"], 1)
        if own:
            act.wait_ge(s["o_done"], b + 1)
            nc.scalar.activation(flat(oT_hi[:, :, :]), pair_o[:, :], ACT.Copy).then_inc(s["o_hi"], 1)
        if cross:
            act.wait_ge(s["fin"], c + 1)
            act.wait_ge(s["y_done"], c + 1)
            for e, bank in enumerate((bank_s, bank_q)):
                last = nc.scalar.activation(y[:, e * N:(e + 1) * N], bank[:, :], ACT.Identity, bias=bo_sb[:, 0:1])
            last.then_inc(s["y_out"], 1)
            act.wait_ge(s["y_out"], c + 1)
            nc.scalar.activation(y_sq[:, :], y[:, :], ACT.Square).then_inc(s["y_squared"], 1)

    def turn_gpsimd(pool, b, own, cross):
        c = b - 1
        if own:
            pool.wait_ge(s["qk_mom"], b + 1)
            nc.gpsimd.tensor_tensor(qk_mom[:, :, 4], qk_mom[:, :, 3], neg8[:, 0:2], ALU.pow).then_inc(s["qk_rstd"], 1)
            pool.wait_ge(s["qk_rstd"], b + 1)
            hold_pool()
            for i in range(2):
                last = nc.gpsimd.tensor_scalar(qk_in[:, i, :], qk_in[:, i, :], qk_mom[:, i, 2:3], qk_mom[:, i, 4:5],
                                               ALU.add, ALU.mult)
            last.then_inc(s["qk_norm"], 1)
        if cross:
            pool.wait_ge(s["x1_mom"], c + 1)
            nc.gpsimd.tensor_tensor(x1_mom[:, 4:5], x1_mom[:, 3:4], neg8[:, 0:1], ALU.pow).then_inc(s["x1_rstd"], 1)
            pool.wait_ge(s["x1_rstd"], c + 1)
            hold_pool()
            nc.gpsimd.tensor_scalar(xn[:, :], x1[:, :], x1_mom[:, 2:3], x1_mom[:, 4:5], ALU.add, ALU.mult).then_inc(
                s["x1_norm"], 1)
        for t in range(STEPS):
            n = t - 1
            if own and 0 <= n < G:
                pool.wait_ge(s["s_rec"], b * G + n + 1)
                nc.gpsimd.tensor_tensor(sc[:, n % SR, :, :], sc[:, n % SR, :, :],
                                        row_rec[:, n, :].unsqueeze(2).to_broadcast([P, HG, P]),
                                        ALU.mult).then_inc(s["s_norm"], 1)
            n = t - 3
            if cross and 0 <= n < KT:
                pool.wait_ge(s["q_recced"], c * KT + n + 1)
                q = qr[:, n % SR, :].rearrange("p (h d) -> p h d", d=XD)
                nc.gpsimd.tensor_tensor(q, q, q_rec[:, n, :].unsqueeze(2).to_broadcast([P, 8, XD]),
                                        ALU.mult).then_inc(s["q_normed"], 1)
        if cross:
            pool.wait_ge(s["n_clamped"], c + 1)
            nc.gpsimd.tensor_tensor(n_sq[:, 1, :], n_sq[:, 0, :], neg8[:, :], ALU.pow).then_inc(s["n_pow"], 1)

    def turn_vector(dve, b, own, cross):
        c = b - 1
        if own:
            dve.wait_ge(s["qk_loaded"], (b + 1) * 16)
            for i in range(2):
                for e in range(2):
                    last = nc.vector.bn_stats(qk_stats[:, i, 6 * e:6 * e + 6], qk_in[:, i, e * N:(e + 1) * N])
            last.then_inc(s["qk_stats"], 1)
            dve.wait_ge(s["qk_stats"], b + 1)
            hold_dve()
            for i in range(2):
                last = nc.vector.bn_aggr(qk_mom[:, i, 0:2], qk_stats[:, i, :])
            last.then_inc(s["qk_aggr"], 1)
            dve.wait_ge(s["qk_aggr"], b + 1)
            nc.vector.tensor_scalar(qk_mom[:, :, 2], qk_mom[:, :, 0], -1.0, None, ALU.mult)
            nc.vector.tensor_scalar(qk_mom[:, :, 3], qk_mom[:, :, 1], EPS, None, ALU.add).then_inc(s["qk_mom"], 1)
        if cross:
            dve.wait_ge(s["x_loaded"], (c + 1) * 16)
            for e in range(2):
                dve.wait_ge(s["x_done"], 2 * c + e + 1)
                nc.vector.tensor_tensor(x1[:, e * N:(e + 1) * N], pair_o[:, e * N:(e + 1) * N],
                                        x1[:, e * N:(e + 1) * N], ALU.add).then_inc(s["x1_done"], 1)
                dve.wait_ge(s["x1_done"], 2 * c + e + 1)
                last = nc.vector.bn_stats(x1_stats[:, 6 * e:6 * e + 6], x1[:, e * N:(e + 1) * N])
            last.then_inc(s["x1_stats"], 1)
            dve.wait_ge(s["x1_stats"], c + 1)
            hold_dve()
            nc.vector.bn_aggr(x1_mom[:, 0:2], x1_stats[:, :]).then_inc(s["x1_aggr"], 1)
            dve.wait_ge(s["x1_aggr"], c + 1)
            nc.vector.tensor_scalar(x1_mom[:, 2:3], x1_mom[:, 0:1], -1.0, None, ALU.mult)
            nc.vector.tensor_scalar(x1_mom[:, 3:4], x1_mom[:, 1:2], EPS, None, ALU.add).then_inc(s["x1_mom"], 1)
        if own:
            dve.wait_ge(s["a_out"], b + 1)
            for j in range(HG):
                at = slice(j * HD, (j + 1) * HD)
                last = nc.vector.tensor_copy(kD[at, :, j, :], qkT[at, 1, :, :])
            last.then_inc(s["kd_out"], 1)
        for t in range(STEPS):
            if own and t < G:
                dve.wait_ge(s["s_done"], b * G + t + 1)
                nc.vector.scalar_tensor_tensor(flat(sc[:, t % SR, :, :]), bank_s[:, :], float(HD) ** -0.5,
                                               flat(bias[:, t * HG:(t + 1) * HG, :]), ALU.mult, ALU.add).then_inc(
                    s["s_biased"], 1)
                dve.wait_ge(s["s_biased"], b * G + t + 1)
                nc.vector.tensor_reduce(neg_max[:, t, :], sc[:, t % SR, :, :], AX.X, ALU.max, negate=True).then_inc(
                    s["s_max"], 1)
            n = t - 2
            if cross and 0 <= n < KT:
                dve.wait_ge(s["q_done"], c * KT + n + 1)
                nc.vector.tensor_reduce(q_max[:, n, :], bank_q[:, :].rearrange("p (h d) -> p h d", d=XD), AX.X,
                                        ALU.max).then_inc(s["q_maxed"], 1)
                dve.wait_ge(s["q_maxed"], c * KT + n + 1)
                nc.vector.tensor_tensor(qr[:, n % SR, :].rearrange("p (h d) -> p h d", d=XD),
                                        bank_q[:, :].rearrange("p (h d) -> p h d", d=XD),
                                        q_max[:, n, :].unsqueeze(2).to_broadcast([P, 8, XD]),
                                        ALU.subtract).then_inc(s["q_subbed"], 1)
            if own and (i := k_tile(t)) is not None:
                dve.wait_ge(s["k_done"], b * XT + i + 1)
                nc.vector.tensor_reduce(kneg[:, i:i + 1], pair_k[:, :], AX.X, ALU.max, negate=True).then_inc(
                    s["k_maxed"], 1)
            if own and t < G:
                dve.wait_ge(s["s_exp"], b * G + t + 1)
                nc.vector.reciprocal(row_rec[:, t, :], row_sum[:, t, :]).then_inc(s["s_rec"], 1)
            n = t - 2
            if cross and 0 <= n < KT:
                dve.wait_ge(s["q_exped"], c * KT + n + 1)
                nc.vector.tensor_reduce(q_sum[:, n, :], qr[:, n % SR, :].rearrange("p (h d) -> p h d", d=XD), AX.X,
                                        ALU.add).then_inc(s["q_summed"], 1)
                dve.wait_ge(s["q_summed"], c * KT + n + 1)
                nc.vector.reciprocal(q_rec[:, n, :], q_sum[:, n, :]).then_inc(s["q_recced"], 1)
        if own:
            dve.wait_ge(s["o_hi"], b + 1)
            nc.vector.tensor_tensor(flat(oT_lo[:, :, :]), pair_o[:, :], flat(oT_hi[:, :, :].bitcast(F32)),
                                    ALU.subtract).then_inc(s["o_lo"], 1)
            dve.wait_ge(s["k_exped"], (b + 1) * XT)
            nc.vector.reciprocal(krec[:, 0, :], ksum[:, :]).then_inc(s["k_recced"], 1)
            dve.wait_ge(s["m_done"], b + 1)
            nc.vector.tensor_copy(mT[:, :], pair_k[:, 0:N]).then_inc(s["m_out"], 1)
            dve.wait_ge(s["k_recced"], 2 * b + 1)
            nc.vector.tensor_scalar(krec[:, 1, :], krec[:, 0, :], float(XD) ** -0.5, None, ALU.mult).then_inc(
                s["k_recced"], 1)
        if cross:
            dve.wait_ge(s["n_done"], c + 1)
            nc.vector.tensor_scalar(n_sq[:, 0, :], pair_k[:, N:N + KT], 1e-24, None, ALU.max).then_inc(s["n_clamped"], 1)
        if own:
            dve.wait_ge(s["b_done"], b + 1)
            for j in range(2):
                at = slice(j * XD, (j + 1) * XD)
                last = nc.vector.tensor_copy(cT[at, :, at], pair_k[at, 0:N].rearrange("p (a b) -> p a b", a=XT)[:, :, at])
            last.then_inc(s["b_out"], 1)
        if cross:
            dve.wait_ge(s["n_pow"], c + 1)
            nc.vector.tensor_tensor(diag[:, :, :], ident[:, :].unsqueeze(1).to_broadcast([P, KT, P]),
                                    n_sq[:, 1, :].unsqueeze(2).to_broadcast([P, KT, P]), ALU.mult).then_inc(s["n_diag"], 1)
        if own:
            dve.wait_ge(s["k_recced"], 2 * (b + 1))
            dve.wait_ge(s["z_done"], b + 1)
            for j in range(XT):
                last = nc.vector.tensor_scalar(z[:, j, :], pair_k[:, N + j * P:N + (j + 1) * P], krec[:, 1, j:j + 1], None,
                                               ALU.mult)
            last.then_inc(s["z_out"], 1)
        if cross:
            dve.wait_ge(s["r_done"], c + 1)
            for e, bank in enumerate((bank_s, bank_q)):
                last = nc.vector.tensor_tensor(y[:, e * N:(e + 1) * N], y[:, e * N:(e + 1) * N], bank[:, :], ALU.mult)
            last.then_inc(s["y_scaled"], 1)
            dve.wait_ge(s["y_scaled"], c + 1)
            nc.vector.scalar_tensor_tensor(x1[:, :], y[:, :], g_sb[:, 0:1], x1[:, :], ALU.mult, ALU.add).then_inc(
                s["fin"], 1)

    def turns(eng, turn):
        turn(eng, 0, True, False)
        with eng.Fori(1, NB) as b:
            turn(eng, b, True, True)
        turn(eng, NB, False, True)

    with nc.Block() as block:
        @block.sync
        def _(sp):
            sp.dma_start(qk_in[:, :, :], qkv[0, :, 0:2 * D].rearrange("p (a d) -> p a d", a=2)).then_inc(
                s["qk_loaded"], 16)
            sp.dma_start(ctx_in[:, :], ctx_kv[0, :, :]).then_inc(s["ctx_loaded"], 16)
            sp.dma_start(v_in[:, :], qkv[0, :, 2 * D:3 * D]).then_inc(s["v_loaded"], 16)
            sp.dma_start(x1[:, :], x[0, :, :]).then_inc(s["x_loaded"], 16)
            turn_sync(sp, 0, True, False)
            with sp.Fori(1, NB - 1) as b:
                turn_sync(sp, b, True, True)
            turn_sync(sp, NB - 1, False, True)
            turn_sync(sp, NB, None, True)
            sp.wait_ge(s["stored"], NB * 16)

        @block.gpsimd
        def _(pool):
            turns(pool, turn_gpsimd)

        @block.scalar
        def _(act):
            turns(act, turn_scalar)

        @block.vector
        def _(dve):
            dve.sem_inc(s["fin"], 1)
            turns(dve, turn_vector)

        @block.tensor
        def _(pe):
            turns(pe, turn_tensor)


def feed_forward_phase(nc, sb, pb, sem, holds, ph, w13, s13, w2, s2, shifts, x2, out, ident, half_neg, ln_stats, ln_moments):
    GROUPS = NT // 2
    acc = sb("acc", [P, HALF, D], F32, ph)
    xT_hi = sb("h_xT_hi", [P, HALF, KT, P], F32R, ph)
    xT_lo = sb("h_xT_lo", [P, HALF, KT, P], F32R, ph)
    w13_hi = [sb(f"w13_hi{i}", [P, 2, KT, P], F32R, ph) for i in range(2)]
    w13_lo = [sb(f"w13_lo{i}", [P, 2, KT, P], F32R, ph) for i in range(2)]
    w2_hi = [sb(f"w2_hi{i}", [P, 2, N], F32R, ph) for i in range(3)]
    w2_lo = [sb(f"w2_lo{i}", [P, 2, N], F32R, ph) for i in range(3)]
    h_hi = [sb(f"h_hi{i}", [P, HALF * P], F32R, ph) for i in range(3)]
    h_lo = [sb(f"h_lo{i}", [P, HALF * P], F32R, ph) for i in range(3)]
    words = [sb(f"words{i}", [P, D], I32, ph) for i in range(3)]
    sc13 = sb("sc13", [P, 2, P], F32, ph)
    sc2 = sb("sc2", [P, D], F32, ph)
    shift = sb("shift", [P, 6], I32, ph)
    gate = [sb(f"gate{i}", [P, N], F32, ph) for i in range(2)]
    ps = [pb(f"ff_ps{i}", [P, N], ph) for i in range(4)]
    po = pb("ff_po", [P, 4, N], ph)

    names = ("shifts acc_loaded stored w1_in w3_in w2_in s13_in s2_in shifted scaled split_hi split_lo "
             "ab_done gated product h_hi h_lo y_done added").split()
    s = {n: sem("f_" + n) for n in names}
    split = [sem(f"f_split_{n}") for n in ("w1", "w3", "w2")]
    loaded = [s["w1_in"], s["w3_in"], s["w2_in"]]

    def columns(rows, k):
        return rows.rearrange("p (q k) -> p k q", k=KT)[:, k, :]

    turn = [po[:, 2 * p:2 * p + 2, :].rearrange("p a (b c) -> p (a b) c", c=P) for p in range(2)]
    rows = sb("h_rows", [P, 2, D], F32, ph)
    ln = LayerNormT(nc, lambda n: sem("h_" + n), holds, x2, rows, columns, ident, half_neg, turn, xT_hi, xT_lo,
                    ln_stats, ln_moments)
    OUTS = 2 * HALF
    FULL_GROUPS = GROUPS - 1

    def groups(eng, group):
        group(0, 0, True)
        with eng.Fori(0, FULL_GROUPS // 2) as i:
            group(i * 2 + 1, 1, False)
            group(i * 2 + 2, 0, False)

    with nc.Block() as block:
        @block.sync
        def _(sp):
            def load13(tile, count):
                for mat in range(2):
                    if count is not None:
                        sp.wait_ge(split[mat], count)
                    sp.dma_start(words[mat][:, :], w13[tile, mat, :, :]).then_inc(loaded[mat], 16)
                    if mat == 0:
                        if count is not None:
                            sp.wait_ge(s["scaled"], count * 3 - 1)
                        sp.dma_start(sc13[:, :, :], s13[tile, :, :, :]).then_inc(s["s13_in"], 16)

            def load2(tile, u):
                sp.wait_ge(split[2], u + 1)
                for a in range(2):
                    at = slice(a * 64, a * 64 + 64)
                    sp.dma_start(words[2][at, 0:N], w2[tile, :, :]).then_inc(s["w2_in"], 16)
                    sp.dma_start(words[2][at, N:D], w2[tile + FF // P + a, :, :]).then_inc(s["w2_in"], 16)
                    sp.dma_start(sc2[at, :], s2[bass.ds(tile * 2 + a, 1), :].to_broadcast([64, D])).then_inc(
                        s["w2_in"], 16)

            sp.sem_inc(ln.transposed, 2)
            sp.sem_inc(split[2], 1)
            sp.sem_inc(s["stored"], 16)
            sp.dma_start(shift[:, :], shifts).then_inc(s["shifts"], 16)
            load13(0, None)
            with sp.Fori(0, 2) as hf:
                sp.wait_ge(s["stored"], hf * (HALF * 16) + 16)
                for t in range(HALF):
                    sp.dma_start(acc[:, t, :], x2[hf * HALF + t, :, :]).then_inc(s["acc_loaded"], 16)
                ln.load(sp, hf * (HALF // 2), HALF // 2)

                def group(j, parity, first):
                    for e in range(2):
                        tile = j * 2 + e
                        u = hf * NT + tile
                        load13(tile + 1, u + 1)
                        load2(tile, u)

                groups(sp, group)
                for t in range(HALF):
                    sp.wait_ge(s["added"], (hf * GROUPS + GROUPS - 1) * OUTS + 2 * t + 2 + 4)
                    sp.dma_start(out[hf * HALF + t, :, :], acc[:, t, :]).then_inc(s["stored"], 16)
            sp.wait_ge(s["stored"], 16 + NB * 16)

        @block.gpsimd
        def _(pool):
            with pool.Fori(0, 2) as hf:
                ln.gpsimd(pool, hf * (HALF // 2), HALF // 2)

        @block.scalar
        def _(act):
            def high(mat, dst, count):
                act.wait_ge(s["scaled"], count)
                src = words[mat][:, :].bitcast(F32)
                nc.scalar.activation(dst, src, ACT.Copy).then_inc(s["split_hi"], 1)

            def tile(u, e, slot, first):
                act.wait_ge(s["ab_done"], u * 4 + 1)
                for mat in range(2):
                    high(mat, flat(w13_hi[1 - e][:, mat, :, :]), u * 3 + 3 + mat)
                if e == 1 and not first:
                    act.wait_ge(s["y_done"], (u - 1) * (OUTS // 2))
                high(2, flat(w2_hi[slot][:, :, :]), u * 3 + 5)
                for sl in range(SL):
                    act.wait_ge(s["h_lo"], u * 2 + sl + 1)
                    act.wait_ge(s["ab_done"], u * 4 + 2 * sl + 2)
                    nc.scalar.activation(gate[sl][:, :], ps[2 * sl][:, :], ACT.Silu).then_inc(s["gated"], 1)
                    act.wait_ge(s["product"], u * 2 + sl + 3)
                    nc.scalar.activation(h_hi[slot][:, sl * N:(sl + 1) * N], gate[sl][:, :], ACT.Copy).then_inc(
                        s["h_hi"], 1)

            for mat in range(2):
                high(mat, flat(w13_hi[0][:, mat, :, :]), mat + 1)
            with act.Fori(0, 2) as hf:
                ln.scalar(act, hf * (HALF // 2), HALF // 2)

                def group(j, parity, first):
                    for e in range(2):
                        tile(hf * NT + j * 2 + e, e, 2 if e else parity, first)

                groups(act, group)

        @block.vector
        def _(dve):
            def unpack(mat, count):
                w = words[mat]
                for kind, at in ((0, slice(0, D)),) if mat < 2 else ((1, slice(0, N)), (2, slice(N, D))):
                    last = nc.vector.tensor_scalar(w[:, at], w[:, at], shift[:, 2 * kind:2 * kind + 1],
                                                   shift[:, 2 * kind + 1:2 * kind + 2], ALU.logical_shift_left,
                                                   ALU.arith_shift_right)
                last.then_inc(s["shifted"], 1)
                if mat < 2:
                    dst, src = [v.rearrange("p (k n) -> p k n", k=KT) for v in (w[:, :].bitcast(F32), w[:, :])]
                    scale = sc13[:, mat, :].unsqueeze(1).to_broadcast([P, KT, P])
                else:
                    dst, src, scale = w[:, :].bitcast(F32), w[:, :], sc2[:, :]
                dve.wait_ge(s["shifted"], count + 1)
                nc.vector.tensor_tensor(dst, src, scale, ALU.mult).then_inc(s["scaled"], 1)

            def low(mat, dst, hi, count):
                dve.wait_ge(s["split_hi"], count + 1)
                nc.vector.tensor_tensor(dst, words[mat][:, :].bitcast(F32), hi.bitcast(F32), ALU.subtract).then_inc(
                    split[mat], 1)

            def low13(e, mat, count):
                low(mat, flat(w13_lo[e][:, mat, :, :]), flat(w13_hi[e][:, mat, :, :]), count)

            def tile(u, e, slot):
                for mat in range(2):
                    dve.wait_ge(loaded[mat], (u + 2) * 16)
                    if mat == 0:
                        dve.wait_ge(s["s13_in"], (u + 2) * 16)
                    unpack(mat, u * 3 + 2 + mat)
                low13(1 - e, 0, u * 3 + 2)
                dve.wait_ge(s["w2_in"], (u + 1) * 96)
                unpack(2, u * 3 + 4)
                low13(1 - e, 1, u * 3 + 3)
                low(2, flat(w2_lo[slot][:, :, :]), flat(w2_hi[slot][:, :, :]), u * 3 + 4)
                for sl in range(SL):
                    dve.wait_ge(s["gated"], u * 2 + sl + 1)
                    dve.wait_ge(s["ab_done"], u * 4 + 2 * sl + 3)
                    nc.vector.tensor_tensor(gate[sl][:, :], gate[sl][:, :], ps[2 * sl + 1][:, :], ALU.mult).then_inc(
                        s["product"], 1)
                    dve.wait_ge(s["h_hi"], u * 2 + sl + 1)
                    at = slice(sl * N, (sl + 1) * N)
                    nc.vector.tensor_tensor(h_lo[slot][:, at], gate[sl][:, :], h_hi[slot][:, at].bitcast(F32),
                                            ALU.subtract).then_inc(s["h_lo"], 1)

            def add(gj):
                for o in range(OUTS):
                    t, par = o // 2, o % 2
                    dve.wait_ge(s["y_done"], gj * OUTS + o + 1)
                    cols = acc[:, t, :].rearrange("p (n two) -> p two n", two=2)[:, par, :]
                    nc.vector.tensor_tensor(cols, po[:, o % 4, :], cols, ALU.add).then_inc(s["added"], 1)

            dve.sem_inc(ln.lo_done, 2)
            dve.sem_inc(s["h_lo"], 2)
            dve.wait_ge(s["shifts"], 16)
            for mat in range(2):
                dve.wait_ge(loaded[mat], 16)
                if mat == 0:
                    dve.wait_ge(s["s13_in"], 16)
                unpack(mat, mat)
                low13(0, mat, mat)
            with dve.Fori(0, 2) as hf:
                ln.vector(dve, hf * (HALF // 2), HALF // 2)
                dve.wait_ge(s["acc_loaded"], (hf + 1) * (HALF * 16))

                def group(j, parity, first):
                    tile(hf * NT + j * 2, 0, parity)
                    if not first:
                        add(hf * GROUPS + j - 1)
                    tile(hf * NT + j * 2 + 1, 1, 2)

                groups(dve, group)
                add(hf * GROUPS + GROUPS - 1)

        @block.tensor
        def _(pe):
            def ab(u, e, hf=None):
                for mat in range(2):
                    pe.wait_ge(split[mat], u + 1)
                for sl in range(SL):
                    if hf is not None:
                        pe.wait_ge(ln.lo_done, hf * HALF + sl * 4 + 6)
                    pe.wait_ge(s["product"], u * 2 + sl + 1)
                    for mat in range(2):
                        at = slice(sl * 4, sl * 4 + 4)
                        product(nc, ps[2 * sl + mat][:, :].rearrange("p (a b) -> p a b", a=4),
                                [(l[:, mat, k, :], r[:, at, k, :]) for k in range(KT)
                                 for l, r in ((w13_hi[e], xT_hi), (w13_hi[e], xT_lo), (w13_lo[e], xT_hi))]).then_inc(
                            s["ab_done"], 1)

            def outputs(gj, slots):
                pe.wait_ge(s["h_lo"], (gj + 1) * 4 + 2)
                pe.wait_ge(split[2], (gj + 1) * 2 + 1)
                for o in range(OUTS):
                    t, par = o // 2, o % 2
                    at = slice(t * P, (t + 1) * P)
                    pe.wait_ge(s["added"], gj * OUTS + o + 1)
                    product(nc, po[:, o % 4, :],
                            [(l[i][:, at], r[i][:, par, :]) for i in slots
                             for l, r in ((h_hi, w2_hi), (h_hi, w2_lo), (h_lo, w2_hi))]).then_inc(s["y_done"], 1)

            pe.sem_inc(s["added"], 4)
            pe.sem_inc(s["product"], 2)
            pe.sem_inc(s["ab_done"], 1)
            with pe.Fori(0, 2) as hf:
                ln.tensor(pe, hf * (HALF // 2), HALF // 2, lambda: pe.wait_ge(s["added"], hf * (GROUPS * OUTS) + 4))

                def group(j, parity, first):
                    ab(hf * NT + j * 2, 0, hf if first else None)
                    if not first:
                        outputs(hf * GROUPS + j - 1, (1 - parity, 2))
                    ab(hf * NT + j * 2 + 1, 1)

                groups(pe, group)
                outputs(hf * GROUPS + GROUPS - 1, (0, 2))


def lay_out_ffn(w1, s1, w2, s2, w3, s3):
    import numpy as np

    pad = NT * P - FF

    def words(w):
        w = np.asarray(w).reshape(FF, 8, 1, 8, 8).repeat(2, axis=2)
        w = np.concatenate([w, np.zeros((pad,) + w.shape[1:], w.dtype)])
        return w.reshape(NT, P, P, 8).transpose(0, 2, 3, 1)

    def scales(s):
        s = np.asarray(s).reshape(FF, 16).repeat(8, axis=1)
        s = np.concatenate([s, np.zeros((pad, P), s.dtype)])
        return s.reshape(NT, P, P).transpose(0, 2, 1)

    w13 = np.stack([words(w1), words(w3)], 1).reshape(NT, 2, P, 8 * P)
    s13 = np.stack([scales(s1), scales(s3)], 2)
    w13, s13 = [np.concatenate([v, v[:1]]) for v in (w13, s13)]
    rows = FF // GROUP
    w2 = np.asarray(w2).reshape(D // 2, rows, GROUP).transpose(1, 2, 0)
    w2 = np.concatenate([w2, np.zeros((1, GROUP, D // 2), w2.dtype)])
    s2 = np.asarray(s2).reshape(D // 2, 2, rows).transpose(2, 1, 0).reshape(rows, D)
    s2 = np.concatenate([s2, np.zeros((1, D), s2.dtype)])
    high, low = (0, 4), (28, 28)
    shifts = np.array([(high, low)[p // 8 % 2] + (high, low)[p // 64] + (low, high)[p // 64] for p in range(P)],
                      np.int32)
    return [np.ascontiguousarray(v) for v in (w13, s13, w2, s2, shifts)]


def kernel(**inputs):
    import numpy as np
    import concourse.bacc as bacc
    from concourse.bass_utils import run_bass_kernel_spmd

    a = {name: np.asarray(value) for name, value in inputs.items()}

    w_attn = np.concatenate([a["L0_attn_Wqkv"], a["L0_attn_Wout"]])
    vectors = [a["L0_attn_" + n].reshape(KT, P).T for n in ("q_ln_w", "q_ln_b", "k_ln_w", "k_ln_b")]
    w13, s13, w2, s2, shifts = lay_out_ffn(*[a["L0_ffn_" + n] for n in ("w1", "s1", "w2", "s2", "w3", "s3")])
    laid_out = dict(
        x=a["x"],
        context=a["ctx_4096"],
        w_attn=w_attn.reshape(CHUNKS, N, KT, P).transpose(0, 3, 2, 1),
        q_w=vectors[0], q_b=vectors[1], k_w=vectors[2], k_b=vectors[3],
        wqk=np.stack([a["L0_xattn_Wq"].T, a["L0_xattn_Wk"].T], 1),
        wv=a["L0_xattn_Wv"].T,
        wo=a["L0_xattn_Wo"].T,
        bo=a["L0_xattn_bo"],
        g=a["L0_xattn_g"],
        w13=w13, s13=s13, w2=w2, s2=s2, shifts=shifts)

    nc = bacc.Bacc("TRN2", target_bir_lowering=False, num_devices=1)
    arrays, args = {}, []
    for name, value in laid_out.items():
        value = np.ascontiguousarray(value)
        arrays[f"in_{name}"] = value
        args.append(nc.dram_tensor(f"in_{name}", value.shape, mybir.dt.from_np(value.dtype),
                                   kind="ExternalInput").ap())
    out = nc.dram_tensor("out_0", (NB, P, D), F32, kind="ExternalOutput").ap()
    qkv = nc.dram_tensor("qkv", (NB, P, 3 * D), F32).ap()
    x2 = nc.dram_tensor("x2", (NB, P, D), F32).ap()
    program(nc, *args, out, qkv, x2)
    r = run_bass_kernel_spmd(nc, [arrays], core_ids=[0])
    return r.results[0]["out_0"]
```

```python
import concourse.bass as bass
from concourse import mybir
from contextlib import ExitStack

F32 = mybir.dt.float32
F32R = mybir.dt.float32r
I32 = mybir.dt.int32
ALU = mybir.AluOpType
ACT = mybir.ActivationFunctionType
AX = mybir.AxisListType

P = 128
NB = 16
D = 1024
KT = D // P
N = 512
HEADS, HD = 32, 32
HG = P // HD
G = HEADS // HG
CLIP = 8.0
EPS = 1e-5
ALIBI_MAX = 8.0
MASKED = -1e30
XO = 512
XD = 64
XT = XO // P
FF = 2752
GROUP = 64
NT = -(-FF // P)
CHUNKS = 4 * D // N
QKV_CHUNKS = 3 * D // N
PIECES = KT // 2
HALF = NB // 2
SL = HALF * P // N
DIM = P


def flat(ap):
    return ap.rearrange("p a b -> p (a b)")


class LayerNormT:

    def __init__(self, nc, sem, holds, source, rows, columns, ident, half_neg, banks, hi, lo, stats, moments):
        self.hold_dve, self.hold_pool = holds
        self.nc, self.source, self.rows, self.columns = nc, source, rows, columns
        self.ident, self.half_neg, self.banks, self.hi, self.lo = ident, half_neg, banks, hi, lo
        self.stats, self.moments = stats, moments
        self.loaded = [sem(f"ln_loaded{p}") for p in range(2)]
        self.stats_done = sem("ln_stats_done")
        self.aggregated = sem("ln_aggregated")
        self.moments_done = sem("ln_moments_done")
        self.rstd_done = sem("ln_rstd_done")
        self.normalised = sem("ln_normalised")
        self.transposed = sem("ln_transposed")
        self.hi_done = sem("ln_hi_done")
        self.lo_done = sem("ln_lo_done")

    def load(self, sp, done, pairs):
        with sp.Fori(0, pairs) as i:
            for p in range(2):
                sp.wait_ge(self.transposed, (done + i) * 2 + p + 1)
                sp.dma_start(self.rows[:, p, :], self.source[(done + i) * 2 + p, :, :]).then_inc(self.loaded[p], 16)

    def _stats(self, dve, n, p):
        nc = self.nc
        dve.wait_ge(self.loaded[p], (n + 1) * 16)
        nc.vector.bn_stats(self.stats[:, p, 0:6], self.rows[:, p, 0:N])
        nc.vector.bn_stats(self.stats[:, p, 6:12], self.rows[:, p, N:D]).then_inc(self.stats_done, 1)
        dve.wait_ge(self.stats_done, n * 2 + p + 1)
        self.hold_dve()
        nc.vector.bn_aggr(self.moments[:, p, 0:2], self.stats[:, p, :]).then_inc(self.aggregated, 1)
        dve.wait_ge(self.aggregated, n * 2 + p + 1)
        nc.vector.tensor_scalar(self.moments[:, p, 2:3], self.moments[:, p, 0:1], -1.0, None, ALU.mult)
        nc.vector.tensor_scalar(self.moments[:, p, 3:4], self.moments[:, p, 1:2], EPS, None, ALU.add).then_inc(
            self.moments_done, 1)

    def _lo(self, dve, n, p, at):
        dve.wait_ge(self.hi_done, n * 2 + p + 1)
        self.nc.vector.tensor_tensor(self.lo[:, at, :, :], self.banks[p],
                                     self.hi[:, at, :, :].bitcast(F32), ALU.subtract).then_inc(self.lo_done, 1)

    def vector(self, dve, done, pairs):
        self._stats(dve, done, 0)
        with dve.Fori(0, pairs - 1) as i:
            self._stats(dve, done + i, 1)
            self._lo(dve, done + i, 0, i * 2)
            self._stats(dve, done + i + 1, 0)
            self._lo(dve, done + i, 1, i * 2 + 1)
        last = done + pairs - 1
        self._stats(dve, last, 1)
        self._lo(dve, last, 0, pairs * 2 - 2)
        self._lo(dve, last, 1, pairs * 2 - 1)

    def gpsimd(self, pool, done, pairs):
        nc = self.nc
        with pool.Fori(0, pairs) as i:
            for p in range(2):
                t = (done + i) * 2 + p + 1
                pool.wait_ge(self.moments_done, t)
                nc.gpsimd.tensor_tensor(self.moments[:, p, 4:5], self.moments[:, p, 3:4], self.half_neg[:, :],
                                        ALU.pow).then_inc(self.rstd_done, 1)
                pool.wait_ge(self.rstd_done, t)
                self.hold_pool()
                nc.gpsimd.tensor_scalar(self.rows[:, p, :], self.rows[:, p, :], self.moments[:, p, 2:3],
                                        self.moments[:, p, 4:5], ALU.add, ALU.mult).then_inc(self.normalised, 1)

    def tensor(self, pe, done, pairs, banks_free=lambda: None):
        with pe.Fori(0, pairs) as i:
            for p in range(2):
                banks_free()
                t = (done + i) * 2 + p + 1
                pe.wait_ge(self.normalised, t)
                pe.wait_ge(self.lo_done, t)
                for k in range(KT):
                    last = self.nc.tensor.transpose(self.banks[p][:, k, :], self.columns(self.rows[:, p, :], k),
                                                    self.ident[:, :])
                last.then_inc(self.transposed, 1)

    def scalar(self, act, done, pairs):
        with act.Fori(0, pairs) as i:
            for p in range(2):
                act.wait_ge(self.transposed, (done + i) * 2 + p + 3)
                self.nc.scalar.activation(self.hi[:, i * 2 + p, :, :], self.banks[p], ACT.Copy).then_inc(self.hi_done, 1)


def program(nc, x, ctx_kv, w_attn, q_w, q_b, k_w, k_b, wqk, wv, wo, bo, g, w13, s13, w2, s2, shifts, out, qkv, x2):
    top = ExitStack()
    with top:
        def sb(name, shape, dt=F32, where=top):
            return where.enter_context(nc.sbuf_tensor(name, shape, dt))

        def pb(name, shape, where=top):
            return where.enter_context(nc.psum_tensor(name, shape, F32))

        def sem(name):
            return top.enter_context(nc.semaphore(name))

        ident = sb("ident", [P, P])
        half_neg = sb("half_neg", [P, 1])
        ln_stats = sb("ln_stats", [P, 2, 12])
        ln_moments = sb("ln_moments", [P, 2, 5])
        held = sb("held", [P, 3])

        def hold_dve():
            nc.vector.memset(held[:, 0:1], 0.0)

        def hold_pool(n=1):
            nc.gpsimd.tensor_tensor(held[:, n:n + 1], half_neg[:, :], half_neg[:, :], ALU.mult)

        holds = hold_dve, hold_pool
        constants(nc, sem, ident, half_neg)
        with ExitStack() as both:
            w_hi = [sb(f"w_hi{i}", [P, KT, N], F32R, both) for i in range(2)]
            w_lo = [sb(f"w_lo{i}", [P, KT, N], F32R, both) for i in range(2)]
            with ExitStack() as ph:
                qkv_phase(nc, sb, pb, sem, holds, ph, x, w_attn, qkv, ident, half_neg, ln_stats, ln_moments,
                          w_hi, w_lo)
            with ExitStack() as ph:
                attention_phase(nc, sb, pb, sem, holds, ph, x, ctx_kv, qkv, x2, q_w, q_b, k_w, k_b, wqk, wv, wo,
                                bo, g, ident, half_neg, w_hi, w_lo)
        with ExitStack() as ph:
            feed_forward_phase(nc, sb, pb, sem, holds, ph, w13, s13, w2, s2, shifts, x2, out, ident, half_neg,
                               ln_stats, ln_moments)


def constants(nc, sem, ident, half_neg):
    zeroed = sem("ident_zeroed")
    with nc.Block() as block:
        @block.gpsimd
        def _(pool):
            nc.gpsimd.memset(ident[:, :], 0.0).then_inc(zeroed, 1)
            pool.wait_ge(zeroed, 1)
            nc.gpsimd.affine_select(out=ident[:, :], in_=ident[:, :], compare_op=ALU.not_equal, fill=1.0, base=0,
                                    pattern=[[-1, P]], channel_multiplier=1)
            nc.gpsimd.memset(half_neg[:, :], -0.5)


def qkv_phase(nc, sb, pb, sem, holds, ph, x, w_attn, qkv, ident, half_neg, ln_stats, ln_moments, w_hi, w_lo):
    xT_hi = sb("xT_hi", [P, NB, KT, P], F32R, ph)
    xT_lo = sb("xT_lo", [P, NB, KT, P], F32R, ph)
    with ExitStack() as inner:
        rows = sb("qkv_rows", [P, 2, D], F32, inner)
        turn = [pb(f"qkv_turn{p}", [P, KT, P], inner) for p in range(2)]
        ln = LayerNormT(nc, lambda n: sem("x_" + n), holds, x, rows, lambda r, k: r[:, k * P:(k + 1) * P], ident, half_neg,
                        [t[:, :, :] for t in turn], xT_hi, xT_lo, ln_stats, ln_moments)
        with nc.Block() as block:
            @block.sync
            def _(sp):
                sp.sem_inc(ln.transposed, 2)
                ln.load(sp, 0, HALF)

            @block.vector
            def _(dve):
                dve.sem_inc(ln.lo_done, 2)
                ln.vector(dve, 0, HALF)

            @block.gpsimd
            def _(pool):
                ln.gpsimd(pool, 0, HALF)

            @block.tensor
            def _(pe):
                ln.tensor(pe, 0, HALF)

            @block.scalar
            def _(act):
                ln.scalar(act, 0, HALF)

    stage = [sb(f"w_stage{i}", [P, 2, N], F32, ph) for i in range(2)]
    res = [sb(f"qkv_out{i}", [P, N], F32, ph) for i in range(2)]
    BANKS = 4
    acc = pb("qkv_acc", [P, BANKS, N], ph)
    w_in = [sem(f"w_in{i}") for i in range(2)]
    w_hi_done = sem("w_hi_done")
    w_lo_done = sem("w_lo_done")
    mm_done = sem("qkv_mm_done")
    clipped = sem("qkv_clipped")
    stored = [sem(f"qkv_stored{i}") for i in range(2)]
    LOAD_AT = {0: 0, 3: 1, 6: 2, 9: 3}
    LO_AT = {2: 0, 5: 1, 8: 2, 11: 3}

    with nc.Block() as block:
        @block.sync
        def _(sp):
            def load(c, r, wait):
                if wait:
                    sp.wait_ge(w_lo_done, c * PIECES + r - 1)
                sp.dma_start(stage[r % 2][:, :, :], w_attn[c, :, 2 * r:2 * r + 2, :]).then_inc(w_in[r % 2], 16)

            for r in range(PIECES):
                load(0, r, r >= 2)
            with sp.Fori(0, QKV_CHUNKS // 2) as i:
                for h in range(2):
                    c = i * 2 + h
                    for t in range(NB):
                        if t in LOAD_AT:
                            load(c + 1, LOAD_AT[t], True)
                        sp.wait_ge(clipped, c * NB + t + 1 + BANKS)
                        sp.dma_start(qkv[t, :, bass.ds(c * N, N)], res[t % 2][:, :]).then_inc(stored[t % 2], 16)
            for r in range(PIECES):
                load(CHUNKS - 1, r, True)
            for p in range(2):
                sp.wait_ge(stored[p], 16 * (QKV_CHUNKS * NB // 2 + 1))

        @block.scalar
        def _(act):
            def high(c, r, dst):
                act.wait_ge(w_in[r % 2], (c * 2 + r // 2 + 1) * 16)
                nc.scalar.activation(dst[:, 2 * r:2 * r + 2, :], stage[r % 2][:, :, :], ACT.Copy).then_inc(w_hi_done, 1)

            act.sem_inc(stored[0], 16)
            act.sem_inc(stored[1], 16)
            for r in range(PIECES):
                high(0, r, w_hi[0])
            with act.Fori(0, QKV_CHUNKS // 2) as i:
                for h in range(2):
                    c = i * 2 + h
                    act.wait_ge(mm_done, c * NB + 1)
                    for r in range(PIECES):
                        high(c + 1, r, w_hi[1 - h])
            act.wait_ge(mm_done, QKV_CHUNKS * NB)
            for r in range(PIECES):
                high(CHUNKS - 1, r, w_hi[1])

        @block.vector
        def _(dve):
            def low(c, r, hi, lo):
                dve.wait_ge(w_hi_done, c * PIECES + r + 1)
                nc.vector.tensor_tensor(lo[:, 2 * r:2 * r + 2, :], stage[r % 2][:, :, :],
                                        hi[:, 2 * r:2 * r + 2, :].bitcast(F32), ALU.subtract).then_inc(w_lo_done, 1)

            for r in range(PIECES):
                low(0, r, w_hi[0], w_lo[0])
            with dve.Fori(0, QKV_CHUNKS // 2) as i:
                for h in range(2):
                    c = i * 2 + h
                    for t in range(NB):
                        dve.wait_ge(mm_done, c * NB + t + 1)
                        dve.wait_ge(stored[t % 2], (c * (NB // 2) + t // 2 + 1) * 16)
                        nc.vector.tensor_scalar(res[t % 2][:, :], acc[:, t % BANKS, :], CLIP, -CLIP, ALU.min,
                                                ALU.max).then_inc(clipped, 1)
                        if t in LO_AT:
                            low(c + 1, LO_AT[t], w_hi[1 - h], w_lo[1 - h])
            for r in range(PIECES):
                low(CHUNKS - 1, r, w_hi[1], w_lo[1])

        @block.tensor
        def _(pe):
            pe.sem_inc(clipped, BANKS)
            with pe.Fori(0, QKV_CHUNKS // 2) as i:
                for h in range(2):
                    c = i * 2 + h
                    pe.wait_ge(w_lo_done, (c + 1) * PIECES)
                    for t in range(NB):
                        pe.wait_ge(clipped, c * NB + t + 1)
                        product(nc, acc[:, t % BANKS, :],
                                [(a[:, t, k, :], b[:, k, :]) for k in range(KT)
                                 for a, b in ((xT_hi, w_hi[h]), (xT_hi, w_lo[h]), (xT_lo, w_hi[h]))]).then_inc(mm_done, 1)


def product(nc, out, pairs):
    for n, (left, right) in enumerate(pairs):
        last = nc.tensor.matmul(out, left, right, start=n == 0, stop=n == len(pairs) - 1)
    return last


def attention_phase(nc, sb, pb, sem, holds, ph, x, ctx_kv, qkv, x2, q_w, q_b, k_w, k_b, wqk, wv, wo, bo, g,
                    ident, half_neg, w_hi, w_lo):
    hold_dve, hold_pool = holds
    bias = sb("alibi", [P, HEADS, P], F32, ph)
    rel = sb("rel", [P, P], F32, ph)
    ones = sb("ones", [P, P], F32, ph)
    wq_sb = sb("wqk_sb", [P, 2, XO], F32, ph)
    wv_sb = sb("wv_sb", [P, XO], F32, ph)
    wo_sb = sb("wo_sb", [P, XT, P], F32, ph)
    affine = sb("affine", [P, 4, KT], F32, ph)
    bo_sb = sb("bo_sb", [P, 1], F32, ph)
    g_sb = sb("g_sb", [P, 1], F32, ph)
    qk_in = sb("qk_in", [P, 2, D], F32, ph)
    v_in = sb("v_in", [P, D], F32, ph)
    ctx_in = sb("ctx_in", [P, D], F32, ph)
    qk_stats = sb("qk_stats", [P, 2, 12], F32, ph)
    qk_mom = sb("qk_mom", [P, 2, 5], F32, ph)
    qkT = sb("qkT", [P, 2, KT, P], F32, ph)
    kD = sb("kD", [P, G, HG, P], F32, ph)
    SR = 3
    sc = sb("scores", [P, SR, HG, P], F32, ph)
    neg_max = sb("neg_max", [P, G, HG], F32, ph)
    row_sum = sb("row_sum", [P, G, HG], F32, ph)
    row_rec = sb("row_rec", [P, G, HG], F32, ph)
    probT = sb("probT", [P, 2, HG, P], F32, ph)
    oT_hi = sb("oT_hi", [P, KT, P], F32R, ph)
    oT_lo = sb("oT_lo", [P, KT, P], F32R, ph)
    x1 = sb("x1", [P, D], F32, ph)
    xn = sb("xn", [P, D], F32, ph)
    res = sb("res", [P, D], F32, ph)
    x1_stats = sb("x1_stats", [P, 12], F32, ph)
    x1_mom = sb("x1_mom", [P, 5], F32, ph)
    ctxT = qk_in[:, 1, :].rearrange("p (a b) -> p a b", a=KT)
    mT = qk_in[:, 0, 0:XO]
    kE = sb("kE", [P, D], F32, ph)
    kneg = sb("kneg", [P, XT], F32, ph)
    ksum = sb("ksum", [P, XT], F32, ph)
    krec = sb("krec", [P, 2, XT], F32, ph)
    kT = sb("kT", [P, KT, XO], F32, ph)
    cT = sb("cT", [P, XT, P], F32, ph)
    z = sb("z", [P, XT, P], F32, ph)
    qr = sb("qr", [P, SR, XO], F32, ph)
    q_max = sb("q_max", [P, KT, 8], F32, ph)
    q_sum = sb("q_sum", [P, KT, 8], F32, ph)
    q_rec = sb("q_rec", [P, KT, 8], F32, ph)
    qT = sb("qT", [P, XT, D], F32, ph)
    y = v_in
    y_sq = kE
    diag = xn[:, :].rearrange("p (a b) -> p a b", a=KT)
    n_sq = sb("n_sq", [P, 2, KT], F32, ph)
    neg8 = sb("neg8", [P, KT], F32, ph)

    bank_s = pb("bank_s", [P, N], ph)
    bank_q = pb("bank_q", [P, N], ph)
    bank_p = pb("bank_p", [P, HG, P], ph)
    bank_d = pb("bank_d", [P, XT, P], ph)
    pair_o = pb("pair_o", [P, 2 * N], ph)
    pair_k = pb("pair_k", [P, 2 * N], ph)
    turn4 = [bank_s[:, :].rearrange("p (a b) -> p a b", a=4), bank_q[:, :].rearrange("p (a b) -> p a b", a=4),
             bank_p[:, :, :], bank_d[:, :, :]]

    names = ("qk_loaded v_loaded x_loaded ctx_loaded stored setup_in setup_v setup_g "
             "qk_stats qk_aggr qk_mom qk_rstd qk_norm a_done a_out kd_out c_done c_out "
             "s_done s_biased s_max s_exp s_rec s_norm p_done p_out o_done o_hi o_lo "
             "q_done q_maxed q_subbed q_exped q_summed q_recced q_normed d_done d_out "
             "k_done k_maxed k_exped kt_done kt_out k_recced m_done m_out b_done b_out z_done z_out "
             "x_done x1_done x1_stats x1_aggr x1_mom x1_rstd x1_norm copied "
             "y_done y_out y_squared n_done n_clamped n_pow n_diag r_done y_scaled fin").split()
    s = {n: sem("a_" + n) for n in names}

    with nc.Block() as block:
        @block.sync
        def _(sp):
            sp.dma_start(wq_sb[:, :, :], wqk).then_inc(s["setup_in"], 16)
            sp.dma_start(wv_sb[:, :], wv).then_inc(s["setup_in"], 16)
            sp.dma_start(wo_sb[:, :, :], wo.rearrange("(a p) n -> p a n", p=P)).then_inc(s["setup_in"], 16)
            for i, v in enumerate((q_w, q_b, k_w, k_b)):
                sp.dma_start(affine[:, i, :], v).then_inc(s["setup_in"], 16)
            sp.dma_start(bo_sb[:, :], bo.rearrange("(p a) -> p a", a=1)).then_inc(s["setup_in"], 16)
            sp.dma_start(g_sb[:, :], g.rearrange("a p b -> p (a b)")).then_inc(s["setup_in"], 16)
            sp.wait_ge(s["setup_in"], 9 * 16)

        @block.gpsimd
        def _(pool):
            nc.gpsimd.iota(rel[:, :], [[1, P]], 0, channel_multiplier=-1, allow_small_or_imprecise_dtypes=True).then_inc(
                s["setup_g"], 1)
            nc.gpsimd.memset(ones[:, :], 1.0)
            nc.gpsimd.memset(neg8[:, :], -0.5)
            nc.gpsimd.memset(cT[:, :, :], 0.0)
            nc.gpsimd.memset(kD[:, :, :, :], 0.0)
            pool.wait_ge(s["setup_v"], 1)
            nc.gpsimd.affine_select(out=bias[:, :, :], in_=bias[:, :, :], compare_op=ALU.is_ge, fill=MASKED, base=0,
                                    pattern=[[0, HEADS], [-1, P]], channel_multiplier=1)

        @block.vector
        def _(dve):
            dve.wait_ge(s["setup_g"], 1)
            for h in range(HEADS):
                slope = 0.5 ** ((h + 1) * ALIBI_MAX / HEADS)
                ins = nc.vector.tensor_scalar(bias[:, h, :], rel[:, :], slope, None, ALU.mult)
            ins.then_inc(s["setup_v"], 1)
            dve.wait_ge(s["setup_in"], 9 * 16)
            nc.vector.tensor_scalar(g_sb[:, :], g_sb[:, :], float(DIM) ** 0.5, None, ALU.mult)

    STEPS = 12

    def k_tile(t):
        return (t - 1) // 2 if t in (1, 3, 5, 7) else None

    def kt_tile(t):
        return (t - 2) // 2 if t in (2, 4, 6, 8) else None

    def m_tile(t):
        return {3: 0, 5: 1, 8: 2, 9: 3}.get(t)

    m_room = [pair_o[:, D - P:D]] * 2 + [bank_s[:, 0:P]] * 2

    def transpose_qk(pe, b):
        pe.wait_ge(s["qk_norm"], b + 1)
        for n in (2, 3, 0, 1):
            for j in range(4):
                last = nc.tensor.transpose(turn4[n][:, j, :], qk_in[:, n // 2, (n % 2 * 4 + j) * P:(n % 2 * 4 + j + 1) * P],
                                           ident[:, :])
            if n % 2:
                last.then_inc(s["a_done"], 1)

    def norm_qk_affine(act, b):
        for i in (1, 0):
            act.wait_ge(s["a_done"], 2 * b + 2 - i)
            for k in range(KT):
                last = nc.scalar.activation(qkT[:, i, k, :], turn4[2 * i + k // 4][:, k % 4, :], ACT.Identity,
                                            scale=affine[:, 2 * i, k:k + 1], bias=affine[:, 2 * i + 1, k:k + 1])
            last.then_inc(s["a_out"], 1)

    def qk_statistics(dve, b):
        dve.wait_ge(s["qk_loaded"], (b + 1) * 16)
        for i in range(2):
            for e in range(2):
                last = nc.vector.bn_stats(qk_stats[:, i, 6 * e:6 * e + 6], qk_in[:, i, e * N:(e + 1) * N])
        last.then_inc(s["qk_stats"], 1)
        dve.wait_ge(s["qk_stats"], b + 1)
        hold_dve()
        for i in range(2):
            last = nc.vector.bn_aggr(qk_mom[:, i, 0:2], qk_stats[:, i, :])
        last.then_inc(s["qk_aggr"], 1)
        dve.wait_ge(s["qk_aggr"], b + 1)
        nc.vector.tensor_scalar(qk_mom[:, :, 2], qk_mom[:, :, 0], -1.0, None, ALU.mult)
        nc.vector.tensor_scalar(qk_mom[:, :, 3], qk_mom[:, :, 1], EPS, None, ALU.add).then_inc(s["qk_mom"], 1)

    def normalise_qk(pool, b):
        pool.wait_ge(s["qk_mom"], b + 1)
        nc.gpsimd.tensor_tensor(qk_mom[:, :, 4], qk_mom[:, :, 3], neg8[:, 0:2], ALU.pow).then_inc(s["qk_rstd"], 1)
        pool.wait_ge(s["qk_rstd"], b + 1)
        hold_pool()
        for i in range(2):
            last = nc.gpsimd.tensor_scalar(qk_in[:, i, :], qk_in[:, i, :], qk_mom[:, i, 2:3], qk_mom[:, i, 4:5],
                                           ALU.add, ALU.mult)
        last.then_inc(s["qk_norm"], 1)

    def key_blocks(dve, b):
        dve.wait_ge(s["a_out"], 2 * b + 1)
        for j in range(HG):
            at = slice(j * HD, (j + 1) * HD)
            last = nc.vector.tensor_copy(kD[at, :, j, :], qkT[at, 1, :, :])
        last.then_inc(s["kd_out"], 1)

    def bias_scores(dve, b, t):
        dve.wait_ge(s["s_done"], b * G + t + 1)
        nc.vector.scalar_tensor_tensor(flat(sc[:, t % SR, :, :]), bank_s[:, :], float(HD) ** -0.5,
                                       flat(bias[:, t * HG:(t + 1) * HG, :]), ALU.mult, ALU.add).then_inc(
            s["s_biased"], 1)

    def maxima(dve, b, t):
        dve.wait_ge(s["s_biased"], b * G + t + 1)
        nc.vector.tensor_reduce(neg_max[:, t, :], sc[:, t % SR, :, :], AX.X, ALU.max, negate=True).then_inc(
            s["s_max"], 1)

    def turn_sync(sp, b, own, cross, ahead):
        c = b - 1
        if own and cross:
            sp.wait_ge(s["copied"], c + 1)
            sp.dma_start(x1[:, :], x[b, :, :]).then_inc(s["x_loaded"], 16)
        if ahead:
            sp.wait_ge(s["k_done"], (b + 1) * XT)
            sp.dma_start(ctx_in[:, :], ctx_kv[b + 1, :, :]).then_inc(s["ctx_loaded"], 16)
            sp.wait_ge(s["b_done"], b + 1)
            sp.dma_start(qk_in[:, :, :], qkv[b + 1, :, 0:2 * D].rearrange("p (a d) -> p a d", a=2)).then_inc(
                s["qk_loaded"], 16)
            sp.wait_ge(s["o_done"], b + 1)
        if cross:
            sp.wait_ge(s["fin"], c + 1)
        if ahead:
            sp.dma_start(v_in[:, :], qkv[b + 1, :, 2 * D:3 * D]).then_inc(s["v_loaded"], 16)
        if cross:
            sp.dma_start(x2[c, :, :], res[:, :]).then_inc(s["stored"], 16)

    def turn_tensor(pe, b, own, cross, ahead):
        c = b - 1
        for t in range(STEPS):
            if own and t < G:
                if t == 0:
                    pe.wait_ge(s["a_out"], 2 * b + 2)
                    pe.wait_ge(s["kd_out"], b + 1)
                else:
                    pe.wait_ge(s["s_biased"], b * G + t)
                nc.tensor.matmul(bank_s[:, :], qkT[:, 0, t, :], flat(kD[:, t, :, :]), start=True,
                                 stop=True).then_inc(s["s_done"], 1)
            if own and t == 0:
                pe.wait_ge(s["ctx_loaded"], (b + 1) * 16)
                if cross:
                    pe.wait_ge(s["z_out"], b)
                    pe.wait_ge(s["y_scaled"], b)
                for k in range(KT):
                    last = nc.tensor.transpose(pair_k[:, k * P:(k + 1) * P], ctx_in[:, k * P:(k + 1) * P], ident[:, :])
                last.then_inc(s["c_done"], 1)
            n = t - 2
            if own and 0 <= n < G:
                pe.wait_ge(s["s_norm"], b * G + n + 1)
                if n:
                    pe.wait_ge(s["p_out"], b * G + n)
                for j in range(HG):
                    last = nc.tensor.transpose(bank_p[:, j, :], sc[:, n % SR, j, :], ident[:, :])
                last.then_inc(s["p_done"], 1)
            n = t - 2
            if cross and 0 <= n < KT:
                if n % 4 == 0:
                    pe.wait_ge(s["x1_norm"], 2 * c + n // 4 + 1)
                if n:
                    pe.wait_ge(s["q_subbed"], c * KT + n)
                elif not own:
                    pe.wait_ge(s["q_subbed"], c * KT)
                nc.tensor.matmul(bank_q[:, :], xn[:, n * P:(n + 1) * P], wq_sb[:, 0, :], start=True,
                                 stop=True).then_inc(s["q_done"], 1)
            if own and (i := k_tile(t)) is not None:
                if i == 0:
                    pe.wait_ge(s["c_out"], b + 1)
                else:
                    pe.wait_ge(s["kt_out"], b * XT + i)
                for e in range(2):
                    last = nc.tensor.matmul(pair_k[:, e * N:(e + 1) * N], wq_sb[:, 1, i * P:(i + 1) * P],
                                            ctx_in[:, e * N:(e + 1) * N], start=True, stop=True)
                last.then_inc(s["k_done"], 1)
            n = t - 4
            if cross and 0 <= n < KT:
                pe.wait_ge(s["q_normed"], c * KT + n + 1)
                if n:
                    pe.wait_ge(s["d_out"], c * KT + n)
                for j in range(XT):
                    last = nc.tensor.transpose(bank_d[:, j, :], qr[:, n % SR, j * P:(j + 1) * P], ident[:, :])
                last.then_inc(s["d_done"], 1)
            if own and (i := m_tile(t)) is not None:
                if cross and i == 0:
                    pe.wait_ge(s["x1_done"], 2 * b)
                pe.wait_ge(s["kt_out"], b * XT + i + 1)
                if i == 2:
                    pe.wait_ge(s["s_biased"], (b + 1) * G)
                elif i:
                    pe.wait_ge(s["m_out"], b * XT + i)
                for k in range(KT):
                    last = nc.tensor.matmul(m_room[i], ctxT[:, k, :], kT[:, k, i * P:(i + 1) * P], start=k == 0,
                                            stop=k == KT - 1)
                last.then_inc(s["m_done"], 1)
            n = t - 3
            if own and 0 <= n < G:
                if n == 0:
                    pe.wait_ge(s["v_loaded"], (b + 1) * 16)
                if n == G // 2:
                    pe.wait_ge(s["m_out"], b * XT + 2)
                pe.wait_ge(s["p_out"], b * G + n + 1)
                for j in range(HG):
                    h = n * HG + j
                    last = nc.tensor.matmul(pair_o[j * HD:(j + 1) * HD, n * P:(n + 1) * P], v_in[:, h * HD:(h + 1) * HD],
                                            probT[:, n % 2, j, :], start=True, stop=True)
                if n == G - 1:
                    last.then_inc(s["o_done"], 1)
            if own and (i := kt_tile(t)) is not None:
                pe.wait_ge(s["k_exped"], b * XT + i + 1)
                for k in range(KT):
                    last = nc.tensor.transpose(pair_k[:, k * P:(k + 1) * P], kE[:, k * P:(k + 1) * P], ident[:, :])
                last.then_inc(s["kt_done"], 1)
            if own and t == STEPS - 2:
                pe.wait_ge(s["m_out"], (b + 1) * XT)
                for j in range(XT):
                    last = nc.tensor.matmul(pair_k[:, j * P:(j + 1) * P], wv_sb[:, j * P:(j + 1) * P],
                                            mT[:, j * P:(j + 1) * P], start=True, stop=True)
                last.then_inc(s["b_done"], 1)
            if own and t == STEPS - 1:
                pe.wait_ge(s["b_out"], b + 1)
                for j in range(XT):
                    last = nc.tensor.matmul(pair_k[:, N + j * P:N + (j + 1) * P], cT[:, j, :], wo_sb[:, j, :],
                                            start=True, stop=True)
                last.then_inc(s["z_done"], 1)
        if cross:
            pe.wait_ge(s["d_out"], (c + 1) * KT)
            if own:
                pe.wait_ge(s["s_biased"], (b + 1) * G)
            for e, bank in enumerate((bank_s, bank_q)):
                for j in range(XT):
                    last = nc.tensor.matmul(bank[:, :], z[:, j, :], qT[:, j, e * N:(e + 1) * N], start=j == 0,
                                            stop=j == XT - 1)
            last.then_inc(s["y_done"], 1)

        def project(e):
            product(nc, pair_o[:, e * N:(e + 1) * N],
                    [(l[:, k, :], r[:, k, :]) for k in range(KT)
                     for l, r in ((oT_hi, w_hi[e]), (oT_hi, w_lo[e]), (oT_lo, w_hi[e]))]).then_inc(s["x_done"], 1)

        if own:
            pe.wait_ge(s["o_lo"], b + 1)
            project(0)
        if ahead:
            pe.wait_ge(s["p_out"], (b + 1) * G)
            if cross:
                pe.wait_ge(s["y_out"], b)
            else:
                pe.wait_ge(s["s_biased"], (b + 1) * G)
            transpose_qk(pe, b + 1)
        if cross:
            pe.wait_ge(s["y_squared"], c + 1)
            for k in range(KT):
                last = nc.tensor.matmul(pair_k[:, k:k + 1], y_sq[:, k * P:(k + 1) * P], ones[:, 0:1],
                                        start=True, stop=True)
            last.then_inc(s["n_done"], 1)
        if own:
            project(1)
        if cross:
            if own:
                pe.wait_ge(s["z_out"], b + 1)
            pe.wait_ge(s["n_diag"], c + 1)
            for e in range(2):
                last = nc.tensor.matmul(pair_k[:, e * N:(e + 1) * N], ones[:, :], flat(diag[:, 4 * e:4 * e + 4, :]),
                                        start=True, stop=True)
            last.then_inc(s["r_done"], 1)

    def turn_scalar(act, b, own, cross, ahead):
        c = b - 1
        for t in range(STEPS):
            if own and t == 0:
                act.wait_ge(s["c_done"], b + 1)
                nc.scalar.activation(qk_in[:, 1, :], pair_k[:, :], ACT.Copy).then_inc(s["c_out"], 1)
            n = t - 2
            if own and 0 <= n < G:
                act.wait_ge(s["p_done"], b * G + n + 1)
                nc.scalar.activation(probT[:, n % 2, :, :], bank_p[:, :, :], ACT.Copy).then_inc(s["p_out"], 1)
            if own and t < G:
                act.wait_ge(s["s_max"], b * G + t + 1)
                for j in range(HG):
                    last = nc.scalar.activation(sc[:, t % SR, j, :], sc[:, t % SR, j, :], ACT.Exp,
                                                bias=neg_max[:, t, j:j + 1], accum_out=row_sum[:, t, j:j + 1])
                last.then_inc(s["s_exp"], 1)
            n = t - 2
            if cross and 0 <= n < KT:
                act.wait_ge(s["q_subbed"], c * KT + n + 1)
                nc.scalar.activation(qr[:, n % SR, :], qr[:, n % SR, :], ACT.Exp).then_inc(s["q_exped"], 1)
            if own and (i := kt_tile(t)) is not None:
                act.wait_ge(s["kt_done"], b * XT + i + 1)
                nc.scalar.activation(kT[:, :, i * P:(i + 1) * P], pair_k[:, :].rearrange("p (a b) -> p a b", a=KT),
                                     ACT.Copy).then_inc(s["kt_out"], 1)
            n = t - 4
            if cross and 0 <= n < KT:
                act.wait_ge(s["d_done"], c * KT + n + 1)
                nc.scalar.activation(qT[:, :, n * P:(n + 1) * P], bank_d[:, :, :], ACT.Copy).then_inc(s["d_out"], 1)
            if own and (i := k_tile(t)) is not None:
                act.wait_ge(s["k_maxed"], b * XT + i + 1)
                nc.scalar.activation(kE[:, :], pair_k[:, :], ACT.Exp, bias=kneg[:, i:i + 1],
                                     accum_out=ksum[:, i:i + 1]).then_inc(s["k_exped"], 1)
            if own and t == STEPS - 2:
                act.wait_ge(s["o_done"], b + 1)
                nc.scalar.activation(flat(oT_hi[:, :, :]), pair_o[:, :], ACT.Copy).then_inc(s["o_hi"], 1)
        if cross:
            act.wait_ge(s["y_done"], c + 1)
            for e, bank in enumerate((bank_s, bank_q)):
                last = nc.scalar.activation(y[:, e * N:(e + 1) * N], bank[:, :], ACT.Identity, bias=bo_sb[:, 0:1])
            last.then_inc(s["y_out"], 1)
            act.wait_ge(s["y_out"], c + 1)
            nc.scalar.activation(y_sq[:, :], y[:, :], ACT.Square).then_inc(s["y_squared"], 1)
        if ahead:
            norm_qk_affine(act, b + 1)

    def turn_gpsimd(pool, b, own, cross, ahead):
        c = b - 1
        if cross:
            pool.wait_ge(s["r_done"], c + 1)
            pool.wait_ge(s["x1_mom"], c + 1)
            nc.gpsimd.tensor_tensor(x1_mom[:, 4:5], x1_mom[:, 3:4], neg8[:, 0:1], ALU.pow).then_inc(s["x1_rstd"], 1)
            pool.wait_ge(s["x1_rstd"], c + 1)
            hold_pool()
            for e in range(2):
                nc.gpsimd.tensor_scalar(xn[:, e * N:(e + 1) * N], x1[:, e * N:(e + 1) * N], x1_mom[:, 2:3],
                                        x1_mom[:, 4:5], ALU.add, ALU.mult).then_inc(s["x1_norm"], 1)
        for t in range(STEPS):
            n = t - 1
            if own and 0 <= n < G:
                pool.wait_ge(s["s_rec"], b * G + n + 1)
                nc.gpsimd.tensor_tensor(sc[:, n % SR, :, :], sc[:, n % SR, :, :],
                                        row_rec[:, n, :].unsqueeze(2).to_broadcast([P, HG, P]),
                                        ALU.mult).then_inc(s["s_norm"], 1)
            if cross and t == 6:
                pool.wait_ge(s["stored"], (c + 1) * 16)
                hold_pool(2)
                nc.gpsimd.tensor_scalar(res[:, :], x1[:, :], 1.0, 0.0, ALU.mult, ALU.add).then_inc(s["copied"], 1)
            n = t - 3
            if cross and 0 <= n < KT:
                pool.wait_ge(s["q_recced"], c * KT + n + 1)
                q = qr[:, n % SR, :].rearrange("p (h d) -> p h d", d=XD)
                nc.gpsimd.tensor_tensor(q, q, q_rec[:, n, :].unsqueeze(2).to_broadcast([P, 8, XD]),
                                        ALU.mult).then_inc(s["q_normed"], 1)
        if ahead:
            normalise_qk(pool, b + 1)
        if cross:
            pool.wait_ge(s["n_clamped"], c + 1)
            nc.gpsimd.tensor_tensor(n_sq[:, 1, :], n_sq[:, 0, :], neg8[:, :], ALU.pow).then_inc(s["n_pow"], 1)

    def turn_vector(dve, b, own, cross, ahead):
        c = b - 1
        for t in range(STEPS):
            n = t - 3
            if cross and 0 <= n < KT:
                dve.wait_ge(s["q_exped"], c * KT + n + 1)
                nc.vector.tensor_reduce(q_sum[:, n, :], qr[:, n % SR, :].rearrange("p (h d) -> p h d", d=XD), AX.X,
                                        ALU.add).then_inc(s["q_summed"], 1)
            if own and 0 < t < G:
                bias_scores(dve, b, t)
            if cross and 0 <= n < KT:
                dve.wait_ge(s["q_summed"], c * KT + n + 1)
                nc.vector.reciprocal(q_rec[:, n, :], q_sum[:, n, :]).then_inc(s["q_recced"], 1)
            if own and 0 < t < G:
                maxima(dve, b, t)
            n = t - 2
            if cross and 0 <= n < KT:
                dve.wait_ge(s["q_done"], c * KT + n + 1)
                nc.vector.tensor_reduce(q_max[:, n, :], bank_q[:, :].rearrange("p (h d) -> p h d", d=XD), AX.X,
                                        ALU.max).then_inc(s["q_maxed"], 1)
                dve.wait_ge(s["q_maxed"], c * KT + n + 1)
                nc.vector.tensor_tensor(qr[:, n % SR, :].rearrange("p (h d) -> p h d", d=XD),
                                        bank_q[:, :].rearrange("p (h d) -> p h d", d=XD),
                                        q_max[:, n, :].unsqueeze(2).to_broadcast([P, 8, XD]),
                                        ALU.subtract).then_inc(s["q_subbed"], 1)
            if own and (i := k_tile(t)) is not None:
                dve.wait_ge(s["k_done"], b * XT + i + 1)
                nc.vector.tensor_reduce(kneg[:, i:i + 1], pair_k[:, :], AX.X, ALU.max, negate=True).then_inc(
                    s["k_maxed"], 1)
            if own and (i := m_tile(t)) is not None:
                dve.wait_ge(s["m_done"], b * XT + i + 1)
                nc.vector.tensor_copy(mT[:, i * P:(i + 1) * P], m_room[i]).then_inc(s["m_out"], 1)
            if own and t < G:
                dve.wait_ge(s["s_exp"], b * G + t + 1)
                nc.vector.reciprocal(row_rec[:, t, :], row_sum[:, t, :]).then_inc(s["s_rec"], 1)
        if own:
            dve.wait_ge(s["b_done"], b + 1)
            for j in range(2):
                at = slice(j * XD, (j + 1) * XD)
                last = nc.vector.tensor_copy(cT[at, :, at], pair_k[at, 0:N].rearrange("p (a b) -> p a b", a=XT)[:, :, at])
            last.then_inc(s["b_out"], 1)
            dve.wait_ge(s["o_hi"], b + 1)
            nc.vector.tensor_tensor(flat(oT_lo[:, :, :]), pair_o[:, :], flat(oT_hi[:, :, :].bitcast(F32)),
                                    ALU.subtract).then_inc(s["o_lo"], 1)
            dve.wait_ge(s["k_exped"], (b + 1) * XT)
            nc.vector.reciprocal(krec[:, 0, :], ksum[:, :]).then_inc(s["k_recced"], 1)
            dve.wait_ge(s["k_recced"], 2 * b + 1)
            nc.vector.tensor_scalar(krec[:, 1, :], krec[:, 0, :], float(XD) ** -0.5, None, ALU.mult).then_inc(
                s["k_recced"], 1)
            if ahead:
                qk_statistics(dve, b + 1)
            dve.wait_ge(s["k_recced"], 2 * (b + 1))
            dve.wait_ge(s["z_done"], b + 1)
            if cross:
                dve.wait_ge(s["y_done"], c + 1)
            for j in range(XT):
                last = nc.vector.tensor_scalar(z[:, j, :], pair_k[:, N + j * P:N + (j + 1) * P], krec[:, 1, j:j + 1], None,
                                               ALU.mult)
            last.then_inc(s["z_out"], 1)
            dve.wait_ge(s["x_loaded"], (b + 1) * 16)

        def residual(e):
            dve.wait_ge(s["x_done"], 2 * b + e + 1)
            nc.vector.tensor_tensor(x1[:, e * N:(e + 1) * N], pair_o[:, e * N:(e + 1) * N],
                                    x1[:, e * N:(e + 1) * N], ALU.add).then_inc(s["x1_done"], 1)
            dve.wait_ge(s["x1_done"], 2 * b + e + 1)
            return nc.vector.bn_stats(x1_stats[:, 6 * e:6 * e + 6], x1[:, e * N:(e + 1) * N])

        if own:
            residual(0)
        if cross:
            dve.wait_ge(s["n_done"], c + 1)
            nc.vector.tensor_scalar(n_sq[:, 0, :], pair_k[:, 0:KT], 1e-24, None, ALU.max).then_inc(s["n_clamped"], 1)
            dve.wait_ge(s["n_pow"], c + 1)
            nc.vector.tensor_tensor(diag[:, :, :], ident[:, :].unsqueeze(1).to_broadcast([P, KT, P]),
                                    n_sq[:, 1, :].unsqueeze(2).to_broadcast([P, KT, P]), ALU.mult).then_inc(s["n_diag"], 1)
        if ahead:
            key_blocks(dve, b + 1)
        if own:
            residual(1).then_inc(s["x1_stats"], 1)
            dve.wait_ge(s["x1_stats"], b + 1)
            hold_dve()
            nc.vector.bn_aggr(x1_mom[:, 0:2], x1_stats[:, :]).then_inc(s["x1_aggr"], 1)
            dve.wait_ge(s["x1_aggr"], b + 1)
            nc.vector.tensor_scalar(x1_mom[:, 2:3], x1_mom[:, 0:1], -1.0, None, ALU.mult)
            nc.vector.tensor_scalar(x1_mom[:, 3:4], x1_mom[:, 1:2], EPS, None, ALU.add).then_inc(s["x1_mom"], 1)
        if cross:
            dve.wait_ge(s["r_done"], c + 2)
            for e in range(2):
                last = nc.vector.tensor_tensor(y[:, e * N:(e + 1) * N], y[:, e * N:(e + 1) * N],
                                               pair_k[:, e * N:(e + 1) * N], ALU.mult)
            last.then_inc(s["y_scaled"], 1)
        if ahead:
            bias_scores(dve, b + 1, 0)
            maxima(dve, b + 1, 0)
        if cross:
            dve.wait_ge(s["y_scaled"], c + 2)
            dve.wait_ge(s["copied"], c + 1)
            nc.vector.scalar_tensor_tensor(res[:, :], y[:, :], g_sb[:, 0:1], res[:, :], ALU.mult, ALU.add).then_inc(
                s["fin"], 1)

    def turns(eng, turn):
        turn(eng, 0, True, False, True)
        with eng.Fori(1, NB - 1) as b:
            turn(eng, b, True, True, True)
        turn(eng, NB - 1, True, True, False)
        turn(eng, NB, False, True, False)

    with nc.Block() as block:
        @block.sync
        def _(sp):
            sp.dma_start(qk_in[:, :, :], qkv[0, :, 0:2 * D].rearrange("p (a d) -> p a d", a=2)).then_inc(
                s["qk_loaded"], 16)
            sp.dma_start(ctx_in[:, :], ctx_kv[0, :, :]).then_inc(s["ctx_loaded"], 16)
            sp.dma_start(v_in[:, :], qkv[0, :, 2 * D:3 * D]).then_inc(s["v_loaded"], 16)
            sp.dma_start(x1[:, :], x[0, :, :]).then_inc(s["x_loaded"], 16)
            sp.sem_inc(s["stored"], 16)
            turns(sp, turn_sync)
            sp.wait_ge(s["stored"], (NB + 1) * 16)

        @block.gpsimd
        def _(pool):
            normalise_qk(pool, 0)
            turns(pool, turn_gpsimd)

        @block.scalar
        def _(act):
            norm_qk_affine(act, 0)
            turns(act, turn_scalar)

        @block.vector
        def _(dve):
            dve.sem_inc(s["y_scaled"], 1)
            qk_statistics(dve, 0)
            key_blocks(dve, 0)
            bias_scores(dve, 0, 0)
            maxima(dve, 0, 0)
            turns(dve, turn_vector)

        @block.tensor
        def _(pe):
            pe.sem_inc(s["r_done"], 1)
            transpose_qk(pe, 0)
            turns(pe, turn_tensor)


def feed_forward_phase(nc, sb, pb, sem, holds, ph, w13, s13, w2, s2, shifts, x2, out, ident, half_neg, ln_stats, ln_moments):
    GROUPS = NT // 2
    acc = sb("acc", [P, HALF, D], F32, ph)
    xT_hi = sb("h_xT_hi", [P, HALF, KT, P], F32R, ph)
    xT_lo = sb("h_xT_lo", [P, HALF, KT, P], F32R, ph)
    w13_hi = [sb(f"w13_hi{i}", [P, 2, KT, P], F32R, ph) for i in range(2)]
    w13_lo = [sb(f"w13_lo{i}", [P, 2, KT, P], F32R, ph) for i in range(2)]
    w2_hi = [sb(f"w2_hi{i}", [P, 2, N], F32R, ph) for i in range(3)]
    w2_lo = [sb(f"w2_lo{i}", [P, 2, N], F32R, ph) for i in range(3)]
    h_hi = [sb(f"h_hi{i}", [P, HALF * P], F32R, ph) for i in range(3)]
    h_lo = [sb(f"h_lo{i}", [P, HALF * P], F32R, ph) for i in range(3)]
    words = [sb(f"words{i}", [P, D], I32, ph) for i in range(3)]
    sc13 = sb("sc13", [P, 2, P], F32, ph)
    sc2 = sb("sc2", [P, D], F32, ph)
    shift = sb("shift", [P, 6], I32, ph)
    gate = [sb(f"gate{i}", [P, N], F32, ph) for i in range(2)]
    ps = [pb(f"ff_ps{i}", [P, N], ph) for i in range(4)]
    po = pb("ff_po", [P, 4, N], ph)

    names = ("shifts acc_loaded stored w1_in w3_in w2_in s13_in s2_in shifted scaled split_hi split_lo "
             "ab_done gated product h_hi h_lo y_done added").split()
    s = {n: sem("f_" + n) for n in names}
    split = [sem(f"f_split_{n}") for n in ("w1", "w3", "w2")]
    loaded = [s["w1_in"], s["w3_in"], s["w2_in"]]

    def columns(rows, k):
        return rows.rearrange("p (q k) -> p k q", k=KT)[:, k, :]

    turn = [po[:, 2 * p:2 * p + 2, :].rearrange("p a (b c) -> p (a b) c", c=P) for p in range(2)]
    rows = sb("h_rows", [P, 2, D], F32, ph)
    ln = LayerNormT(nc, lambda n: sem("h_" + n), holds, x2, rows, columns, ident, half_neg, turn, xT_hi, xT_lo,
                    ln_stats, ln_moments)
    OUTS = 2 * HALF
    FULL_GROUPS = GROUPS - 1

    def groups(eng, group):
        group(0, 0, True)
        with eng.Fori(0, FULL_GROUPS // 2) as i:
            group(i * 2 + 1, 1, False)
            group(i * 2 + 2, 0, False)

    with nc.Block() as block:
        @block.sync
        def _(sp):
            def load13(tile, count):
                for mat in range(2):
                    if count is not None:
                        sp.wait_ge(split[mat], count)
                    sp.dma_start(words[mat][:, :], w13[tile, mat, :, :]).then_inc(loaded[mat], 16)
                    if mat == 0:
                        if count is not None:
                            sp.wait_ge(s["scaled"], count * 3 - 1)
                        sp.dma_start(sc13[:, :, :], s13[tile, :, :, :]).then_inc(s["s13_in"], 16)

            def load2(tile, u):
                sp.wait_ge(split[2], u + 1)
                for a in range(2):
                    at = slice(a * 64, a * 64 + 64)
                    sp.dma_start(words[2][at, 0:N], w2[tile, :, :]).then_inc(s["w2_in"], 16)
                    sp.dma_start(words[2][at, N:D], w2[tile + FF // P + a, :, :]).then_inc(s["w2_in"], 16)
                    sp.dma_start(sc2[at, :], s2[bass.ds(tile * 2 + a, 1), :].to_broadcast([64, D])).then_inc(
                        s["w2_in"], 16)

            sp.sem_inc(ln.transposed, 2)
            sp.sem_inc(split[2], 1)
            sp.sem_inc(s["stored"], 16)
            sp.dma_start(shift[:, :], shifts).then_inc(s["shifts"], 16)
            load13(0, None)
            with sp.Fori(0, 2) as hf:
                sp.wait_ge(s["stored"], hf * (HALF * 16) + 16)
                for t in range(HALF):
                    sp.dma_start(acc[:, t, :], x2[hf * HALF + t, :, :]).then_inc(s["acc_loaded"], 16)
                ln.load(sp, hf * (HALF // 2), HALF // 2)

                def group(j, parity, first):
                    for e in range(2):
                        tile = j * 2 + e
                        u = hf * NT + tile
                        load13(tile + 1, u + 1)
                        load2(tile, u)

                groups(sp, group)
                for t in range(HALF):
                    sp.wait_ge(s["added"], (hf * GROUPS + GROUPS - 1) * OUTS + 2 * t + 2 + 4)
                    sp.dma_start(out[hf * HALF + t, :, :], acc[:, t, :]).then_inc(s["stored"], 16)
            sp.wait_ge(s["stored"], 16 + NB * 16)

        @block.gpsimd
        def _(pool):
            with pool.Fori(0, 2) as hf:
                ln.gpsimd(pool, hf * (HALF // 2), HALF // 2)

        @block.scalar
        def _(act):
            def high(mat, dst, count):
                act.wait_ge(s["scaled"], count)
                src = words[mat][:, :].bitcast(F32)
                nc.scalar.activation(dst, src, ACT.Copy).then_inc(s["split_hi"], 1)

            def tile(u, e, slot, first):
                act.wait_ge(s["ab_done"], u * 4 + 1)
                for mat in range(2):
                    high(mat, flat(w13_hi[1 - e][:, mat, :, :]), u * 3 + 3 + mat)
                if e == 1 and not first:
                    act.wait_ge(s["y_done"], (u - 1) * (OUTS // 2))
                high(2, flat(w2_hi[slot][:, :, :]), u * 3 + 5)
                for sl in range(SL):
                    act.wait_ge(s["h_lo"], u * 2 + sl + 1)
                    act.wait_ge(s["ab_done"], u * 4 + 2 * sl + 2)
                    nc.scalar.activation(gate[sl][:, :], ps[2 * sl][:, :], ACT.Silu).then_inc(s["gated"], 1)
                    act.wait_ge(s["product"], u * 2 + sl + 3)
                    nc.scalar.activation(h_hi[slot][:, sl * N:(sl + 1) * N], gate[sl][:, :], ACT.Copy).then_inc(
                        s["h_hi"], 1)

            for mat in range(2):
                high(mat, flat(w13_hi[0][:, mat, :, :]), mat + 1)
            with act.Fori(0, 2) as hf:
                ln.scalar(act, hf * (HALF // 2), HALF // 2)

                def group(j, parity, first):
                    for e in range(2):
                        tile(hf * NT + j * 2 + e, e, 2 if e else parity, first)

                groups(act, group)

        @block.vector
        def _(dve):
            def unpack(mat, count):
                w = words[mat]
                for kind, at in ((0, slice(0, D)),) if mat < 2 else ((1, slice(0, N)), (2, slice(N, D))):
                    last = nc.vector.tensor_scalar(w[:, at], w[:, at], shift[:, 2 * kind:2 * kind + 1],
                                                   shift[:, 2 * kind + 1:2 * kind + 2], ALU.logical_shift_left,
                                                   ALU.arith_shift_right)
                last.then_inc(s["shifted"], 1)
                if mat < 2:
                    dst, src = [v.rearrange("p (k n) -> p k n", k=KT) for v in (w[:, :].bitcast(F32), w[:, :])]
                    scale = sc13[:, mat, :].unsqueeze(1).to_broadcast([P, KT, P])
                else:
                    dst, src, scale = w[:, :].bitcast(F32), w[:, :], sc2[:, :]
                dve.wait_ge(s["shifted"], count + 1)
                nc.vector.tensor_tensor(dst, src, scale, ALU.mult).then_inc(s["scaled"], 1)

            def low(mat, dst, hi, count):
                dve.wait_ge(s["split_hi"], count + 1)
                nc.vector.tensor_tensor(dst, words[mat][:, :].bitcast(F32), hi.bitcast(F32), ALU.subtract).then_inc(
                    split[mat], 1)

            def low13(e, mat, count):
                low(mat, flat(w13_lo[e][:, mat, :, :]), flat(w13_hi[e][:, mat, :, :]), count)

            def tile(u, e, slot):
                for mat in range(2):
                    dve.wait_ge(loaded[mat], (u + 2) * 16)
                    if mat == 0:
                        dve.wait_ge(s["s13_in"], (u + 2) * 16)
                    unpack(mat, u * 3 + 2 + mat)
                low13(1 - e, 0, u * 3 + 2)
                dve.wait_ge(s["w2_in"], (u + 1) * 96)
                unpack(2, u * 3 + 4)
                low13(1 - e, 1, u * 3 + 3)
                low(2, flat(w2_lo[slot][:, :, :]), flat(w2_hi[slot][:, :, :]), u * 3 + 4)
                for sl in range(SL):
                    dve.wait_ge(s["gated"], u * 2 + sl + 1)
                    dve.wait_ge(s["ab_done"], u * 4 + 2 * sl + 3)
                    nc.vector.tensor_tensor(gate[sl][:, :], gate[sl][:, :], ps[2 * sl + 1][:, :], ALU.mult).then_inc(
                        s["product"], 1)
                    dve.wait_ge(s["h_hi"], u * 2 + sl + 1)
                    at = slice(sl * N, (sl + 1) * N)
                    nc.vector.tensor_tensor(h_lo[slot][:, at], gate[sl][:, :], h_hi[slot][:, at].bitcast(F32),
                                            ALU.subtract).then_inc(s["h_lo"], 1)

            def add(gj):
                for o in range(OUTS):
                    t, par = o // 2, o % 2
                    dve.wait_ge(s["y_done"], gj * OUTS + o + 1)
                    cols = acc[:, t, :].rearrange("p (n two) -> p two n", two=2)[:, par, :]
                    nc.vector.tensor_tensor(cols, po[:, o % 4, :], cols, ALU.add).then_inc(s["added"], 1)

            dve.sem_inc(ln.lo_done, 2)
            dve.sem_inc(s["h_lo"], 2)
            dve.wait_ge(s["shifts"], 16)
            for mat in range(2):
                dve.wait_ge(loaded[mat], 16)
                if mat == 0:
                    dve.wait_ge(s["s13_in"], 16)
                unpack(mat, mat)
                low13(0, mat, mat)
            with dve.Fori(0, 2) as hf:
                ln.vector(dve, hf * (HALF // 2), HALF // 2)
                dve.wait_ge(s["acc_loaded"], (hf + 1) * (HALF * 16))

                def group(j, parity, first):
                    tile(hf * NT + j * 2, 0, parity)
                    if not first:
                        add(hf * GROUPS + j - 1)
                    tile(hf * NT + j * 2 + 1, 1, 2)

                groups(dve, group)
                add(hf * GROUPS + GROUPS - 1)

        @block.tensor
        def _(pe):
            def ab(u, e, hf=None):
                for mat in range(2):
                    pe.wait_ge(split[mat], u + 1)
                for sl in range(SL):
                    if hf is not None:
                        pe.wait_ge(ln.lo_done, hf * HALF + sl * 4 + 6)
                    pe.wait_ge(s["product"], u * 2 + sl + 1)
                    for mat in range(2):
                        at = slice(sl * 4, sl * 4 + 4)
                        product(nc, ps[2 * sl + mat][:, :].rearrange("p (a b) -> p a b", a=4),
                                [(l[:, mat, k, :], r[:, at, k, :]) for k in range(KT)
                                 for l, r in ((w13_hi[e], xT_hi), (w13_hi[e], xT_lo), (w13_lo[e], xT_hi))]).then_inc(
                            s["ab_done"], 1)

            def outputs(gj, slots):
                pe.wait_ge(s["h_lo"], (gj + 1) * 4 + 2)
                pe.wait_ge(split[2], (gj + 1) * 2 + 1)
                for o in range(OUTS):
                    t, par = o // 2, o % 2
                    at = slice(t * P, (t + 1) * P)
                    pe.wait_ge(s["added"], gj * OUTS + o + 1)
                    product(nc, po[:, o % 4, :],
                            [(l[i][:, at], r[i][:, par, :]) for i in slots
                             for l, r in ((h_hi, w2_hi), (h_hi, w2_lo), (h_lo, w2_hi))]).then_inc(s["y_done"], 1)

            pe.sem_inc(s["added"], 4)
            pe.sem_inc(s["product"], 2)
            pe.sem_inc(s["ab_done"], 1)
            with pe.Fori(0, 2) as hf:
                ln.tensor(pe, hf * (HALF // 2), HALF // 2, lambda: pe.wait_ge(s["added"], hf * (GROUPS * OUTS) + 4))

                def group(j, parity, first):
                    ab(hf * NT + j * 2, 0, hf if first else None)
                    if not first:
                        outputs(hf * GROUPS + j - 1, (1 - parity, 2))
                    ab(hf * NT + j * 2 + 1, 1)

                groups(pe, group)
                outputs(hf * GROUPS + GROUPS - 1, (0, 2))


def lay_out_ffn(w1, s1, w2, s2, w3, s3):
    import numpy as np

    pad = NT * P - FF

    def words(w):
        w = np.asarray(w).reshape(FF, 8, 1, 8, 8).repeat(2, axis=2)
        w = np.concatenate([w, np.zeros((pad,) + w.shape[1:], w.dtype)])
        return w.reshape(NT, P, P, 8).transpose(0, 2, 3, 1)

    def scales(s):
        s = np.asarray(s).reshape(FF, 16).repeat(8, axis=1)
        s = np.concatenate([s, np.zeros((pad, P), s.dtype)])
        return s.reshape(NT, P, P).transpose(0, 2, 1)

    w13 = np.stack([words(w1), words(w3)], 1).reshape(NT, 2, P, 8 * P)
    s13 = np.stack([scales(s1), scales(s3)], 2)
    w13, s13 = [np.concatenate([v, v[:1]]) for v in (w13, s13)]
    rows = FF // GROUP
    w2 = np.asarray(w2).reshape(D // 2, rows, GROUP).transpose(1, 2, 0)
    w2 = np.concatenate([w2, np.zeros((1, GROUP, D // 2), w2.dtype)])
    s2 = np.asarray(s2).reshape(D // 2, 2, rows).transpose(2, 1, 0).reshape(rows, D)
    s2 = np.concatenate([s2, np.zeros((1, D), s2.dtype)])
    high, low = (0, 4), (28, 28)
    shifts = np.array([(high, low)[p // 8 % 2] + (high, low)[p // 64] + (low, high)[p // 64] for p in range(P)],
                      np.int32)
    return [np.ascontiguousarray(v) for v in (w13, s13, w2, s2, shifts)]


def kernel(**inputs):
    import numpy as np
    import concourse.bacc as bacc
    from concourse.bass_utils import run_bass_kernel_spmd

    a = {name: np.asarray(value) for name, value in inputs.items()}

    w_attn = np.concatenate([a["L0_attn_Wqkv"], a["L0_attn_Wout"]])
    vectors = [a["L0_attn_" + n].reshape(KT, P).T for n in ("q_ln_w", "q_ln_b", "k_ln_w", "k_ln_b")]
    w13, s13, w2, s2, shifts = lay_out_ffn(*[a["L0_ffn_" + n] for n in ("w1", "s1", "w2", "s2", "w3", "s3")])
    laid_out = dict(
        x=a["x"],
        context=a["ctx_4096"],
        w_attn=w_attn.reshape(CHUNKS, N, KT, P).transpose(0, 3, 2, 1),
        q_w=vectors[0], q_b=vectors[1], k_w=vectors[2], k_b=vectors[3],
        wqk=np.stack([a["L0_xattn_Wq"].T, a["L0_xattn_Wk"].T], 1),
        wv=a["L0_xattn_Wv"].T,
        wo=a["L0_xattn_Wo"].T,
        bo=a["L0_xattn_bo"],
        g=a["L0_xattn_g"],
        w13=w13, s13=s13, w2=w2, s2=s2, shifts=shifts)

    nc = bacc.Bacc("TRN2", target_bir_lowering=False, num_devices=1)
    arrays, args = {}, []
    for name, value in laid_out.items():
        value = np.ascontiguousarray(value)
        arrays[f"in_{name}"] = value
        args.append(nc.dram_tensor(f"in_{name}", value.shape, mybir.dt.from_np(value.dtype),
                                   kind="ExternalInput").ap())
    out = nc.dram_tensor("out_0", (NB, P, D), F32, kind="ExternalOutput").ap()
    qkv = nc.dram_tensor("qkv", (NB, P, 3 * D), F32).ap()
    x2 = nc.dram_tensor("x2", (NB, P, D), F32).ap()
    program(nc, *args, out, qkv, x2)
    r = run_bass_kernel_spmd(nc, [arrays], core_ids=[0])
    return r.results[0]["out_0"]
```

```python
import concourse.bass as bass
from concourse import mybir
from contextlib import ExitStack

F32 = mybir.dt.float32
F32R = mybir.dt.float32r
I32 = mybir.dt.int32
ALU = mybir.AluOpType
ACT = mybir.ActivationFunctionType
AX = mybir.AxisListType

P = 128
NB = 16
D = 1024
KT = D // P
N = 512
HEADS, HD = 32, 32
HG = P // HD
G = HEADS // HG
CLIP = 8.0
EPS = 1e-5
ALIBI_MAX = 8.0
MASKED = -1e30
XO = 512
XD = 64
XT = XO // P
FF = 2752
GROUP = 64
NT = -(-FF // P)
CHUNKS = 4 * D // N
QKV_CHUNKS = 3 * D // N
HALF = NB // 2
SL = HALF * P // N
DIM = P


def flat(ap):
    return ap.rearrange("p a b -> p (a b)")


class LayerNormT:

    def __init__(self, nc, sem, rows, columns, ident, half_neg, hi, lo, stats, moments):
        self.nc, self.rows, self.columns = nc, rows, columns
        self.ident, self.half_neg, self.hi, self.lo = ident, half_neg, hi, lo
        self.stats, self.moments = stats, moments
        self.stats_done = sem("ln_stats_done")
        self.aggregated = sem("ln_aggregated")
        self.moments_done = sem("ln_moments_done")
        self.rstd_done = sem("ln_rstd_done")
        self.normalised = sem("ln_normalised")
        self.transposed = sem("ln_transposed")
        self.hi_done = sem("ln_hi_done")
        self.lo_done = sem("ln_lo_done")


    def statistics(self, dve, n, p, rows):
        nc = self.nc
        nc.vector.bn_stats(self.stats[:, p, 0:6], rows[:, 0:N])
        nc.vector.bn_stats(self.stats[:, p, 6:12], rows[:, N:D]).then_inc(self.stats_done, 1)
        dve.wait_ge(self.stats_done, n + 1)
        nc.vector.bn_aggr(self.moments[:, p, 0:2], self.stats[:, p, :]).then_inc(self.aggregated, 1)
        dve.wait_ge(self.aggregated, n + 1)
        nc.vector.tensor_scalar(self.moments[:, p, 2:3], self.moments[:, p, 0:1], -1.0, None, ALU.mult)
        nc.vector.tensor_scalar(self.moments[:, p, 3:4], self.moments[:, p, 1:2], EPS, None, ALU.add).then_inc(
            self.moments_done, 1)

    def normalise(self, pool, n, p, rows):
        nc = self.nc
        pool.wait_ge(self.moments_done, n + 1)
        nc.gpsimd.tensor_tensor(self.moments[:, p, 4:5], self.moments[:, p, 3:4], self.half_neg[:, :],
                                ALU.pow).then_inc(self.rstd_done, 1)
        pool.wait_ge(self.rstd_done, n + 1)
        nc.gpsimd.tensor_scalar(self.rows[:, p, :], rows, self.moments[:, p, 2:3],
                                self.moments[:, p, 4:5], ALU.add, ALU.mult).then_inc(self.normalised, 1)

    def transpose(self, pe, n, p, bank):
        pe.wait_ge(self.normalised, n + 1)
        pe.wait_ge(self.lo_done, n + 1)
        for k in range(KT):
            last = self.nc.tensor.transpose(bank[:, k, :], self.columns(self.rows[:, p, :], k),
                                            self.ident[:, :])
        last.then_inc(self.transposed, 1)

    def high(self, act, n, at, bank):
        act.wait_ge(self.transposed, n + 3)
        self.nc.scalar.activation(self.hi[:, at, :, :], bank, ACT.Copy).then_inc(self.hi_done, 1)

    def low(self, dve, n, at, bank):
        dve.wait_ge(self.hi_done, n + 1)
        self.nc.vector.tensor_tensor(self.lo[:, at, :, :], bank,
                                     self.hi[:, at, :, :].bitcast(F32), ALU.subtract).then_inc(self.lo_done, 1)


def program(nc, x, ctx_kv, w_attn, q_w, q_b, k_w, k_b, wqk, wv, wo, bo, g, w13, s13, w2, s2, shifts, out, qkv, x2):
    top = ExitStack()
    with top:
        def sb(name, shape, dt=F32, where=top):
            return where.enter_context(nc.sbuf_tensor(name, shape, dt))

        def pb(name, shape, where=top):
            return where.enter_context(nc.psum_tensor(name, shape, F32))

        def sem(name):
            return top.enter_context(nc.semaphore(name))

        ident = sb("ident", [P, P])
        half_neg = sb("half_neg", [P, 1])
        ln_stats = sb("ln_stats", [P, 2, 12])
        ln_moments = sb("ln_moments", [P, 2, 5])
        held = sb("held", [P, 3])

        def hold_dve():
            nc.vector.memset(held[:, 0:1], 0.0)

        def hold_pool(n=1):
            nc.gpsimd.tensor_tensor(held[:, n:n + 1], half_neg[:, :], half_neg[:, :], ALU.mult)

        holds = hold_dve, hold_pool
        constants(nc, sem, ident, half_neg)
        with ExitStack() as both:
            w_hi = [sb(f"w_hi{i}", [P, KT, N], F32R, both) for i in range(2)]
            w_lo = [sb(f"w_lo{i}", [P, KT, N], F32R, both) for i in range(2)]
            with ExitStack() as ph:
                qkv_phase(nc, sb, pb, sem, ph, x, w_attn, qkv, ident, half_neg, ln_stats, ln_moments,
                          w_hi, w_lo)
            with ExitStack() as ph:
                attention_phase(nc, sb, pb, sem, holds, ph, x, ctx_kv, w_attn, qkv, x2, q_w, q_b, k_w, k_b, wqk, wv, wo,
                                bo, g, ident, half_neg, w_hi, w_lo)
        with ExitStack() as ph:
            feed_forward_phase(nc, sb, pb, sem, ph, w13, s13, w2, s2, shifts, x2, out, ident, half_neg,
                               ln_stats, ln_moments)


def constants(nc, sem, ident, half_neg):
    zeroed = sem("ident_zeroed")
    with nc.Block() as block:
        @block.gpsimd
        def _(pool):
            nc.gpsimd.memset(ident[:, :], 0.0).then_inc(zeroed, 1)
            pool.wait_ge(zeroed, 1)
            nc.gpsimd.affine_select(out=ident[:, :], in_=ident[:, :], compare_op=ALU.not_equal, fill=1.0, base=0,
                                    pattern=[[-1, P]], channel_multiplier=1)
            nc.gpsimd.memset(half_neg[:, :], -0.5)


def qkv_phase(nc, sb, pb, sem, ph, x, w_attn, qkv, ident, half_neg, ln_stats, ln_moments, w_hi, w_lo):
    PIECES = KT
    BANKS = 4
    xT_hi = sb("xT_hi", [P, NB, KT, P], F32R, ph)
    xT_lo = sb("xT_lo", [P, NB, KT, P], F32R, ph)
    rows = sb("qkv_rows", [P, 2, D], F32, ph)
    stage = sb("w_stage", [P, 2, N], F32, ph)
    res = sb("qkv_out", [P, N], F32, ph)
    turn = [pb(f"qkv_turn{p}", [P, KT, P], ph) for p in range(2)]
    acc = pb("qkv_acc", [P, BANKS, N], ph)
    turn = [t[:, :, :] for t in turn]
    ln = LayerNormT(nc, lambda n: sem("x_" + n), rows, lambda r, k: r[:, k * P:(k + 1) * P], ident, half_neg,
                    xT_hi, xT_lo, ln_stats, ln_moments)
    x_in = [sem(f"x_in{p}") for p in range(2)]
    w_in = [sem(f"w_in{i}") for i in range(2)]
    w_hi_done = sem("w_hi_done")
    w_lo_done = sem("w_lo_done")
    mm_done = sem("qkv_mm_done")
    clipped = sem("qkv_clipped")
    stored = sem("qkv_stored")

    def chunks(eng, chunk):
        chunk(0, 0, True)
        with eng.Fori(0, QKV_CHUNKS // 2 - 1) as i:
            chunk(i * 2 + 1, 1, False)
            chunk(i * 2 + 2, 0, False)
        chunk(QKV_CHUNKS - 1, 1, False)

    with nc.Block() as block:
        @block.sync
        def _(sp):
            def load(c, r, wait=True):
                if wait:
                    sp.wait_ge(w_lo_done, c * PIECES + r - 1)
                sp.dma_start(stage[:, r % 2, :], w_attn[c, :, r, :]).then_inc(w_in[r % 2], 16)

            def load_rows(t):
                sp.wait_ge(ln.transposed, t + 1)
                sp.dma_start(rows[:, t % 2, :], x[t, :, :]).then_inc(x_in[t % 2], 16)

            sp.sem_inc(ln.transposed, 2)
            for t in range(2):
                load_rows(t)
            for r in range(PIECES):
                load(0, r, r >= 2)
            load_rows(2)

            def chunk(c, parity, first):
                for t in range(NB):
                    if first and t + 3 < NB:
                        load_rows(t + 3)
                    if t % 2 == 0:
                        load(c + 1, t // 2)
                    sp.wait_ge(clipped, c * NB + t + 1 + BANKS)
                    sp.dma_start(qkv[t, :, bass.ds(c * N, N)], res[:, :]).then_inc(stored, 16)

            chunks(sp, chunk)
            sp.wait_ge(stored, 16 * (QKV_CHUNKS * NB + 1))

        @block.gpsimd
        def _(pool):
            for t in range(NB):
                ln.normalise(pool, t, t % 2, rows[:, t % 2, :])

        @block.scalar
        def _(act):
            def high(c, r, dst):
                act.wait_ge(w_in[r % 2], (c * (PIECES // 2) + r // 2 + 1) * 16)
                nc.scalar.activation(dst[:, r, :], stage[:, r % 2, :], ACT.Copy).then_inc(w_hi_done, 1)

            act.sem_inc(stored, 16)
            for r in range(PIECES // 2):
                high(0, r, w_hi[0])
            ln.high(act, 0, 0, turn[0])
            for r in range(PIECES // 2, PIECES):
                high(0, r, w_hi[0])

            def chunk(c, parity, first):
                if not first:
                    act.wait_ge(mm_done, c * NB)
                for t in range(NB):
                    if first and t + 1 < NB:
                        ln.high(act, t + 1, t + 1, turn[(t + 1) % 2])
                    if t % 2 == 0:
                        high(c + 1, t // 2, w_hi[1 - parity])

            chunks(act, chunk)

        @block.vector
        def _(dve):
            def low(c, r, hi, lo):
                dve.wait_ge(w_hi_done, c * PIECES + r + 1)
                nc.vector.tensor_tensor(lo[:, r, :], stage[:, r % 2, :], hi[:, r, :].bitcast(F32),
                                        ALU.subtract).then_inc(w_lo_done, 1)

            def statistics(t):
                dve.wait_ge(x_in[t % 2], (t // 2 + 1) * 16)
                ln.statistics(dve, t, t % 2, rows[:, t % 2, :])

            dve.sem_inc(ln.lo_done, 2)
            statistics(0)
            low(0, 0, w_hi[0], w_lo[0])
            statistics(1)
            for r in range(1, PIECES // 2):
                low(0, r, w_hi[0], w_lo[0])
            ln.low(dve, 0, 0, turn[0])
            for r in range(PIECES // 2, PIECES):
                low(0, r, w_hi[0], w_lo[0])

            def chunk(c, parity, first):
                for t in range(NB):
                    if first and t + 2 < NB:
                        statistics(t + 2)
                    if first and t + 1 < NB:
                        ln.low(dve, t + 1, t + 1, turn[(t + 1) % 2])
                    if t % 2 == 1:
                        low(c + 1, t // 2, w_hi[1 - parity], w_lo[1 - parity])
                    dve.wait_ge(mm_done, c * NB + t + 1)
                    dve.wait_ge(stored, (c * NB + t + 1) * 16)
                    nc.vector.tensor_scalar(res[:, :], acc[:, t % BANKS, :], CLIP, -CLIP, ALU.min,
                                            ALU.max).then_inc(clipped, 1)

            chunks(dve, chunk)

        @block.tensor
        def _(pe):
            pe.sem_inc(clipped, BANKS)
            ln.transpose(pe, 0, 0, turn[0])

            def chunk(c, parity, first):
                for t in range(NB):
                    if first and t + 1 < NB:
                        ln.transpose(pe, t + 1, (t + 1) % 2, turn[(t + 1) % 2])
                    if t == 0:
                        pe.wait_ge(w_lo_done, (c + 1) * PIECES)
                    if first:
                        pe.wait_ge(ln.lo_done, t + 3)
                    pe.wait_ge(clipped, c * NB + t + 1)
                    product(nc, acc[:, t % BANKS, :],
                            [(a[:, t, k, :], b[:, k, :]) for k in range(KT)
                             for a, b in ((xT_hi, w_hi[parity]), (xT_hi, w_lo[parity]),
                                          (xT_lo, w_hi[parity]))]).then_inc(mm_done, 1)

            chunks(pe, chunk)


def product(nc, out, pairs):
    for n, (left, right) in enumerate(pairs):
        last = nc.tensor.matmul(out, left, right, start=n == 0, stop=n == len(pairs) - 1)
    return last


def attention_phase(nc, sb, pb, sem, holds, ph, x, ctx_kv, w_attn, qkv, x2, q_w, q_b, k_w, k_b, wqk, wv, wo, bo, g,
                    ident, half_neg, w_hi, w_lo):
    hold_dve, hold_pool = holds
    bias = sb("alibi", [P, HEADS, P], F32, ph)
    rel = sb("rel", [P, P], F32, ph)
    ones = sb("ones", [P, P], F32, ph)
    wq_sb = sb("wqk_sb", [P, 2, XO], F32, ph)
    wv_sb = sb("wv_sb", [P, XO], F32, ph)
    wo_sb = sb("wo_sb", [P, XT, P], F32, ph)
    affine = sb("affine", [P, 4, KT], F32, ph)
    bo_sb = sb("bo_sb", [P, 1], F32, ph)
    g_sb = sb("g_sb", [P, 1], F32, ph)
    qk_in = sb("qk_in", [P, 2, D], F32, ph)
    v_in = sb("v_in", [P, D], F32, ph)
    ctx_in = sb("ctx_in", [P, D], F32, ph)
    qk_stats = sb("qk_stats", [P, 2, 12], F32, ph)
    qk_mom = sb("qk_mom", [P, 2, 5], F32, ph)
    qkT = sb("qkT", [P, 2, KT, P], F32, ph)
    kD = sb("kD", [P, G, HG, P], F32, ph)
    SR = 3
    sc = sb("scores", [P, SR, HG, P], F32, ph)
    neg_max = sb("neg_max", [P, G, HG], F32, ph)
    row_sum = sb("row_sum", [P, G, HG], F32, ph)
    row_rec = sb("row_rec", [P, G, HG], F32, ph)
    probT = sb("probT", [P, 2, HG, P], F32, ph)
    oT_hi = sb("oT_hi", [P, KT, P], F32R, ph)
    oT_lo = sb("oT_lo", [P, KT, P], F32R, ph)
    x1 = sb("x1", [P, D], F32, ph)
    xn = sb("xn", [P, D], F32, ph)
    res = sb("res", [P, D], F32, ph)
    x1_stats = sb("x1_stats", [P, 12], F32, ph)
    x1_mom = sb("x1_mom", [P, 5], F32, ph)
    ctxT = qk_in[:, 1, :].rearrange("p (a b) -> p a b", a=KT)
    mT = qk_in[:, 0, 0:XO]
    kE = sb("kE", [P, D], F32, ph)
    kneg = sb("kneg", [P, XT], F32, ph)
    ksum = sb("ksum", [P, XT], F32, ph)
    krec = sb("krec", [P, 2, XT], F32, ph)
    kT = sb("kT", [P, KT, XO], F32, ph)
    cT = sb("cT", [P, XT, P], F32, ph)
    z = sb("z", [P, XT, P], F32, ph)
    qr = sb("qr", [P, SR, XO], F32, ph)
    q_max = sb("q_max", [P, KT, 8], F32, ph)
    q_sum = sb("q_sum", [P, KT, 8], F32, ph)
    q_rec = sb("q_rec", [P, KT, 8], F32, ph)
    qT = sb("qT", [P, XT, D], F32, ph)
    y = v_in
    y_sq = kE
    diag = xn[:, :].rearrange("p (a b) -> p a b", a=KT)
    n_sq = sb("n_sq", [P, 2, KT], F32, ph)
    neg8 = sb("neg8", [P, KT], F32, ph)

    bank_s = pb("bank_s", [P, N], ph)
    bank_q = pb("bank_q", [P, N], ph)
    bank_p = pb("bank_p", [P, HG, P], ph)
    bank_d = pb("bank_d", [P, XT, P], ph)
    pair_o = pb("pair_o", [P, 2 * N], ph)
    pair_k = pb("pair_k", [P, 2 * N], ph)
    norm_banks = [bank_q[:, :], flat(bank_d[:, :, :])]
    turn4 = [bank_s[:, :].rearrange("p (a b) -> p a b", a=4), bank_q[:, :].rearrange("p (a b) -> p a b", a=4),
             bank_p[:, :, :], bank_d[:, :, :]]

    names = ("qk_loaded v_loaded x_loaded ctx_loaded stored setup_in distances powers filled slopes masked gain "
             "w_in0 w_in1 w_in2 w_in3 w_hi_done w_lo_done "
             "qk_stats qk_aggr qk_mom qk_rstd qk_norm a_done a_out kd_out c_done c_out "
             "s_done s_biased s_max s_exp s_rec s_norm p_done p_out o_done o_hi o_lo "
             "q_done q_maxed q_subbed q_exped q_summed q_recced q_normed d_done d_out "
             "k_done k_maxed k_exped kt_done kt_out k_recced m_done m_out b_done b_out z_done z_out "
             "x_done x1_done x1_stats x1_aggr x1_mom x1_rstd x1_norm copied "
             "y_done y_out y_squared y_gained n_done n_clamped n_pow n_diag r_done y_scaled fin").split()
    s = {n: sem("a_" + n) for n in names}

    STEPS = 12

    def k_tile(t):
        return t // 2 if t in (0, 2, 4, 6) else None

    def kt_tile(t):
        return t // 2 if t in (1, 3, 5, 7) else None

    def m_tile(t):
        return {3: 0, 5: 1, 8: 2, 9: 3}.get(t)

    m_room = [pair_o[:, D - P:D]] * 2 + [bank_s[:, 0:P]] * 2

    W_PIECES = KT // 2

    def w_stage(n):
        return kT[:, 2 * n:2 * n + 2, :]

    def transpose_qk(pe, b):
        pe.wait_ge(s["qk_norm"], b + 1)
        for n in (2, 3, 0, 1):
            for j in range(4):
                last = nc.tensor.transpose(turn4[n][:, j, :], qk_in[:, n // 2, (n % 2 * 4 + j) * P:(n % 2 * 4 + j + 1) * P],
                                           ident[:, :])
            if n % 2:
                last.then_inc(s["a_done"], 1)

    def norm_qk_affine(act, b):
        for i in (1, 0):
            act.wait_ge(s["a_done"], 2 * b + 2 - i)
            for k in range(KT):
                last = nc.scalar.activation(qkT[:, i, k, :], turn4[2 * i + k // 4][:, k % 4, :], ACT.Identity,
                                            scale=affine[:, 2 * i, k:k + 1], bias=affine[:, 2 * i + 1, k:k + 1])
            last.then_inc(s["a_out"], 1)

    def transpose_context(pe, b):
        pe.wait_ge(s["ctx_loaded"], (b + 1) * 16)
        for k in range(KT):
            last = nc.tensor.transpose(pair_k[:, k * P:(k + 1) * P], ctx_in[:, k * P:(k + 1) * P], ident[:, :])
        last.then_inc(s["c_done"], 1)

    def context_out(act, b):
        act.wait_ge(s["c_done"], b + 1)
        nc.scalar.activation(qk_in[:, 1, :], pair_k[:, :], ACT.Copy).then_inc(s["c_out"], 1)

    def qk_statistics(dve, b):
        dve.wait_ge(s["qk_loaded"], (b + 1) * 16)
        for i in range(2):
            for e in range(2):
                last = nc.vector.bn_stats(qk_stats[:, i, 6 * e:6 * e + 6], qk_in[:, i, e * N:(e + 1) * N])
        last.then_inc(s["qk_stats"], 1)
        dve.wait_ge(s["qk_stats"], b + 1)
        hold_dve()
        for i in range(2):
            last = nc.vector.bn_aggr(qk_mom[:, i, 0:2], qk_stats[:, i, :])
        last.then_inc(s["qk_aggr"], 1)
        dve.wait_ge(s["qk_aggr"], b + 1)
        nc.vector.tensor_scalar(qk_mom[:, :, 2], qk_mom[:, :, 0], -1.0, None, ALU.mult)
        nc.vector.tensor_scalar(qk_mom[:, :, 3], qk_mom[:, :, 1], EPS, None, ALU.add).then_inc(s["qk_mom"], 1)

    def normalise_qk(pool, b):
        pool.wait_ge(s["qk_mom"], b + 1)
        nc.gpsimd.tensor_tensor(qk_mom[:, :, 4], qk_mom[:, :, 3], neg8[:, 0:2], ALU.pow).then_inc(s["qk_rstd"], 1)
        pool.wait_ge(s["qk_rstd"], b + 1)
        hold_pool()
        for i in range(2):
            last = nc.gpsimd.tensor_scalar(qk_in[:, i, :], qk_in[:, i, :], qk_mom[:, i, 2:3], qk_mom[:, i, 4:5],
                                           ALU.add, ALU.mult)
        last.then_inc(s["qk_norm"], 1)

    def key_blocks(dve, b):
        dve.wait_ge(s["a_out"], 2 * b + 1)
        for j in range(HG):
            at = slice(j * HD, (j + 1) * HD)
            last = nc.vector.tensor_copy(kD[at, :, j, :], qkT[at, 1, :, :])
        last.then_inc(s["kd_out"], 1)

    def bias_scores(dve, b, t):
        dve.wait_ge(s["s_done"], b * G + t + 1)
        nc.vector.scalar_tensor_tensor(flat(sc[:, t % SR, :, :]), bank_s[:, :], float(HD) ** -0.5,
                                       flat(bias[:, t * HG:(t + 1) * HG, :]), ALU.mult, ALU.add).then_inc(
            s["s_biased"], 1)

    def maxima(dve, b, t):
        dve.wait_ge(s["s_biased"], b * G + t + 1)
        nc.vector.tensor_reduce(neg_max[:, t, :], sc[:, t % SR, :, :], AX.X, ALU.max, negate=True).then_inc(
            s["s_max"], 1)

    def turn_sync(sp, b, own, cross, ahead):
        c = b - 1
        if own and cross:
            sp.wait_ge(s["copied"], c + 1)
            sp.dma_start(x1[:, :], x[b, :, :]).then_inc(s["x_loaded"], 16)
        if ahead:
            sp.wait_ge(s["k_done"], (b + 1) * XT)
            sp.dma_start(ctx_in[:, :], ctx_kv[b + 1, :, :]).then_inc(s["ctx_loaded"], 16)
            sp.wait_ge(s["b_done"], b + 1)
            sp.dma_start(qk_in[:, :, :], qkv[b + 1, :, 0:2 * D].rearrange("p (a d) -> p a d", a=2)).then_inc(
                s["qk_loaded"], 16)
            sp.wait_ge(s["o_done"], b + 1)
        if cross:
            sp.wait_ge(s["fin"], c + 1)
        if ahead:
            sp.dma_start(v_in[:, :], qkv[b + 1, :, 2 * D:3 * D]).then_inc(s["v_loaded"], 16)
        if cross:
            sp.dma_start(x2[c, :, :], res[:, :]).then_inc(s["stored"], 16)

    def turn_tensor(pe, b, own, cross, ahead):
        c = b - 1
        for t in range(STEPS):
            n = t - 2
            if own and 0 <= n < G:
                pe.wait_ge(s["s_norm"], b * G + n + 1)
                if n:
                    pe.wait_ge(s["p_out"], b * G + n)
                for j in range(HG):
                    last = nc.tensor.transpose(bank_p[:, j, :], sc[:, n % SR, j, :], ident[:, :])
                last.then_inc(s["p_done"], 1)
            if own and t < G:
                if t == 0:
                    pe.wait_ge(s["a_out"], 2 * b + 2)
                    pe.wait_ge(s["kd_out"], b + 1)
                else:
                    pe.wait_ge(s["s_biased"], b * G + t)
                nc.tensor.matmul(bank_s[:, :], qkT[:, 0, t, :], flat(kD[:, t, :, :]), start=True,
                                 stop=True).then_inc(s["s_done"], 1)
            n = t - 2
            if cross and 0 <= n < KT:
                if n % 4 == 0:
                    pe.wait_ge(s["x1_norm"], 2 * c + n // 4 + 1)
                if n:
                    pe.wait_ge(s["q_subbed"], c * KT + n)
                else:
                    pe.wait_ge(s["y_scaled"], b)
                nc.tensor.matmul(bank_q[:, :], xn[:, n * P:(n + 1) * P], wq_sb[:, 0, :], start=True,
                                 stop=True).then_inc(s["q_done"], 1)
            n = t - 3
            if own and 0 <= n < G:
                if n == 0:
                    pe.wait_ge(s["v_loaded"], (b + 1) * 16)
                if n == G // 2:
                    pe.wait_ge(s["m_out"], b * XT + 2)
                pe.wait_ge(s["p_out"], b * G + n + 1)
                for j in range(HG):
                    h = n * HG + j
                    last = nc.tensor.matmul(pair_o[j * HD:(j + 1) * HD, n * P:(n + 1) * P], v_in[:, h * HD:(h + 1) * HD],
                                            probT[:, n % 2, j, :], start=True, stop=True)
                if n == G - 1:
                    last.then_inc(s["o_done"], 1)
            if own and (i := k_tile(t)) is not None:
                if i == 0:
                    pe.wait_ge(s["c_out"], b + 1)
                else:
                    pe.wait_ge(s["kt_out"], b * XT + i)
                for e in range(2):
                    last = nc.tensor.matmul(pair_k[:, e * N:(e + 1) * N], wq_sb[:, 1, i * P:(i + 1) * P],
                                            ctx_in[:, e * N:(e + 1) * N], start=True, stop=True)
                last.then_inc(s["k_done"], 1)
            if own and (i := kt_tile(t)) is not None:
                pe.wait_ge(s["k_exped"], b * XT + i + 1)
                for k in range(KT):
                    last = nc.tensor.transpose(pair_k[:, k * P:(k + 1) * P], kE[:, k * P:(k + 1) * P], ident[:, :])
                last.then_inc(s["kt_done"], 1)
            if own and (i := m_tile(t)) is not None:
                if cross and i == 0:
                    pe.wait_ge(s["x1_done"], 2 * b)
                pe.wait_ge(s["kt_out"], b * XT + i + 1)
                if i == 2:
                    pe.wait_ge(s["s_biased"], (b + 1) * G)
                elif i:
                    pe.wait_ge(s["m_out"], b * XT + i)
                for k in range(KT):
                    last = nc.tensor.matmul(m_room[i], ctxT[:, k, :], kT[:, k, i * P:(i + 1) * P], start=k == 0,
                                            stop=k == KT - 1)
                last.then_inc(s["m_done"], 1)
            n = t - 4
            if cross and 0 <= n < KT:
                pe.wait_ge(s["q_normed"], c * KT + n + 1)
                if n:
                    pe.wait_ge(s["d_out"], c * KT + n)
                for j in range(XT):
                    last = nc.tensor.transpose(bank_d[:, j, :], qr[:, n % SR, j * P:(j + 1) * P], ident[:, :])
                last.then_inc(s["d_done"], 1)
            if own and t == STEPS - 2:
                pe.wait_ge(s["m_out"], (b + 1) * XT)
                for j in range(XT):
                    last = nc.tensor.matmul(pair_k[:, j * P:(j + 1) * P], wv_sb[:, j * P:(j + 1) * P],
                                            mT[:, j * P:(j + 1) * P], start=True, stop=True)
                last.then_inc(s["b_done"], 1)
            if own and t == STEPS - 1:
                pe.wait_ge(s["b_out"], b + 1)
                for j in range(XT):
                    last = nc.tensor.matmul(pair_k[:, N + j * P:N + (j + 1) * P], cT[:, j, :], wo_sb[:, j, :],
                                            start=True, stop=True)
                last.then_inc(s["z_done"], 1)
        if cross:
            pe.wait_ge(s["d_out"], (c + 1) * KT)
            if own:
                pe.wait_ge(s["s_biased"], (b + 1) * G)
            for e, bank in enumerate((bank_s, bank_q)):
                for j in range(XT):
                    last = nc.tensor.matmul(bank[:, :], z[:, j, :], qT[:, j, e * N:(e + 1) * N], start=j == 0,
                                            stop=j == XT - 1)
            last.then_inc(s["y_done"], 1)

        def project(e):
            product(nc, pair_o[:, e * N:(e + 1) * N],
                    [(l[:, k, :], r[:, k, :]) for k in range(KT)
                     for l, r in ((oT_hi, w_hi[e]), (oT_hi, w_lo[e]), (oT_lo, w_hi[e]))]).then_inc(s["x_done"], 1)

        if own:
            pe.wait_ge(s["o_lo"], b + 1)
            project(0)
        if ahead:
            pe.wait_ge(s["p_out"], (b + 1) * G)
            if cross:
                pe.wait_ge(s["y_out"], b)
            else:
                pe.wait_ge(s["s_biased"], (b + 1) * G)
            transpose_qk(pe, b + 1)
        if cross:
            pe.wait_ge(s["y_squared"], c + 1)
            for k in range(KT):
                last = nc.tensor.matmul(pair_k[:, k:k + 1], y_sq[:, k * P:(k + 1) * P], ones[:, 0:1],
                                        start=True, stop=True)
            last.then_inc(s["n_done"], 1)
        if own:
            if not cross:
                pe.wait_ge(s["w_lo_done"], W_PIECES)
            project(1)
        if ahead:
            pe.wait_ge(s["z_out"], b + 1)
            if cross:
                pe.wait_ge(s["n_clamped"], c + 1)
            transpose_context(pe, b + 1)
        if cross:
            if ahead:
                pe.wait_ge(s["a_out"], 2 * b + 4)
            pe.wait_ge(s["n_diag"], c + 1)
            for e, bank in enumerate(norm_banks):
                last = nc.tensor.matmul(bank, ones[:, :], flat(diag[:, 4 * e:4 * e + 4, :]), start=True, stop=True)
            last.then_inc(s["r_done"], 1)

    def turn_scalar(act, b, own, cross, ahead):
        c = b - 1
        for t in range(STEPS):
            n = t - 2
            if own and 0 <= n < G:
                act.wait_ge(s["p_done"], b * G + n + 1)
                nc.scalar.activation(probT[:, n % 2, :, :], bank_p[:, :, :], ACT.Copy).then_inc(s["p_out"], 1)
            if own and t < G:
                act.wait_ge(s["s_max"], b * G + t + 1)
                for j in range(HG):
                    last = nc.scalar.activation(sc[:, t % SR, j, :], sc[:, t % SR, j, :], ACT.Exp,
                                                bias=neg_max[:, t, j:j + 1], accum_out=row_sum[:, t, j:j + 1])
                last.then_inc(s["s_exp"], 1)
            n = t - 2
            if cross and 0 <= n < KT:
                act.wait_ge(s["q_subbed"], c * KT + n + 1)
                nc.scalar.activation(qr[:, n % SR, :], qr[:, n % SR, :], ACT.Exp).then_inc(s["q_exped"], 1)
            n = t - 4
            if cross and 0 <= n < KT:
                act.wait_ge(s["d_done"], c * KT + n + 1)
                nc.scalar.activation(qT[:, :, n * P:(n + 1) * P], bank_d[:, :, :], ACT.Copy).then_inc(s["d_out"], 1)
            if own and (i := kt_tile(t)) is not None:
                act.wait_ge(s["kt_done"], b * XT + i + 1)
                nc.scalar.activation(kT[:, :, i * P:(i + 1) * P], pair_k[:, :].rearrange("p (a b) -> p a b", a=KT),
                                     ACT.Copy).then_inc(s["kt_out"], 1)
            if own and (i := k_tile(t)) is not None:
                act.wait_ge(s["k_maxed"], b * XT + i + 1)
                nc.scalar.activation(kE[:, :], pair_k[:, :], ACT.Exp, bias=kneg[:, i:i + 1],
                                     accum_out=ksum[:, i:i + 1]).then_inc(s["k_exped"], 1)
            if own and t == STEPS - 2:
                act.wait_ge(s["o_done"], b + 1)
                nc.scalar.activation(flat(oT_hi[:, :, :]), pair_o[:, :], ACT.Copy).then_inc(s["o_hi"], 1)
        if cross:
            act.wait_ge(s["y_done"], c + 1)
            for e, bank in enumerate((bank_s, bank_q)):
                last = nc.scalar.activation(y[:, e * N:(e + 1) * N], bank[:, :], ACT.Identity, bias=bo_sb[:, 0:1])
            last.then_inc(s["y_out"], 1)
            act.wait_ge(s["y_out"], c + 1)
            nc.scalar.activation(y_sq[:, :], y[:, :], ACT.Square).then_inc(s["y_squared"], 1)
            act.wait_ge(s["y_squared"], c + 1)
            nc.scalar.activation(y[:, :], y[:, :], ACT.Copy, scale=g_sb[:, 0:1]).then_inc(s["y_gained"], 1)
        if ahead:
            norm_qk_affine(act, b + 1)
            context_out(act, b + 1)

    def turn_gpsimd(pool, b, own, cross, ahead):
        c = b - 1
        for t in range(STEPS):
            n = t - 1
            if own and 0 <= n < G:
                pool.wait_ge(s["s_rec"], b * G + n + 1)
                nc.gpsimd.tensor_tensor(sc[:, n % SR, :, :], sc[:, n % SR, :, :],
                                        row_rec[:, n, :].unsqueeze(2).to_broadcast([P, HG, P]),
                                        ALU.mult).then_inc(s["s_norm"], 1)
            if cross and t == 6:
                pool.wait_ge(s["stored"], (c + 1) * 16)
                hold_pool(2)
                nc.gpsimd.tensor_scalar(res[:, :], x1[:, :], 1.0, 0.0, ALU.mult, ALU.add).then_inc(s["copied"], 1)
            n = t - 3
            if cross and 0 <= n < KT:
                pool.wait_ge(s["q_recced"], c * KT + n + 1)
                q = qr[:, n % SR, :].rearrange("p (h d) -> p h d", d=XD)
                nc.gpsimd.tensor_tensor(q, q, q_rec[:, n, :].unsqueeze(2).to_broadcast([P, 8, XD]),
                                        ALU.mult).then_inc(s["q_normed"], 1)
        if ahead:
            normalise_qk(pool, b + 1)
        if cross:
            pool.wait_ge(s["n_clamped"], c + 1)
            nc.gpsimd.tensor_tensor(n_sq[:, 1, :], n_sq[:, 0, :], neg8[:, :], ALU.pow).then_inc(s["n_pow"], 1)
        if own:
            if cross:
                pool.wait_ge(s["r_done"], b + 1)
            pool.wait_ge(s["x1_mom"], b + 1)
            nc.gpsimd.tensor_tensor(x1_mom[:, 4:5], x1_mom[:, 3:4], neg8[:, 0:1], ALU.pow).then_inc(s["x1_rstd"], 1)
            pool.wait_ge(s["x1_rstd"], b + 1)
            hold_pool()
            for e in range(2):
                nc.gpsimd.tensor_scalar(xn[:, e * N:(e + 1) * N], x1[:, e * N:(e + 1) * N], x1_mom[:, 2:3],
                                        x1_mom[:, 4:5], ALU.add, ALU.mult).then_inc(s["x1_norm"], 1)
        if cross:
            pool.wait_ge(s["copied"], c + 1)
            pool.wait_ge(s["y_scaled"], c + 2)
            nc.gpsimd.tensor_tensor(res[:, :], y[:, :], res[:, :], ALU.add).then_inc(s["fin"], 1)

    def turn_vector(dve, b, own, cross, ahead):
        c = b - 1
        for t in range(STEPS):
            n = t - 3
            if cross and 0 <= n < KT:
                dve.wait_ge(s["q_exped"], c * KT + n + 1)
                nc.vector.tensor_reduce(q_sum[:, n, :], qr[:, n % SR, :].rearrange("p (h d) -> p h d", d=XD), AX.X,
                                        ALU.add).then_inc(s["q_summed"], 1)
            if own and 0 < t < G:
                bias_scores(dve, b, t)
            n = t - 3
            if cross and 0 <= n < KT:
                dve.wait_ge(s["q_summed"], c * KT + n + 1)
                nc.vector.reciprocal(q_rec[:, n, :], q_sum[:, n, :]).then_inc(s["q_recced"], 1)
            if own and 0 < t < G:
                maxima(dve, b, t)
            n = t - 2
            if cross and 0 <= n < KT:
                dve.wait_ge(s["q_done"], c * KT + n + 1)
                nc.vector.tensor_reduce(q_max[:, n, :], bank_q[:, :].rearrange("p (h d) -> p h d", d=XD), AX.X,
                                        ALU.max).then_inc(s["q_maxed"], 1)
                dve.wait_ge(s["q_maxed"], c * KT + n + 1)
                nc.vector.tensor_tensor(qr[:, n % SR, :].rearrange("p (h d) -> p h d", d=XD),
                                        bank_q[:, :].rearrange("p (h d) -> p h d", d=XD),
                                        q_max[:, n, :].unsqueeze(2).to_broadcast([P, 8, XD]),
                                        ALU.subtract).then_inc(s["q_subbed"], 1)
            if own and (i := k_tile(t)) is not None:
                dve.wait_ge(s["k_done"], b * XT + i + 1)
                nc.vector.tensor_reduce(kneg[:, i:i + 1], pair_k[:, :], AX.X, ALU.max, negate=True).then_inc(
                    s["k_maxed"], 1)
            if own and (i := m_tile(t)) is not None:
                dve.wait_ge(s["m_done"], b * XT + i + 1)
                nc.vector.tensor_copy(mT[:, i * P:(i + 1) * P], m_room[i]).then_inc(s["m_out"], 1)
            if own and t < G:
                dve.wait_ge(s["s_exp"], b * G + t + 1)
                nc.vector.reciprocal(row_rec[:, t, :], row_sum[:, t, :]).then_inc(s["s_rec"], 1)
        if own:
            dve.wait_ge(s["b_done"], b + 1)
            for j in range(2):
                at = slice(j * XD, (j + 1) * XD)
                last = nc.vector.tensor_copy(cT[at, :, at], pair_k[at, 0:N].rearrange("p (a b) -> p a b", a=XT)[:, :, at])
            last.then_inc(s["b_out"], 1)
            dve.wait_ge(s["o_hi"], b + 1)
            nc.vector.tensor_tensor(flat(oT_lo[:, :, :]), pair_o[:, :], flat(oT_hi[:, :, :].bitcast(F32)),
                                    ALU.subtract).then_inc(s["o_lo"], 1)
            dve.wait_ge(s["k_exped"], (b + 1) * XT)
            nc.vector.reciprocal(krec[:, 0, :], ksum[:, :]).then_inc(s["k_recced"], 1)
            dve.wait_ge(s["k_recced"], 2 * b + 1)
            nc.vector.tensor_scalar(krec[:, 1, :], krec[:, 0, :], float(XD) ** -0.5, None, ALU.mult).then_inc(
                s["k_recced"], 1)
            if ahead:
                qk_statistics(dve, b + 1)
            dve.wait_ge(s["k_recced"], 2 * (b + 1))
            dve.wait_ge(s["z_done"], b + 1)
            if cross:
                dve.wait_ge(s["y_done"], c + 1)
            for j in range(XT):
                last = nc.vector.tensor_scalar(z[:, j, :], pair_k[:, N + j * P:N + (j + 1) * P], krec[:, 1, j:j + 1], None,
                                               ALU.mult)
            last.then_inc(s["z_out"], 1)
            dve.wait_ge(s["x_loaded"], (b + 1) * 16)

        def residual(e):
            dve.wait_ge(s["x_done"], 2 * b + e + 1)
            nc.vector.tensor_tensor(x1[:, e * N:(e + 1) * N], pair_o[:, e * N:(e + 1) * N],
                                    x1[:, e * N:(e + 1) * N], ALU.add).then_inc(s["x1_done"], 1)
            dve.wait_ge(s["x1_done"], 2 * b + e + 1)
            return nc.vector.bn_stats(x1_stats[:, 6 * e:6 * e + 6], x1[:, e * N:(e + 1) * N])

        if own:
            residual(0)
        if cross:
            dve.wait_ge(s["n_done"], c + 1)
            nc.vector.tensor_scalar(n_sq[:, 0, :], pair_k[:, 0:KT], 1e-24, None, ALU.max).then_inc(s["n_clamped"], 1)
            dve.wait_ge(s["n_pow"], c + 1)
            nc.vector.tensor_tensor(diag[:, :, :], ident[:, :].unsqueeze(1).to_broadcast([P, KT, P]),
                                    n_sq[:, 1, :].unsqueeze(2).to_broadcast([P, KT, P]), ALU.mult).then_inc(s["n_diag"], 1)
        if ahead:
            key_blocks(dve, b + 1)
        if own:
            residual(1).then_inc(s["x1_stats"], 1)
            dve.wait_ge(s["x1_stats"], b + 1)
            hold_dve()
            nc.vector.bn_aggr(x1_mom[:, 0:2], x1_stats[:, :]).then_inc(s["x1_aggr"], 1)
            dve.wait_ge(s["x1_aggr"], b + 1)
            nc.vector.tensor_scalar(x1_mom[:, 2:3], x1_mom[:, 0:1], -1.0, None, ALU.mult)
            nc.vector.tensor_scalar(x1_mom[:, 3:4], x1_mom[:, 1:2], EPS, None, ALU.add).then_inc(s["x1_mom"], 1)
        if cross:
            dve.wait_ge(s["y_gained"], c + 1)
            dve.wait_ge(s["r_done"], c + 2)
            for e, bank in enumerate(norm_banks):
                last = nc.vector.tensor_tensor(y[:, e * N:(e + 1) * N], y[:, e * N:(e + 1) * N], bank, ALU.mult)
            last.then_inc(s["y_scaled"], 1)
        if ahead:
            bias_scores(dve, b + 1, 0)
            maxima(dve, b + 1, 0)

    def turns(eng, turn):
        turn(eng, 0, True, False, True)
        with eng.Fori(1, NB - 1) as b:
            turn(eng, b, True, True, True)
        turn(eng, NB - 1, True, True, False)
        turn(eng, NB, False, True, False)

    with nc.Block() as block:
        @block.sync
        def _(sp):
            sp.dma_start(qk_in[:, :, :], qkv[0, :, 0:2 * D].rearrange("p (a d) -> p a d", a=2)).then_inc(
                s["qk_loaded"], 16)
            sp.dma_start(ctx_in[:, :], ctx_kv[0, :, :]).then_inc(s["ctx_loaded"], 16)
            sp.dma_start(v_in[:, :], qkv[0, :, 2 * D:3 * D]).then_inc(s["v_loaded"], 16)
            sp.dma_start(wq_sb[:, :, :], wqk).then_inc(s["setup_in"], 16)
            for i, v in enumerate((q_w, q_b, k_w, k_b)):
                sp.dma_start(affine[:, i, :], v).then_inc(s["setup_in"], 16)
            sp.dma_start(wv_sb[:, :], wv).then_inc(s["setup_in"], 16)
            sp.dma_start(wo_sb[:, :, :], wo.rearrange("(a p) n -> p a n", p=P)).then_inc(s["setup_in"], 16)
            sp.dma_start(bo_sb[:, :], bo.rearrange("(p a) -> p a", a=1)).then_inc(s["setup_in"], 16)
            sp.dma_start(g_sb[:, :], g.rearrange("a p b -> p (a b)")).then_inc(s["setup_in"], 16)
            sp.dma_start(x1[:, :], x[0, :, :]).then_inc(s["x_loaded"], 16)
            for n in range(W_PIECES):
                sp.dma_start(w_stage(n), w_attn[CHUNKS - 1, :, 2 * n:2 * n + 2, :]).then_inc(s[f"w_in{n}"], 16)
            sp.sem_inc(s["stored"], 16)
            turns(sp, turn_sync)
            sp.wait_ge(s["stored"], (NB + 1) * 16)

        @block.gpsimd
        def _(pool):
            nc.gpsimd.iota(rel[:, :], [[1, P]], 0, channel_multiplier=-1, allow_small_or_imprecise_dtypes=True).then_inc(
                s["distances"], 1)
            nc.gpsimd.memset(neg8[:, :], -0.5).then_inc(s["powers"], 1)
            pool.wait_ge(s["powers"], 1)
            normalise_qk(pool, 0)
            nc.gpsimd.memset(kD[:, :, :, :], 0.0)
            nc.gpsimd.memset(ones[:, :], 1.0)
            nc.gpsimd.memset(cT[:, :, :], 0.0).then_inc(s["filled"], 1)
            pool.wait_ge(s["slopes"], 1)
            nc.gpsimd.affine_select(out=bias[:, :, :], in_=bias[:, :, :], compare_op=ALU.is_ge, fill=MASKED, base=0,
                                    pattern=[[0, HEADS], [-1, P]], channel_multiplier=1).then_inc(s["masked"], 1)
            turns(pool, turn_gpsimd)

        @block.scalar
        def _(act):
            act.wait_ge(s["setup_in"], 9 * 16)
            norm_qk_affine(act, 0)
            context_out(act, 0)
            for n in range(W_PIECES):
                act.wait_ge(s[f"w_in{n}"], 16)
                nc.scalar.activation(w_hi[1][:, 2 * n:2 * n + 2, :], w_stage(n), ACT.Copy).then_inc(s["w_hi_done"], 1)
            turns(act, turn_scalar)

        @block.vector
        def _(dve):
            dve.sem_inc(s["y_scaled"], 1)
            qk_statistics(dve, 0)
            dve.wait_ge(s["distances"], 1)
            for h in range(HEADS):
                slope = 0.5 ** ((h + 1) * ALIBI_MAX / HEADS)
                last = nc.vector.tensor_scalar(bias[:, h, :], rel[:, :], slope, None, ALU.mult)
            last.then_inc(s["slopes"], 1)
            dve.wait_ge(s["setup_in"], 9 * 16)
            nc.vector.tensor_scalar(g_sb[:, :], g_sb[:, :], float(DIM) ** 0.5, None, ALU.mult).then_inc(s["gain"], 1)
            dve.wait_ge(s["filled"], 1)
            key_blocks(dve, 0)
            dve.wait_ge(s["masked"], 1)
            dve.wait_ge(s["gain"], 1)
            bias_scores(dve, 0, 0)
            maxima(dve, 0, 0)
            for n in range(W_PIECES):
                dve.wait_ge(s["w_hi_done"], n + 1)
                at = slice(2 * n, 2 * n + 2)
                nc.vector.tensor_tensor(w_lo[1][:, at, :], w_stage(n), w_hi[1][:, at, :].bitcast(F32),
                                        ALU.subtract).then_inc(s["w_lo_done"], 1)
            turns(dve, turn_vector)

        @block.tensor
        def _(pe):
            pe.sem_inc(s["r_done"], 1)
            transpose_qk(pe, 0)
            transpose_context(pe, 0)
            pe.wait_ge(s["setup_in"], 9 * 16)
            pe.wait_ge(s["filled"], 1)
            turns(pe, turn_tensor)


def feed_forward_phase(nc, sb, pb, sem, ph, w13, s13, w2, s2, shifts, x2, out, ident, half_neg, ln_stats, ln_moments):
    GROUPS = NT // 2
    acc = sb("acc", [P, HALF, D], F32, ph)
    xT_hi = sb("h_xT_hi", [P, HALF, KT, P], F32R, ph)
    xT_lo = sb("h_xT_lo", [P, HALF, KT, P], F32R, ph)
    w13_hi = [sb(f"w13_hi{i}", [P, 2, KT, P], F32R, ph) for i in range(2)]
    w13_lo = [sb(f"w13_lo{i}", [P, 2, KT, P], F32R, ph) for i in range(2)]
    w2_hi = [sb(f"w2_hi{i}", [P, 2, N], F32R, ph) for i in range(3)]
    w2_lo = [sb(f"w2_lo{i}", [P, 2, N], F32R, ph) for i in range(3)]
    h_hi = [sb(f"h_hi{i}", [P, HALF * P], F32R, ph) for i in range(3)]
    h_lo = [sb(f"h_lo{i}", [P, HALF * P], F32R, ph) for i in range(3)]
    words = [sb(f"words{i}", [P, D], I32, ph) for i in range(3)]
    sc13 = sb("sc13", [P, 2, P], F32, ph)
    sc2 = sb("sc2", [P, D], F32, ph)
    shift = sb("shift", [P, 6], I32, ph)
    gate = [sb(f"gate{i}", [P, N], F32, ph) for i in range(2)]
    ps_room = pb("ff_ps", [P, 4, N], ph)
    ps = [ps_room[:, i, :] for i in range(4)]
    po = pb("ff_po", [P, 4, N], ph)

    names = ("shifts w1_in w3_in w2_in s13_in shifted scaled split_hi "
             "ab_done gated product h_hi h_lo y_done added").split()
    s = {n: sem("f_" + n) for n in names}
    split = [sem(f"f_split_{n}") for n in ("w1", "w3", "w2")]
    loaded = [s["w1_in"], s["w3_in"], s["w2_in"]]

    def columns(rows, k):
        return rows.rearrange("p (q k) -> p k q", k=KT)[:, k, :]

    turn = [room[:, 2 * p:2 * p + 2, :].rearrange("p a (b c) -> p (a b) c", c=P)
            for room in (ps_room, ps_room, po, po) for p in range(2)]
    rows = sb("h_rows", [P, 2, D], F32, ph)
    ln = LayerNormT(nc, lambda n: sem("h_" + n), rows, columns, ident, half_neg, xT_hi, xT_lo, ln_stats,
                    ln_moments)
    acc_in = [sem(f"f_acc_in{t}") for t in range(HALF)]
    stored = [sem(f"f_stored{t}") for t in range(HALF)]
    OUTS = 2 * HALF
    FULL_GROUPS = GROUPS - 1
    LAST_UNITS = FF - (NT - 1) * P
    LAG, LAG_T = 3, 5

    def groups(eng, group):
        group(0, 0, True, False)
        with eng.Fori(0, FULL_GROUPS // 2 - 1) as i:
            group(i * 2 + 1, 1, False, False)
            group(i * 2 + 2, 0, False, False)
        group(GROUPS - 2, 1, False, False)
        group(GROUPS - 1, 0, False, True)

    with nc.Block() as block:
        @block.sync
        def _(sp):
            def load13(tile, count):
                for mat in range(2):
                    if count is not None:
                        sp.wait_ge(split[mat], count)
                    sp.dma_start(words[mat][:, :], w13[tile, mat, :, :]).then_inc(loaded[mat], 16)
                    if mat == 0:
                        if count is not None:
                            sp.wait_ge(s["scaled"], count * 3 - 1)
                        sp.dma_start(sc13[:, :, :], s13[tile, :, :, :]).then_inc(s["s13_in"], 16)

            def load2(tile, u):
                sp.wait_ge(split[2], u + 1)
                for a in range(2):
                    at = slice(a * 64, a * 64 + 64)
                    sp.dma_start(words[2][at, 0:N], w2[tile, :, :]).then_inc(s["w2_in"], 16)
                    sp.dma_start(words[2][at, N:D], w2[tile + FF // P + a, :, :]).then_inc(s["w2_in"], 16)
                    sp.dma_start(sc2[at, :], s2[bass.ds(tile * 2 + a, 1), :].to_broadcast([64, D])).then_inc(
                        s["w2_in"], 16)

            sp.sem_inc(split[2], 1)
            for t in range(2):
                sp.dma_start(acc[:, t, :], x2[t, :, :]).then_inc(acc_in[t], 16)
            sp.dma_start(shift[:, :], shifts).then_inc(s["shifts"], 16)
            load13(0, None)
            for t in range(2, HALF):
                sp.dma_start(acc[:, t, :], x2[t, :, :]).then_inc(acc_in[t], 16)
            for hf in range(2):
                def group(j, parity, first, last):
                    for e in range(2):
                        tile = j * 2 + e
                        u = hf * NT + tile
                        load13(tile + 1, u + 1)
                        load2(tile, u)

                def reload(t):
                    sp.wait_ge(stored[t], 16)
                    sp.dma_start(acc[:, t, :], x2[HALF + t, :, :]).then_inc(acc_in[t], 16)

                groups(sp, group)
                for t in range(HALF):
                    sp.wait_ge(s["added"], (hf * GROUPS + GROUPS - 1) * OUTS + 2 * t + 2 + 4)
                    sp.dma_start(out[hf * HALF + t, :, :], acc[:, t, :]).then_inc(stored[t], 16)
                    if hf == 0 and t:
                        reload(t - 1)
                if hf == 0:
                    reload(HALF - 1)
            for t in range(HALF):
                sp.wait_ge(stored[t], 32)

        @block.gpsimd
        def _(pool):
            for n in range(NB):
                pool.wait_ge(ln.transposed, n + 1)
                ln.normalise(pool, n, n % 2, acc[:, n % HALF, :])

        @block.scalar
        def _(act):
            def high(mat, dst, count):
                act.wait_ge(s["scaled"], count)
                src = words[mat][:, :].bitcast(F32)
                nc.scalar.activation(dst, src, ACT.Copy).then_inc(s["split_hi"], 1)

            def tile(u, e, slot, first, units=P):
                act.wait_ge(s["ab_done"], u * 4 + 1)
                for mat in range(2):
                    high(mat, flat(w13_hi[1 - e][:, mat, :, :]), u * 3 + 3 + mat)
                if e == 1 and not first:
                    act.wait_ge(s["y_done"], (u - 1) * (OUTS // 2))
                high(2, flat(w2_hi[slot][:, :, :]), u * 3 + 5)
                for sl in range(SL):
                    act.wait_ge(s["h_lo"], u * 2 + sl + 1)
                    act.wait_ge(s["ab_done"], u * 4 + 2 * sl + 2)
                    nc.scalar.activation(gate[sl][0:units, :], ps[2 * sl][0:units], ACT.Silu).then_inc(s["gated"], 1)
                    act.wait_ge(s["product"], u * 2 + sl + 3)
                    nc.scalar.activation(h_hi[slot][:, sl * N:(sl + 1) * N], gate[sl][:, :], ACT.Copy).then_inc(
                        s["h_hi"], 1)

            for mat in range(2):
                high(mat, flat(w13_hi[0][:, mat, :, :]), mat + 1)
            for hf in range(2):
                for t in range(HALF):
                    ln.high(act, hf * HALF + t, t, turn[t])

                def group(j, parity, first, last):
                    for e in range(2):
                        tile(hf * NT + j * 2 + e, e, 2 if e else parity, first, LAST_UNITS if last and e else P)

                groups(act, group)

        @block.vector
        def _(dve):
            def unpack(mat, count):
                w = words[mat]
                for kind, at in ((0, slice(0, D)),) if mat < 2 else ((1, slice(0, N)), (2, slice(N, D))):
                    last = nc.vector.tensor_scalar(w[:, at], w[:, at], shift[:, 2 * kind:2 * kind + 1],
                                                   shift[:, 2 * kind + 1:2 * kind + 2], ALU.logical_shift_left,
                                                   ALU.arith_shift_right)
                last.then_inc(s["shifted"], 1)
                if mat < 2:
                    dst, src = [v.rearrange("p (k n) -> p k n", k=KT) for v in (w[:, :].bitcast(F32), w[:, :])]
                    scale = sc13[:, mat, :].unsqueeze(1).to_broadcast([P, KT, P])
                else:
                    dst, src, scale = w[:, :].bitcast(F32), w[:, :], sc2[:, :]
                dve.wait_ge(s["shifted"], count + 1)
                nc.vector.tensor_tensor(dst, src, scale, ALU.mult).then_inc(s["scaled"], 1)

            def low(mat, dst, hi, count):
                dve.wait_ge(s["split_hi"], count + 1)
                nc.vector.tensor_tensor(dst, words[mat][:, :].bitcast(F32), hi.bitcast(F32), ALU.subtract).then_inc(
                    split[mat], 1)

            def low13(e, mat, count):
                low(mat, flat(w13_lo[e][:, mat, :, :]), flat(w13_hi[e][:, mat, :, :]), count)

            def tile(u, e, slot, units=P):
                for mat in range(2):
                    dve.wait_ge(loaded[mat], (u + 2) * 16)
                    if mat == 0:
                        dve.wait_ge(s["s13_in"], (u + 2) * 16)
                    unpack(mat, u * 3 + 2 + mat)
                low13(1 - e, 0, u * 3 + 2)
                dve.wait_ge(s["w2_in"], (u + 1) * 96)
                unpack(2, u * 3 + 4)
                low13(1 - e, 1, u * 3 + 3)
                low(2, flat(w2_lo[slot][:, :, :]), flat(w2_hi[slot][:, :, :]), u * 3 + 4)
                for sl in range(SL):
                    dve.wait_ge(s["gated"], u * 2 + sl + 1)
                    dve.wait_ge(s["ab_done"], u * 4 + 2 * sl + 3)
                    b = ps[2 * sl + 1]
                    if units < P:
                        b = ps[2 * sl][units:P]
                        nc.vector.memset(gate[sl][units:P, :], 0.0)
                    nc.vector.tensor_tensor(gate[sl][0:units, :], gate[sl][0:units, :], b, ALU.mult).then_inc(
                        s["product"], 1)
                    dve.wait_ge(s["h_hi"], u * 2 + sl + 1)
                    at = slice(sl * N, (sl + 1) * N)
                    nc.vector.tensor_tensor(h_lo[slot][:, at], gate[sl][:, :], h_hi[slot][:, at].bitcast(F32),
                                            ALU.subtract).then_inc(s["h_lo"], 1)

            def add(gj, after=lambda t: None):
                for o in range(OUTS):
                    t, par = o // 2, o % 2
                    dve.wait_ge(s["y_done"], gj * OUTS + o + 1)
                    cols = acc[:, t, :].rearrange("p (n two) -> p two n", two=2)[:, par, :]
                    nc.vector.tensor_tensor(cols, po[:, o % 4, :], cols, ALU.add).then_inc(s["added"], 1)
                    if par:
                        after(t)

            def norm(hf, stats, low):
                if stats < HALF:
                    dve.wait_ge(acc_in[stats], (hf + 1) * 16)
                    if hf * HALF + stats >= 2:
                        dve.wait_ge(ln.normalised, hf * HALF + stats - 1)
                    ln.statistics(dve, hf * HALF + stats, stats % 2, acc[:, stats, :])
                if low < HALF:
                    ln.low(dve, hf * HALF + low, low, turn[low])

            dve.sem_inc(ln.lo_done, 2)
            dve.sem_inc(s["h_lo"], 2)
            norm(0, 0, HALF)
            dve.wait_ge(s["shifts"], 16)
            for mat in range(2):
                dve.wait_ge(loaded[mat], 16)
                if mat == 0:
                    dve.wait_ge(s["s13_in"], 16)
                unpack(mat, mat)
                if mat == 0:
                    norm(0, 1, HALF)
                low13(0, mat, mat)
            for hf in range(2):
                if hf == 0:
                    for t in range(2, HALF):
                        norm(0, t, t - 2)
                    norm(0, HALF, HALF - 2)
                    norm(0, HALF, HALF - 1)
                else:
                    add(GROUPS - 1, lambda t: norm(1, t - LAG if t >= LAG else HALF,
                                                   t - LAG_T if t >= LAG_T else HALF))
                    for t in range(HALF, HALF + LAG_T):
                        norm(1, t - LAG, t - LAG_T)

                def group(j, parity, first, last):
                    tile(hf * NT + j * 2, 0, parity)
                    if not first:
                        add(hf * GROUPS + j - 1)
                    tile(hf * NT + j * 2 + 1, 1, 2, LAST_UNITS if last else P)

                groups(dve, group)
            add(2 * GROUPS - 1)

        @block.tensor
        def _(pe):
            def ab(u, e, hf=None, units=P):
                for mat in range(2):
                    pe.wait_ge(split[mat], u + 1)
                for sl in range(SL):
                    if hf is not None:
                        pe.wait_ge(ln.lo_done, hf * HALF + sl * 4 + 6)
                    pe.wait_ge(s["product"], u * 2 + sl + 1)
                    mats = 2 if units == P else 1
                    for mat in range(mats):
                        at = slice(sl * 4, sl * 4 + 4)
                        product(nc, ps[2 * sl + mat].rearrange("p (a b) -> p a b", a=4),
                                [(l[:, mat, k, :], r[:, at, k, :]) for k in range(KT)
                                 for l, r in ((w13_hi[e], xT_hi), (w13_hi[e], xT_lo), (w13_lo[e], xT_hi))]).then_inc(
                            s["ab_done"], 2 // mats)
                        if hf is not None and sl == 0:
                            transpose(hf, 4 + 2 * mat)
                            transpose(hf, 5 + 2 * mat)

            def transpose(hf, t):
                if hf and t < 4:
                    pe.wait_ge(s["product"], NT * 2 + 2)
                elif hf:
                    pe.wait_ge(s["added"], GROUPS * OUTS + 4)
                ln.transpose(pe, hf * HALF + t, t % 2, turn[t])

            def outputs(gj, slots, after=lambda t: None):
                pe.wait_ge(s["h_lo"], (gj + 1) * 4 + 2)
                pe.wait_ge(split[2], (gj + 1) * 2 + 1)
                for o in range(OUTS):
                    t, par = o // 2, o % 2
                    at = slice(t * P, (t + 1) * P)
                    pe.wait_ge(s["added"], gj * OUTS + o + 1)
                    product(nc, po[:, o % 4, :],
                            [(l[i][:, at], r[i][:, par, :]) for i in slots
                             for l, r in ((h_hi, w2_hi), (h_hi, w2_lo), (h_lo, w2_hi))]).then_inc(s["y_done"], 1)
                    if par:
                        after(t)

            pe.sem_inc(s["added"], 4)
            pe.sem_inc(s["product"], 2)
            pe.sem_inc(s["ab_done"], 1)
            pe.sem_inc(ln.transposed, 2)
            for hf in range(2):
                if hf:
                    outputs(GROUPS - 1, (0, 2), lambda t: transpose(1, t - LAG_T) if t >= LAG_T else None)
                for t in range(HALF - LAG_T if hf else 0, 4):
                    transpose(hf, t)

                def group(j, parity, first, last):
                    ab(hf * NT + j * 2, 0, hf if first else None)
                    if not first:
                        outputs(hf * GROUPS + j - 1, (1 - parity, 2))
                    ab(hf * NT + j * 2 + 1, 1, None, LAST_UNITS if last else P)

                groups(pe, group)
            outputs(2 * GROUPS - 1, (0, 2))


def lay_out_ffn(w1, s1, w2, s2, w3, s3):
    import numpy as np

    pad = NT * P - FF

    def words(w):
        w = np.asarray(w).reshape(FF, 8, 1, 8, 8).repeat(2, axis=2)
        w = np.concatenate([w, np.zeros((pad,) + w.shape[1:], w.dtype)])
        return w.reshape(NT, P, P, 8).transpose(0, 2, 3, 1)

    def scales(s):
        s = np.asarray(s).reshape(FF, 16).repeat(8, axis=1)
        s = np.concatenate([s, np.zeros((pad, P), s.dtype)])
        return s.reshape(NT, P, P).transpose(0, 2, 1)

    w13 = np.stack([words(w1), words(w3)], 1)
    s13 = np.stack([scales(s1), scales(s3)], 2)
    last = P - pad
    w13[-1, 0, :, :, last:] = w13[-1, 1, :, :, :pad]
    s13[-1, :, 0, last:] = s13[-1, :, 1, :pad]
    w13 = w13.reshape(NT, 2, P, 8 * P)
    w13, s13 = [np.concatenate([v, v[:1]]) for v in (w13, s13)]
    rows = FF // GROUP
    w2 = np.asarray(w2).reshape(D // 2, rows, GROUP).transpose(1, 2, 0)
    w2 = np.concatenate([w2, np.zeros((1, GROUP, D // 2), w2.dtype)])
    s2 = np.asarray(s2).reshape(D // 2, 2, rows).transpose(2, 1, 0).reshape(rows, D)
    s2 = np.concatenate([s2, np.zeros((1, D), s2.dtype)])
    high, low = (0, 4), (28, 28)
    shifts = np.array([(high, low)[p // 8 % 2] + (high, low)[p // 64] + (low, high)[p // 64] for p in range(P)],
                      np.int32)
    return [np.ascontiguousarray(v) for v in (w13, s13, w2, s2, shifts)]


def kernel(**inputs):
    import numpy as np
    import concourse.bacc as bacc
    from concourse.bass_utils import run_bass_kernel_spmd

    a = {name: np.asarray(value) for name, value in inputs.items()}

    w_attn = np.concatenate([a["L0_attn_Wqkv"], a["L0_attn_Wout"]])
    vectors = [a["L0_attn_" + n].reshape(KT, P).T for n in ("q_ln_w", "q_ln_b", "k_ln_w", "k_ln_b")]
    w13, s13, w2, s2, shifts = lay_out_ffn(*[a["L0_ffn_" + n] for n in ("w1", "s1", "w2", "s2", "w3", "s3")])
    laid_out = dict(
        x=a["x"],
        context=a["ctx_4096"],
        w_attn=w_attn.reshape(CHUNKS, N, KT, P).transpose(0, 3, 2, 1),
        q_w=vectors[0], q_b=vectors[1], k_w=vectors[2], k_b=vectors[3],
        wqk=np.stack([a["L0_xattn_Wq"].T, a["L0_xattn_Wk"].T], 1),
        wv=a["L0_xattn_Wv"].T,
        wo=a["L0_xattn_Wo"].T,
        bo=a["L0_xattn_bo"],
        g=a["L0_xattn_g"],
        w13=w13, s13=s13, w2=w2, s2=s2, shifts=shifts)

    nc = bacc.Bacc("TRN2", target_bir_lowering=False, num_devices=1)
    arrays, args = {}, []
    for name, value in laid_out.items():
        value = np.ascontiguousarray(value)
        arrays[f"in_{name}"] = value
        args.append(nc.dram_tensor(f"in_{name}", value.shape, mybir.dt.from_np(value.dtype),
                                   kind="ExternalInput").ap())
    out = nc.dram_tensor("out_0", (NB, P, D), F32, kind="ExternalOutput").ap()
    qkv = nc.dram_tensor("qkv", (NB, P, 3 * D), F32).ap()
    x2 = nc.dram_tensor("x2", (NB, P, D), F32).ap()
    program(nc, *args, out, qkv, x2)
    r = run_bass_kernel_spmd(nc, [arrays], core_ids=[0])
    return r.results[0]["out_0"]
```
